# Optimizing a Trainium2 kernel written in Bass

```python
import numpy as np
import jax
import jax.numpy as jnp

def _softmax(x, axis=-1):
    return jax.nn.softmax(x, axis=axis)

def _gelu(x):
    return jax.nn.gelu(x, approximate=True)

def _silu(x):
    return jax.nn.silu(x)

def _sigmoid(x):
    return jax.nn.sigmoid(x)

def _layernorm(x, axis=-1, eps=1e-05):
    m = jnp.mean(x, axis=axis, keepdims=True)
    v = jnp.var(x, axis=axis, keepdims=True)
    return (x - m) / jnp.sqrt(v + eps)

def _scatter_add(tgt, idx, src, axis=0):
    return tgt.at[idx].add(src)

def _segment_sum(src, seg, n):
    return jax.ops.segment_sum(src, seg, n)
kernel_name = 'mk_decoder_preln_d1_seqx_r4_07fc2c'

def setup_inputs(seed: int=0):
    np.random.seed(seed)
    _w = jnp.asarray

    def _rec_inputs():
        import jax
        import jax.numpy as jnp
        _rk = jax.random.key(seed)
        x = -0.0003929 + 0.9999 * jax.random.normal(jax.random.fold_in(_rk, 1), (4, 512, 256), jnp.float32)
        _lenS = 512 - jax.random.randint(jax.random.fold_in(_rk, 7), (4,), 0, max(1, 512 // 4) + 1, jnp.int32)
        _lenS2 = 1024 - jax.random.randint(jax.random.fold_in(_rk, 8), (4,), 0, max(1, 1024 // 4) + 1, jnp.int32)
        _ctx_768P = jax.random.normal(jax.random.fold_in(_rk, 11), (4, 16, 192), jnp.float32)
        _ctx_768c = jax.random.dirichlet(jax.random.fold_in(_rk, 511), 0.3 * jnp.ones((16,), jnp.float32), (4, 1024))
        _ctx_768t = jnp.einsum('bsk,bkd->bsd', _ctx_768c, _ctx_768P)
        _ctx_768t = _ctx_768t * jax.lax.rsqrt(jnp.mean(jnp.square(_ctx_768t)) + 1e-12) * 0.953939
        ctx_768 = 0.00095986 + 0.999812 * (_ctx_768t + 0.3 * jax.random.normal(jax.random.fold_in(_rk, 611), (4, 1024, 192), jnp.float32))
        _validS = jnp.arange(512)[None, :] < _lenS[:, None]
        _validS2 = jnp.arange(1024)[None, :] < _lenS2[:, None]
        _causal = jnp.tril(jnp.ones((512, 512), dtype=bool))
        mask_BxS2_bf1 = jnp.ones((4, 1024), dtype=bool)
        return (x, ctx_768, mask_BxS2_bf1)
    x, ctx_768, mask_BxS2_bf1 = _rec_inputs()

    def _L0_attn_setup():
        import jax, jax.numpy as jnp
        import numpy as np
        B, L, D_MODEL, H, HD, FD = (1, 256, 256, 16, 64, 64)
        EPS = 1e-12

        def _heads(t):
            b, l, _ = t.shape
            return t.reshape(b, l, H, HD).transpose(0, 2, 1, 3)

        def _feature_map(t, K):
            f = jnp.einsum('hdf,bhld->bhlf', K, t)
            feats = jnp.concatenate([jax.nn.softmax(f, axis=-1), jax.nn.softmax(-f, axis=-1)], axis=-1)
            return jnp.maximum(feats, EPS)
        key = jax.random.key(seed)
        ks = jax.random.split(key, 7)
        s = 1.0 / np.sqrt(D_MODEL)
        return {'x': jax.random.normal(ks[0], (B, L, D_MODEL), jnp.float32), 'Wq': jax.random.normal(ks[1], (D_MODEL, H * HD), jnp.float32) * s, 'Wk': jax.random.normal(ks[2], (D_MODEL, H * HD), jnp.float32) * s, 'Wv': jax.random.normal(ks[3], (D_MODEL, H * HD), jnp.float32) * s, 'Wo': jax.random.normal(ks[4], (H * HD, D_MODEL), jnp.float32) * s, 'Kq': jax.random.normal(ks[5], (H, HD, FD), jnp.float32) * (1.0 / np.sqrt(HD)), 'Kk': jax.random.normal(ks[6], (H, HD, FD), jnp.float32) * (1.0 / np.sqrt(HD))}
    _L0_attn_all = _L0_attn_setup()
    _L0_attn_in = {k: v for k, v in _L0_attn_all.items() if k in ('Wq', 'Wk', 'Wv', 'Wo', 'Kq', 'Kk')}
    del _L0_attn_all

    def _L0_xattn_setup():
        import jax, jax.numpy as jnp
        import numpy as np
        DIM = 256
        CTX_DIM = 192
        HEADS = 16
        key = jax.random.key(seed)
        ks = jax.random.split(key, 7)
        B, N, M = (4, 1024, 64)
        x = jax.random.normal(ks[0], (B, N, DIM), dtype=jnp.float32)
        context = jax.random.normal(ks[1], (B, M, CTX_DIM), dtype=jnp.float32)
        context_mask = jnp.ones((B, M), dtype=bool)
        s_d = 1.0 / np.sqrt(DIM)
        s_c = 1.0 / np.sqrt(CTX_DIM)
        Wq = jax.random.normal(ks[2], (DIM, DIM), dtype=jnp.float32) * s_d
        Wk = jax.random.normal(ks[3], (CTX_DIM, DIM), dtype=jnp.float32) * s_c
        Wv = jax.random.normal(ks[4], (CTX_DIM, DIM), dtype=jnp.float32) * s_c
        Wo = jax.random.normal(ks[5], (DIM, DIM), dtype=jnp.float32) * s_d
        return {'x': x, 'context': context, 'context_mask': context_mask, 'Wq': Wq, 'Wk': Wk, 'Wv': Wv, 'Wo': Wo}
    _L0_xattn_all = _L0_xattn_setup()
    _L0_xattn_in = {k: v for k, v in _L0_xattn_all.items() if k in ('Wq', 'Wk', 'Wv', 'Wo')}
    del _L0_xattn_all

    def _L0_ffn_setup():
        import jax, jax.numpy as jnp
        import numpy as np
        DIM = 256
        E = 8
        K = 2
        EPS = 1e-05

        def _ln(x, g, b):
            mu = jnp.mean(x, axis=-1, keepdims=True)
            var = jnp.mean(jnp.square(x - mu), axis=-1, keepdims=True)
            return (x - mu) * jax.lax.rsqrt(var + EPS) * g + b
        key = jax.random.key(seed)
        ks = jax.random.split(key, 8)
        H = 2 * DIM
        s_in = 1.0 / np.sqrt(DIM)
        s_h = 1.0 / np.sqrt(H)
        return {'x': jax.random.normal(ks[0], (2, 512, DIM), dtype=jnp.float32), 'gate_w': jax.random.uniform(ks[1], (DIM, E), minval=-s_in, maxval=s_in, dtype=jnp.float32), 'w1': jax.random.uniform(ks[2], (E, DIM, H), minval=-s_in, maxval=s_in, dtype=jnp.float32), 'b1': jax.random.uniform(ks[3], (E, H), minval=-s_in, maxval=s_in, dtype=jnp.float32), 'ln1_g': jnp.ones((E, H), dtype=jnp.float32), 'ln1_b': jnp.zeros((E, H), dtype=jnp.float32), 'w2': jax.random.uniform(ks[4], (E, H, DIM), minval=-s_h, maxval=s_h, dtype=jnp.float32), 'b2': jax.random.uniform(ks[5], (E, DIM), minval=-s_h, maxval=s_h, dtype=jnp.float32), 'ln_g': jnp.ones((DIM,), dtype=jnp.float32), 'ln_b': jnp.zeros((DIM,), dtype=jnp.float32)}
    _L0_ffn_all = _L0_ffn_setup()
    _L0_ffn_in = {k: v for k, v in _L0_ffn_all.items() if k in ('gate_w', 'w1', 'b1', 'ln1_g', 'ln1_b', 'w2', 'b2', 'ln_g', 'ln_b')}
    del _L0_ffn_all
    return {'x': x, 'ctx_768': ctx_768, 'mask_BxS2_bf1': mask_BxS2_bf1, 'L0_attn_Wq': _L0_attn_in['Wq'], 'L0_attn_Wk': _L0_attn_in['Wk'], 'L0_attn_Wv': _L0_attn_in['Wv'], 'L0_attn_Wo': _L0_attn_in['Wo'], 'L0_attn_Kq': _L0_attn_in['Kq'], 'L0_attn_Kk': _L0_attn_in['Kk'], 'L0_xattn_Wq': _L0_xattn_in['Wq'], 'L0_xattn_Wk': _L0_xattn_in['Wk'], 'L0_xattn_Wv': _L0_xattn_in['Wv'], 'L0_xattn_Wo': _L0_xattn_in['Wo'], 'L0_ffn_gate_w': _L0_ffn_in['gate_w'], 'L0_ffn_w1': _L0_ffn_in['w1'], 'L0_ffn_b1': _L0_ffn_in['b1'], 'L0_ffn_ln1_g': _L0_ffn_in['ln1_g'], 'L0_ffn_ln1_b': _L0_ffn_in['ln1_b'], 'L0_ffn_w2': _L0_ffn_in['w2'], 'L0_ffn_b2': _L0_ffn_in['b2'], 'L0_ffn_ln_g': _L0_ffn_in['ln_g'], 'L0_ffn_ln_b': _L0_ffn_in['ln_b']}

def reference(x, ctx_768, mask_BxS2_bf1, L0_attn_Wq, L0_attn_Wk, L0_attn_Wv, L0_attn_Wo, L0_attn_Kq, L0_attn_Kk, L0_xattn_Wq, L0_xattn_Wk, L0_xattn_Wv, L0_xattn_Wo, L0_ffn_gate_w, L0_ffn_w1, L0_ffn_b1, L0_ffn_ln1_g, L0_ffn_ln1_b, L0_ffn_w2, L0_ffn_b2, L0_ffn_ln_g, L0_ffn_ln_b):
    import jax
    import jax.numpy as jnp

    def _L0_attn_ref(x, Wq, Wk, Wv, Wo, Kq, Kk):
        import jax, jax.numpy as jnp
        import numpy as np
        B, L, D_MODEL, H, HD, FD = (1, 256, 256, 16, 64, 64)
        EPS = 1e-12

        def _heads(t):
            b, l, _ = t.shape
            return t.reshape(b, l, H, HD).transpose(0, 2, 1, 3)

        def _feature_map(t, K):
            f = jnp.einsum('hdf,bhld->bhlf', K, t)
            feats = jnp.concatenate([jax.nn.softmax(f, axis=-1), jax.nn.softmax(-f, axis=-1)], axis=-1)
            return jnp.maximum(feats, EPS)
        q = _heads(x @ Wq)
        k = _heads(x @ Wk)
        v = _heads(x @ Wv)
        qf = _feature_map(q, Kq)
        kf = _feature_map(k, Kk)
        kv = jnp.cumsum(kf[:, :, :, None, :] * v[..., None], axis=2)
        o = jnp.einsum('bhlf,bhldf->bhld', qf, kv)
        z = jnp.einsum('bhlf,bhlf->bhl', qf, jnp.cumsum(kf, axis=2)) + EPS
        o = o / z[..., None]
        y = o.transpose(0, 2, 1, 3).reshape(x.shape[0], x.shape[1], H * HD)
        return y @ Wo

    def _L0_xattn_ref(x, context, context_mask, Wq, Wk, Wv, Wo):
        import jax, jax.numpy as jnp
        import numpy as np
        DIM = 256
        CTX_DIM = 192
        HEADS = 16
        B, N, _ = x.shape
        M = context.shape[1]
        hd = DIM // HEADS
        scale = hd ** (-0.5)
        q = (x @ Wq).reshape(B, N, HEADS, hd).transpose(0, 2, 1, 3)
        k = (context @ Wk).reshape(B, M, HEADS, hd).transpose(0, 2, 1, 3)
        v = (context @ Wv).reshape(B, M, HEADS, hd).transpose(0, 2, 1, 3)
        scores = jnp.einsum('bhid,bhjd->bhij', q, k) * scale
        max_neg = -jnp.finfo(scores.dtype).max
        scores = jnp.where(context_mask[:, None, None, :], scores, max_neg)
        attn = jax.nn.softmax(scores, axis=-1)
        out = jnp.einsum('bhij,bhjd->bhid', attn, v)
        out = out.transpose(0, 2, 1, 3).reshape(B, N, DIM)
        return out @ Wo

    def _L0_ffn_ref(x, gate_w, w1, b1, ln1_g, ln1_b, w2, b2, ln_g, ln_b):
        import jax, jax.numpy as jnp
        import numpy as np
        DIM = 256
        E = 8
        K = 2
        EPS = 1e-05

        def _ln(x, g, b):
            mu = jnp.mean(x, axis=-1, keepdims=True)
            var = jnp.mean(jnp.square(x - mu), axis=-1, keepdims=True)
            return (x - mu) * jax.lax.rsqrt(var + EPS) * g + b
        shape = x.shape
        xf = x.reshape(-1, shape[-1])
        gates = jax.nn.softmax(xf @ gate_w, axis=-1)
        topw, topi = jax.lax.top_k(gates, K)
        topw = topw / jnp.sum(topw, axis=-1, keepdims=True)
        combine = jnp.sum(topw[:, :, None] * jax.nn.one_hot(topi, E, dtype=xf.dtype), axis=1)
        h = jnp.einsum('td,edh->teh', xf, w1) + b1
        h = _ln(h, ln1_g, ln1_b)
        h = jax.nn.gelu(h, approximate=False)
        y = jnp.einsum('teh,ehd->ted', h, w2) + b2
        out = jnp.einsum('ted,te->td', y, combine)
        out = _ln(out + xf, ln_g, ln_b)
        return out.reshape(shape)
    x = x + _L0_attn_ref(_layernorm(x, axis=-1), L0_attn_Wq, L0_attn_Wk, L0_attn_Wv, L0_attn_Wo, L0_attn_Kq, L0_attn_Kk)
    x = x + _L0_xattn_ref(_layernorm(x, axis=-1), ctx_768, mask_BxS2_bf1, L0_xattn_Wq, L0_xattn_Wk, L0_xattn_Wv, L0_xattn_Wo)
    x = x + _L0_ffn_ref(_layernorm(x, axis=-1), L0_ffn_gate_w, L0_ffn_w1, L0_ffn_b1, L0_ffn_ln1_g, L0_ffn_ln1_b, L0_ffn_w2, L0_ffn_b2, L0_ffn_ln_g, L0_ffn_ln_b)
    return x

_drawn_inputs = setup_inputs


def setup_inputs(seed=0):
    import zlib

    import numpy as np

    out = dict(_drawn_inputs(seed))
    spreads = {'L0_ffn_ln1_g': (1.0, 0.556),
     'L0_ffn_ln1_b': (0.0, 0.608),
     'L0_ffn_ln_g': (1.0, 0.2),
     'L0_ffn_ln_b': (0.0, 0.1)}
    factors = {'L0_ffn_b1': 6.444, 'L0_ffn_b2': 6.441}
    for name, (base, spread) in spreads.items():
        noise = np.random.default_rng([zlib.crc32(name.encode()), seed]).standard_normal(out[name].shape)
        drawn = base * np.exp(spread * noise) if base else spread * noise
        out[name] = jnp.asarray(drawn.astype(out[name].dtype))
    for name, factor in factors.items():
        out[name] = (out[name] * factor).astype(out[name].dtype)
    return out
```

```python
from contextlib import ExitStack

import concourse.bass as bass
from concourse import mybir

P = 128
F32 = mybir.dt.float32
BF16 = mybir.dt.bfloat16
I32 = mybir.dt.int32
U32 = mybir.dt.uint32
U8 = mybir.dt.uint8
ALU = mybir.AluOpType
ACT = mybir.ActivationFunctionType
AX_X = mybir.AxisListType.X

B, L, D = 4, 512, 256
T = B * L // P
TB = L // P
KD = D // P
H, HD = 16, 64
F2 = 2 * HD
VW = 96
G = 4
LN_EPS = 1e-5
FEAT_EPS = 1e-12


def wait(eng, sem, value):
    if not isinstance(value, int) or value > 0:
        eng.wait_ge(sem, value)


class Chain:

    def __init__(self, eng, sem, base=0):
        self.eng, self.sem, self.base, self.n = eng, sem, base, 0

    def did(self, ins):
        ins.then_inc(self.sem, 1)
        self.n += 1

    def wait(self):
        wait(self.eng, self.sem, self.base + self.n)


def make_identity(pool, ident, sem):
    pool.memset(ident, 0.0).then_inc(sem, 1)
    pool.wait_ge(sem, 1)
    pool.affine_select(out=ident, in_=ident, compare_op=ALU.not_equal, fill=1.0, base=0,
                       pattern=[[-1, P]], channel_multiplier=1).then_inc(sem, 1)


def linear_attention(nc, x, Wq, Wk, Wv, Wo, Kq, Kk, xr):
    with ExitStack() as ctx:
        def sb(name, shape, dt=F32):
            return ctx.enter_context(nc.sbuf_tensor(name, shape, dt))

        def ps(name, shape, dt=F32):
            return ctx.enter_context(nc.psum_tensor(name, shape, dt))

        def sem(name):
            return ctx.enter_context(nc.semaphore("a_" + name))

        ident = sb("a_ident", [P, P])
        causal = sb("a_causal", [P, P])
        w_raw = sb("w_raw", [P, 2, KD, H * HD])
        k_diag = sb("k_diag", [P, 2, H // 2, P])
        w_t = sb("w_t", [P, 2, 4, P])
        w_feat = sb("w_feat", [P, 2, KD, H * HD])
        wv = sb("wv", [P, KD, H * HD])
        wo = sb("wo", [P, H // 2, D])
        stats = sb("a_stats", [P, T, 6])
        mv = sb("a_mv", [P, T, 2])
        rstd = sb("a_rstd", [P, T])
        xn = sb("a_xn", [P, D])
        xT = sb("a_xT", [P, KD, P])
        hi = sb("hi", [P, H])
        lo = sb("lo", [P, H])
        fsum = sb("fsum", [P, 2 * H])
        feat = [sb("kf", [P, 2, H, F2]), sb("qf", [P, 2, H, F2])]
        v1 = sb("v1", [P, 2, H, VW])
        fT = [sb("kfT", [P, 2, G, P]), sb("qfT", [P, 2, G, P])]
        am = sb("am", [P, G, P])
        state = sb("state", [P, H, VW])
        z = sb("z", [P, G])
        rz = sb("rz", [P, G])
        o_sb = sb("o_sb", [P, H * HD])
        oT = sb("oT", [P, H // 2, P])

        pP = ps("pP", [P, 1024])
        pT = [ps("pT0", [P, 512]), ps("pT1", [P, 512])]
        pA = ps("pA", [P, G, P])
        pO = ps("pO", [P, 512])
        pD = ps("pD", [P, 512])
        pW = ps("pW", [P, 512])
        o_ps = pO[:, 0:G * VW].rearrange("p (h v) -> p h v", h=G)
        d_ps = pD[:, 0:G * VW].rearrange("p (h v) -> p h v", h=G)
        y_ps = pW[:, 0:D]
        x_ps = pW[:, D:2 * D]

        s_x, s_w, s_kd, s_wv, s_wo = sem("x"), sem("w"), sem("kd"), sem("wv"), sem("wo")
        s_id, s_cz, s_kz, s_vz = sem("ident"), sem("causal"), sem("kdiag0"), sem("vzero")
        s_dve = sem("dve")
        s_var, s_std = sem("var"), sem("std")
        w_tr, w_ev, w_mm, w_cp = sem("w_tr"), sem("w_ev"), sem("w_mm"), sem("w_cp")
        xn_ready, x_tr, xT_ready = sem("xn"), sem("x_tr"), sem("xT")
        proj = [sem("k_proj"), sem("q_proj")]
        v_proj, v_copied = sem("v_proj"), sem("v_copied")
        shifted = [sem("k_shifted"), sem("q_shifted")]
        expd = [sem("k_exp"), sem("q_exp")]
        summed = [sem("k_sum"), sem("q_sum")]
        scaled = [sem("k_scaled"), sem("q_scaled")]
        f_ready = [sem("k_feat"), sem("q_feat")]
        f_tr = [sem("k_tr"), sem("q_tr")]
        fT_ready = [sem("kT"), sem("qT")]
        a_done, a_masked = sem("a_done"), sem("a_masked")
        d_done, s_upd = sem("d_done"), sem("state")
        o_done, o_norm = sem("o_done"), sem("o_norm")
        o_tr, oT_ready = sem("o_tr"), sem("oT")
        y_done, x1_done = sem("y_done"), sem("x1")

        ROUNDS = 8
        DVE_BATCH = 56

        with nc.Block() as block:

            @block.sync
            def _(sp):
                sp.dma_start(xr[:, :, :], x.rearrange("b (c p) d -> p (b c) d", p=P)).then_inc(s_x, 16)
                for m, w in enumerate((Wk, Wq)):
                    sp.dma_start(w_raw[:, m], w.rearrange("(k p) n -> p k n", p=P)).then_inc(s_w, 16)
                sp.wait_ge(s_kz, 1)
                for m, kk in enumerate((Kk, Kq)):
                    pairs = kk.rearrange("(j two) d f -> two d j f", two=2)
                    for s in range(2):
                        sp.dma_start(k_diag[HD * s:HD * s + HD, m, :, HD * s:HD * s + HD],
                                     pairs[s]).then_inc(s_kd, 16)
                sp.dma_start(wv[:, :, :], Wv.rearrange("(k p) n -> p k n", p=P)).then_inc(s_wv, 16)
                sp.dma_start(wo[:, :, :], Wo.rearrange("(k p) n -> p k n", p=P)).then_inc(s_wo, 16)

            @block.gpsimd
            def _(pool):
                pool.memset(k_diag[:, :, :, :], 0.0).then_inc(s_kz, 1)
                make_identity(pool, ident[:, :], s_id)
                pool.memset(causal[:, :], 1.0).then_inc(s_cz, 1)
                pool.wait_ge(s_cz, 1)
                pool.affine_select(out=causal[:, :], in_=causal[:, :], compare_op=ALU.is_ge, fill=0.0,
                                   base=0, pattern=[[1, P]], channel_multiplier=-1).then_inc(s_cz, 1)
                pool.memset(v1[:, :, :, HD:VW], 0.0).then_inc(s_vz, 1)
                pool.wait_ge(s_vz, 1)
                pool.memset(v1[:, :, :, HD:HD + 1], 1.0).then_inc(s_vz, 1)

                def scale(m, t, par):
                    wait(pool, summed[m], t + 1)
                    e = feat[m][:, par].rearrange("p h (s f) -> p (h s) f", s=2)
                    nc.gpsimd.tensor_tensor(e, e, fsum[:, :].unsqueeze(2).broadcast_to([P, 2 * H, HD]),
                                            ALU.mult).then_inc(scaled[m], 1)

                scale(0, 0, 0)
                scale(1, 0, 0)

                def batch(b, last):
                    for c in range(TB):
                        if not (last and c == TB - 1):
                            scale(0, TB * b + c + 1, (c + 1) % 2)
                            scale(1, TB * b + c + 1, (c + 1) % 2)

                with pool.Fori(0, B - 1) as b:
                    batch(b, False)
                batch(B - 1, True)

            @block.tensor
            def _(pe):
                pe.wait_ge(s_id, 2)
                pe.wait_ge(s_w, 32)

                def w_transposes(r):
                    m, j = r // 4, 2 * (r % 4)
                    if r >= 2:
                        wait(pe, w_ev, r - 1)
                    for i in range(4):
                        col = P * (j + i // 2)
                        ins = pe.transpose(pT[r % 2][:, P * i:P * i + P],
                                           w_raw[:, m, i % 2, col:col + P], ident[:, :])
                    ins.then_inc(w_tr, 1)

                def w_products(r):
                    m, j = r // 4, 2 * (r % 4)
                    wait(pe, w_ev, r + 1)
                    if r >= 2:
                        wait(pe, w_cp, r - 1)
                    out = (pP[:, 0:512], pP[:, 512:1024])[r % 2]
                    for i in range(4):
                        ins = pe.matmul(out[:, P * i:P * i + P], w_t[:, r % 2, i, :],
                                        k_diag[:, m, j + i // 2, :], start=True, stop=True)
                    ins.then_inc(w_mm, 1)

                w_transposes(0)
                pe.wait_ge(s_kd, 64)
                for r in range(ROUNDS):
                    if r + 1 < ROUNDS:
                        w_transposes(r + 1)
                    w_products(r)
                pe.wait_ge(w_cp, ROUNDS)

                def x_transposes(t):
                    wait(pe, xn_ready, t + 1)
                    wait(pe, x1_done, t - 2)
                    for k in range(KD):
                        ins = pe.transpose(x_ps[:, P * k:P * k + P], xn[:, P * k:P * k + P], ident[:, :])
                    ins.then_inc(x_tr, 1)

                def project(w, done):
                    for half in range(2):
                        for k in range(KD):
                            ins = pe.matmul(pP[:, 512 * half:512 * half + 512], xT[:, k, :],
                                            w[:, k, 512 * half:512 * half + 512],
                                            start=(k == 0), stop=(k == KD - 1))
                    ins.then_inc(done, 1)

                def project_k(t):
                    wait(pe, xT_ready, t + 1)
                    wait(pe, v_copied, t)
                    project(w_feat[:, 0], proj[0])

                def project_q(t):
                    wait(pe, shifted[0], t + 1)
                    project(w_feat[:, 1], proj[1])

                def project_v(t):
                    wait(pe, shifted[1], t + 1)
                    project(wv, v_proj)

                def transposes(t, g, par):
                    for m in (1, 0):
                        if g == 0:
                            wait(pe, f_ready[m], t + 1)
                        if g == 1:
                            wait(pe, oT_ready, 2 * t)
                        wait(pe, fT_ready[m], 4 * t + g)
                        for h in range(G):
                            ins = pe.transpose(pT[m][:, P * h:P * h + P], feat[m][:, par, G * g + h, :],
                                               ident[:, :])
                        ins.then_inc(f_tr[m], 1)

                def chunk_scores(t, g):
                    wait(pe, fT_ready[0], 4 * t + g + 1)
                    wait(pe, fT_ready[1], 4 * t + g + 1)
                    wait(pe, a_masked, 4 * t + g)
                    for h in range(G):
                        ins = pe.matmul(pA[:, h, :], fT[0][:, g % 2, h, :], fT[1][:, g % 2, h, :],
                                        start=True, stop=True)
                    ins.then_inc(a_done, 1)

                def state_delta(b, c, g, par):
                    wait(pe, v_copied, TB * b + c + 1)
                    wait(pe, s_upd, 12 * b + 4 * c + g)
                    for h in range(G):
                        ins = pe.matmul(d_ps[:, h, :], feat[0][:, par, G * g + h, :],
                                        v1[:, par, G * g + h, :], start=True, stop=True)
                    ins.then_inc(d_done, 1)

                def outputs(b, c, g, par):
                    t = TB * b + c
                    wait(pe, v_copied, t + 1)
                    wait(pe, o_norm, 4 * t + g)
                    if c:
                        wait(pe, s_upd, 12 * b + 4 * (c - 1) + g + 1)
                    wait(pe, a_masked, 4 * t + g + 1)
                    for h in range(G):
                        if c:
                            pe.matmul(o_ps[:, h, :], fT[1][:, g % 2, h, :], state[:, G * g + h, :],
                                      start=True, stop=False)
                        ins = pe.matmul(o_ps[:, h, :], am[:, h, :], v1[:, par, G * g + h, :],
                                        start=(c == 0), stop=True)
                    ins.then_inc(o_done, 1)

                def o_transposes(t, next_ready):
                    wait(pe, o_norm, 4 * t + 4)
                    for half in range(2):
                        wait(pe, fT_ready[half], next_ready)
                        for j in range(4):
                            col = P * (4 * half + j)
                            ins = pe.transpose(pT[half][:, P * j:P * j + P], o_sb[:, col:col + P],
                                               ident[:, :])
                        ins.then_inc(o_tr, 1)

                def out_product(t, xT_count):
                    wait(pe, oT_ready, 2 * t + 2)
                    wait(pe, xT_ready, xT_count)
                    wait(pe, x1_done, t)
                    for j in range(H // 2):
                        ins = pe.matmul(y_ps, oT[:, j, :], wo[:, j, :], start=(j == 0), stop=(j == H // 2 - 1))
                    ins.then_inc(y_done, 1)

                x_transposes(0)
                project_k(0)
                project_q(0)
                pe.wait_ge(s_wv, 16)
                project_v(0)
                x_transposes(1)
                project_k(1)
                transposes(0, 0, 0)
                pe.wait_ge(s_wo, 16)

                def batch(b, last):
                    for c in range(TB):
                        t, par = TB * b + c, c % 2
                        has1, has2 = not (last and c == TB - 1), not (last and c >= TB - 2)
                        for g in range(G):
                            if g < G - 1:
                                transposes(t, g + 1, par)
                            elif has1:
                                transposes(t + 1, 0, 1 - par)
                            if g == 0 and has1:
                                project_q(t + 1)
                            if g == 1 and has1:
                                project_v(t + 1)
                            chunk_scores(t, g)
                            if c < TB - 1:
                                state_delta(b, c, g, par)
                            outputs(b, c, g, par)
                        if has2:
                            x_transposes(t + 2)
                        o_transposes(t, 4 * t + 5 if has1 else 4 * t + 4)
                        if has2:
                            project_k(t + 2)
                        out_product(t, t + 3 if has2 else T)

                with pe.Fori(0, B - 1) as b:
                    batch(b, False)
                batch(B - 1, True)

            @block.scalar
            def _(act):
                act.wait_ge(s_var, 1)
                nc.scalar.activation(rstd[:, :], rstd[:, :], ACT.Sqrt).then_inc(s_std, 1)
                for r in range(ROUNDS):
                    wait(act, w_tr, r + 1)
                    if r >= 2:
                        wait(act, w_mm, r - 1)
                    nc.scalar.copy(w_t[:, r % 2], pT[r % 2][:, :].rearrange("p (i n) -> p i n", i=4)
                                   ).then_inc(w_ev, 1)

                def x_copy(t):
                    wait(act, x_tr, t + 1)
                    wait(act, v_proj, t)
                    nc.scalar.copy(xT[:, :, :], x_ps.rearrange("p (k n) -> p k n", k=KD)).then_inc(xT_ready, 1)

                def exponentials(m, t, par):
                    wait(act, shifted[m], t + 1)
                    nc.scalar.activation(feat[m][:, par], feat[m][:, par], ACT.Exp).then_inc(expd[m], 1)

                def v_copy(t, par):
                    wait(act, v_proj, t + 1)
                    wait(act, o_done, 4 * (t - 1))
                    wait(act, s_vz, 2)
                    nc.scalar.copy(v1[:, par, :, 0:HD], pP[:, :].rearrange("p (h d) -> p h d", h=H)
                                   ).then_inc(v_copied, 1)

                def f_copies(t, g):
                    for m in (1, 0):
                        wait(act, f_tr[m], 4 * t + g + 1)
                        wait(act, o_done, 4 * t + g - 1)
                        nc.scalar.copy(fT[m][:, g % 2], pT[m][:, :].rearrange("p (h n) -> p h n", h=G)
                                       ).then_inc(fT_ready[m], 1)

                x_copy(0)
                exponentials(0, 0, 0)
                exponentials(1, 0, 0)
                v_copy(0, 0)
                x_copy(1)
                exponentials(0, 1, 1)
                f_copies(0, 0)

                def batch(b, last):
                    for c in range(TB):
                        t, par = TB * b + c, c % 2
                        has1, has2 = not (last and c == TB - 1), not (last and c >= TB - 2)
                        f_copies(t, 1)
                        f_copies(t, 2)
                        if has1:
                            exponentials(1, t + 1, 1 - par)
                            v_copy(t + 1, 1 - par)
                        f_copies(t, 3)
                        if has1:
                            f_copies(t + 1, 0)
                        if has2:
                            x_copy(t + 2)
                        for half in range(2):
                            wait(act, o_tr, 2 * t + half + 1)
                            wait(act, y_done, t)
                            nc.scalar.copy(oT[:, 4 * half:4 * half + 4, :],
                                           pT[half][:, :].rearrange("p (j n) -> p j n", j=4)
                                           ).then_inc(oT_ready, 1)
                        if has2:
                            exponentials(0, t + 2, par)

                with act.Fori(0, B - 1) as b:
                    batch(b, False)
                batch(B - 1, True)

            @block.vector
            def _(dve):
                own = Chain(dve, s_dve)
                dve.wait_ge(s_x, 16)
                for t in range(T):
                    own.did(nc.vector.bn_stats(stats[:, t, :], xr[:, t, :]))
                own.wait()
                for t in range(T):
                    own.did(nc.vector.bn_aggr(mv[:, t, :], stats[:, t, :]))
                own.wait()
                nc.vector.tensor_scalar(rstd[:, :], mv[:, :, 1], LN_EPS, None, ALU.add).then_inc(s_var, 1)
                dve.wait_ge(s_std, 1)
                own.did(nc.vector.reciprocal(rstd[:, :], rstd[:, :]))
                own.wait()

                def normalise(t):
                    wait(dve, x_tr, t)
                    nc.vector.tensor_scalar(xn[:, :], xr[:, bass.ds(t, 1), :].rearrange("p a d -> p (a d)"),
                                            mv[:, bass.ds(t, 1), 0], rstd[:, bass.ds(t, 1)],
                                            ALU.subtract, ALU.mult).then_inc(xn_ready, 1)

                normalise(0)
                for r in range(ROUNDS):
                    wait(dve, w_mm, r + 1)
                    m, col = r // 4, 2 * P * (r % 4)
                    nc.vector.tensor_copy(
                        w_feat[:, m, :, col:col + 2 * P].rearrange("p k (j n) -> p j k n", j=2),
                        pP[:, 512 * (r % 2):512 * (r % 2) + 512].rearrange("p (j k n) -> p j k n", j=2, k=KD)
                    ).then_inc(w_cp, 1)

                def shift(m, t, par, own):
                    f = pP[:, :].rearrange("p (h f) -> p h f", h=H)
                    wait(dve, proj[m], t + 1)
                    wait(dve, o_done, 4 * (t - 1))
                    own.did(nc.vector.tensor_reduce(hi[:, :], f, AX_X, ALU.max))
                    own.did(nc.vector.tensor_reduce(lo[:, :], f, AX_X, ALU.min))
                    own.wait()
                    nc.vector.tensor_tensor(feat[m][:, par, :, 0:HD], f,
                                            hi[:, :].unsqueeze(2).broadcast_to([P, H, HD]), ALU.subtract)
                    nc.vector.tensor_tensor(feat[m][:, par, :, HD:F2],
                                            lo[:, :].unsqueeze(2).broadcast_to([P, H, HD]), f,
                                            ALU.subtract).then_inc(shifted[m], 1)

                def denominators(m, t, par, own):
                    wait(dve, expd[m], t + 1)
                    wait(dve, scaled[1 - m], t + m)
                    own.did(nc.vector.tensor_reduce(
                        fsum[:, :], feat[m][:, par].rearrange("p h (s f) -> p (h s) f", s=2), AX_X, ALU.add))
                    own.wait()
                    nc.vector.reciprocal(fsum[:, :], fsum[:, :]).then_inc(summed[m], 1)

                def clamp(m, t, par):
                    wait(dve, scaled[m], t + 1)
                    nc.vector.tensor_scalar(feat[m][:, par], feat[m][:, par], FEAT_EPS, None,
                                            ALU.max).then_inc(f_ready[m], 1)

                def mask(t, g):
                    wait(dve, a_done, 4 * t + g + 1)
                    wait(dve, o_done, 4 * t + g)
                    nc.vector.tensor_tensor(am[:, :, :], pA[:, :, :],
                                            causal[:, :].unsqueeze(1).broadcast_to([P, G, P]),
                                            ALU.mult).then_inc(a_masked, 1)

                def update(b, c, g):
                    wait(dve, d_done, 12 * b + 4 * c + g + 1)
                    wait(dve, o_done, 4 * (TB * b + c) + g + 1)
                    st = state[:, G * g:G * g + G, :]
                    if c == 0:
                        nc.vector.tensor_copy(st, d_ps).then_inc(s_upd, 1)
                    else:
                        nc.vector.tensor_tensor(st, st, d_ps, ALU.add).then_inc(s_upd, 1)

                def normalise_o(t, g, own):
                    wait(dve, o_done, 4 * t + g + 1)
                    if g == 0:
                        wait(dve, o_tr, 2 * t)
                    own.did(nc.vector.tensor_scalar(z[:, :], o_ps[:, :, HD], FEAT_EPS, None, ALU.add))
                    own.wait()
                    own.did(nc.vector.reciprocal(rz[:, :], z[:, :]))
                    own.wait()
                    nc.vector.tensor_tensor(
                        o_sb[:, 256 * g:256 * g + 256].rearrange("p (h d) -> p h d", h=G),
                        o_ps[:, :, 0:HD], rz[:, :].unsqueeze(2).broadcast_to([P, G, HD]),
                        ALU.mult).then_inc(o_norm, 1)

                def residual(t):
                    wait(dve, y_done, t + 1)
                    xt = xr[:, bass.ds(t, 1), :].rearrange("p a d -> p (a d)")
                    nc.vector.tensor_tensor(xt, xt, y_ps, ALU.add).then_inc(x1_done, 1)

                shift(0, 0, 0, own)
                denominators(0, 0, 0, own)
                shift(1, 0, 0, own)
                normalise(1)
                denominators(1, 0, 0, own)
                clamp(0, 0, 0)
                clamp(1, 0, 0)
                shift(0, 1, 1, own)
                dve.wait_ge(s_cz, 2)
                before = own.n

                def batch(b, last):
                    own = Chain(dve, s_dve, DVE_BATCH * b + before)
                    for c in range(TB):
                        t, par = TB * b + c, c % 2
                        has1, has2 = not (last and c == TB - 1), not (last and c >= TB - 2)
                        for g in range(G):
                            mask(t, g)
                            if g == 0 and has1:
                                denominators(0, t + 1, 1 - par, own)
                                shift(1, t + 1, 1 - par, own)
                            if g == 1 and has1:
                                denominators(1, t + 1, 1 - par, own)
                            if g == 2 and has1:
                                clamp(0, t + 1, 1 - par)
                                clamp(1, t + 1, 1 - par)
                            if c < TB - 1:
                                update(b, c, g)
                            normalise_o(t, g, own)
                            if g == 1 and has2:
                                normalise(t + 2)
                        if has2:
                            shift(0, t + 2, par, own)
                        residual(t)
                    assert last or own.n == DVE_BATCH, own.n

                with dve.Fori(0, B - 1) as b:
                    batch(b, False)
                batch(B - 1, True)


CD = 192
CS = CD // 2
M = 1024
JT = M // P
XH, XD = 16, 16
XV = 32
PAIRS = ((0, 0), (0, 1), (1, 0), (1, 1), (0, 2), (2, 0))
AUG = XD * len(PAIRS)
KR = AUG + 4
MASKED = 1e30
NG = B * G


def cross_attention(nc, ctx_in, mask, Wq, Wk, Wv, Wo, k_scr, q_scr, aug_scr, xr):
    with ExitStack() as ctx:
        def sb(name, shape, dt=F32):
            return ctx.enter_context(nc.sbuf_tensor(name, shape, dt))

        def ps(name, shape, dt=F32):
            return ctx.enter_context(nc.psum_tensor(name, shape, dt))

        def sem(name):
            return ctx.enter_context(nc.semaphore("b_" + name))

        ident = sb("b_ident", [P, P])
        ident_h = sb("b_ident_h", [P, P], BF16)
        wq = sb("b_wq", [P, KD, D])
        wo = sb("b_wo", [P, KD, D])
        wk = sb("b_wk", [CS, 2, D])
        wv = sb("b_wv", [CS, 2, D])
        m_col = sb("m_col", [P, B, JT], U8)
        any_on = sb("any_on", [P, B])
        big = sb("big", [P, B])
        q_scale = sb("q_scale", [P, B])
        bias = sb("bias", [P, G, JT])
        last_row = sb("last_row", [P, 1])
        other_rows = sb("other_rows", [P, 1])
        q_aug = sb("q_aug", [P, L], BF16)
        stats = sb("b_stats", [P, T, 6])
        mv = sb("b_mv", [P, T, 2])
        rstd = sb("b_rstd", [P, T])
        xn = sb("b_xn", [P, TB, D])
        xT = sb("b_xT", [P, KD, L])
        cx = sb("cx", [P, JT, CD])
        cT = sb("cT", [CS, 2, M])
        rest = sb("rest", [P, 512])
        parts = sb("parts", [P, 2, 3, 2, 512], BF16)
        ks = sb("ks", [P, 2, XH, M], BF16)
        qs = sb("qs", [P, 2, XH, L], BF16)
        v_new = sb("v_new", [P, G, JT, G * XD])
        v1 = sb("b_v1", [P, G, JT, G, XV])
        neg_max = sb("neg_max", [P, 2, TB, G])
        max_rest = sb("max_rest", [P, TB, G])
        max_parts = sb("max_parts", [P, TB, G, XV], BF16)
        pt = sb("pt", [P, 2, G, L])
        ot = sb("ot", [P, L])
        rz = sb("b_rz", [P, TB, G])
        o = sb("b_o", [P, TB, D])
        oT = xT
        m_row = qs[:, 1, 0:4, :].rearrange("p h n -> p (h n)").bitcast(U8).rearrange("p (b m) -> p b m", b=B)
        aug_f = pt[:, :, :, :].rearrange("p s i n -> p (s i n)").rearrange("p (b m) -> p b m", b=B)
        k_aug = ks[:, 1, 0:B, :]

        pS1 = ps("pS1", [P, 2, M])
        pS2 = ps("pS2", [P, 2, L])
        pO = ps("b_pO", [P, L])
        pM = ps("pM", [P, 512])

        s_w, s_mask, s_cx, s_id = sem("w"), sem("mask"), sem("cx"), sem("ident")
        s_dve, s_act = sem("dve"), sem("act")
        s_z, s_row, s_var, s_std, s_aug = sem("zero"), sem("row"), sem("var"), sem("std"), sem("aug")
        xn_ready = sem("xn")
        filled, emptied = sem("filled"), sem("emptied")
        head_done, split_done = sem("head"), sem("split")
        stored = [sem("k0_stored"), sem("k1_stored"), sem("q_stored")]
        aug_stored = sem("aug_stored")
        k_loaded, q_loaded = sem("k_loaded"), sem("q_loaded")
        placed = sem("placed")
        s1_done, max_done = sem("s1"), sem("max")
        m_ready = sem("m_ready")
        s2_done, exp_done, av_done, ot_ready = sem("s2"), sem("exp"), sem("av"), sem("ot")

        N_LOAD = 16 * (len(PAIRS) + 1)

        def small_steps(hg, j, first, last):
            plan = {(0, 2): [("o_turn", 3)] * (not first)}
            for g in range(1, G):
                plan[g, 2] = [("o_turn", g - 1)]
            if not first:
                plan[0, 3], plan[0, 4] = [("oT", 0)], [("oT", 1)]
                plan[0, 5], plan[0, 6] = [("y", 0)], [("y", 1)]
            for g in range(G):
                plan[g, 6] = plan.get((g, 6), []) + [("m_turn", g + 1)] * (g < G - 1 or not last)
            if not last:
                plan[0, 0], plan[0, 1] = [("cT", 0)], [("cT", 1)]
                plan[1, 0], plan[1, 1] = [("cT", 2)], [("cT", 3)]
                plan[1, 3], plan[1, 4] = [("k", 0), ("xT", 0)], [("k", 1), ("xT", 1)]
                plan[1, 5], plan[1, 6] = [("k", 2), ("k", 3)], [("q", 0), ("q", 1)] + plan[1, 6]
                for i in range(4):
                    plan[2, (0, 1, 3, 4)[i]] = [("v", i)]
            return plan.get((hg, j), [])

        PREPARE = [("cT", i) for i in range(4)] + [("k", i) for i in range(4)] + \
            [("xT", 0), ("xT", 1), ("q", 0), ("q", 1)] + [("v", i) for i in range(4)]
        FINISH = [("o_turn", 3), ("oT", 0), ("oT", 1), ("y", 0), ("y", 1)]

        OWN_FIRST, OWN_MIDDLE = 21, 22

        def slot(b, n):
            return bass.ds((3 * b + n) % 2, 1)

        def batch_of(b, kind, i, hg):
            if kind in ("cT", "k", "v", "xT", "q"):
                return b + 1
            return b - 1 if kind in ("oT", "y") or (kind == "o_turn" and i > hg) else b

        def steps_of(first, last):
            return sum(len(small_steps(g, j, first, last)) for g in range(G) for j in range(JT))

        START = len(PREPARE) + 1
        FIRST, MIDDLE = steps_of(True, False), steps_of(False, False)

        def steps_before(b):
            return (b - 1) * MIDDLE + (START + FIRST)

        def score_units(hg, j, last):
            ahead, u = (hg + 1, 2 * j + 4) if j < 6 else (hg + 2, 2 * j - 12)
            if ahead >= G and last:
                return []
            return [(ahead // G, ahead % G, u), (ahead // G, ahead % G, u + 1)]

        with nc.Block() as block:

            @block.sync
            def _(sp):
                def load_cx(b):
                    sp.dma_start(cx[:, :, :], ctx_in[b].rearrange("(j p) c -> p j c", p=P)).then_inc(s_cx, 16)

                def stack_k(b):
                    for half in range(2):
                        n = 3 * b + half
                        wait(sp, split_done, 2 * (n + 1))
                        for c in range(3):
                            sp.dma_start(k_scr[b, c].rearrange("(m p) n -> p m n", p=P)[:, :, 512 * half:512 * half + 512],
                                         parts[:, n % 2, c]).then_inc(stored[half], 16)
                    for half in range(2):
                        wait(sp, stored[half], 48 * (b + 1))
                    wait(sp, s2_done, G * JT * G * (b - 1))
                    for s, pair in enumerate(PAIRS):
                        sp.dma_start(ks[XD * s:XD * s + XD, b % 2],
                                     k_scr[b, pair[1]].rearrange("(h d) n -> d h n", d=XD)).then_inc(k_loaded, 16)
                    sp.dma_start(ks[AUG:KR, b % 2],
                                 aug_scr[b].unsqueeze(1).broadcast_to([4, XH, M])).then_inc(k_loaded, 16)

                def stack_q(b):
                    n = 3 * b + 2
                    wait(sp, split_done, 2 * (n + 1))
                    for c in range(3):
                        sp.dma_start(q_scr[b, c].rearrange("(m p) n -> p m n", p=P),
                                     parts[:, n % 2, c]).then_inc(stored[2], 16)
                    wait(sp, stored[2], 48 * (b + 1))
                    for s, pair in enumerate(PAIRS):
                        sp.dma_start(qs[XD * s:XD * s + XD, b % 2],
                                     q_scr[b, pair[0]].rearrange("(h d) n -> d h n", d=XD)).then_inc(q_loaded, 16)
                    sp.dma_start(qs[AUG:KR, b % 2],
                                 q_aug[AUG:KR, :].unsqueeze(1).broadcast_to([4, XH, L])).then_inc(q_loaded, 16)

                load_cx(0)
                flat = mask.rearrange("b m -> (b m)").unsqueeze(0)
                sp.dma_start(m_row.rearrange("p b m -> p (b m)"),
                             flat.broadcast_to([P, B * M])).then_inc(s_mask, 16)
                with nc.allow_non_contiguous_dma(reason="4096 bytes of the mask"):
                    sp.dma_start(m_col[:, :, :], mask.rearrange("b (j p) -> p b j", p=P)).then_inc(s_mask, 16)
                for w, src in ((wk, Wk), (wv, Wv)):
                    sp.dma_start(w[:, :, :], src.rearrange("(s p) n -> p s n", p=CS)).then_inc(s_w, 16)
                for w, src in ((wq, Wq), (wo, Wo)):
                    sp.dma_start(w[:, :, :], src.rearrange("(k p) n -> p k n", p=P)).then_inc(s_w, 16)
                sp.wait_ge(s_aug, 3)
                for b in range(B):
                    sp.dma_start(aug_scr[b], k_aug[AUG:KR, b]).then_inc(aug_stored, 16)
                wait(sp, filled, 4)
                load_cx(1)
                sp.wait_ge(aug_stored, 16 * B)
                stack_k(0)
                stack_q(0)
                for b in range(1, B):
                    n = sum(len(small_steps(0, j, b == 1, False)) for j in range(JT)) + 2
                    if b + 1 < B:
                        wait(sp, filled, n + (START if b == 1 else steps_before(b - 1)))
                        load_cx(b + 1)
                    stack_k(b)
                    stack_q(b)

            @block.gpsimd
            def _(pool):
                make_identity(pool, ident[:, :], s_id)
                pool.memset(last_row[:, :], 0.0).then_inc(s_row, 1)
                pool.wait_ge(s_row, 1)
                pool.affine_select(out=last_row[:, :], in_=last_row[:, :], compare_op=ALU.not_equal, fill=1.0,
                                   base=-(KR - 1), pattern=[[0, 1]], channel_multiplier=1).then_inc(s_row, 1)
                pool.memset(q_aug[:, :], 0.0).then_inc(s_row, 1)
                pool.memset(max_parts[:, :, :, :], 0.0).then_inc(s_z, 1)
                pool.memset(v1[:, :, :, :, XD:XV], 0.0).then_inc(s_z, 1)
                pool.wait_ge(s_z, 2)
                pool.memset(v1[:, :, :, :, XD:XD + 1], 1.0).then_inc(s_z, 1)

            @block.tensor
            def _(pe):
                def small(b, kind, i, n):
                    wait(pe, emptied, n)
                    if kind == "cT":
                        wait(pe, s_cx, 16 * (b + 1))
                        for q in range(4):
                            j, s = 2 * i + q // 2, q % 2
                            ins = pe.transpose(pM[0:CS, P * q:P * q + P], cx[:, j, CS * s:CS * s + CS],
                                               ident[:, :])
                    elif kind == "k":
                        half, m = i // 2, i % 2
                        for s in range(2):
                            ins = pe.matmul(pM[:, :], wk[:, s, P * m:P * m + P],
                                            cT[:, s, 512 * half:512 * half + 512],
                                            start=(s == 0), stop=(s == 1))
                    elif kind == "v":
                        for q in range(2):
                            j = 2 * i + q
                            for s in range(2):
                                ins = pe.matmul(pM[:, D * q:D * q + D], cT[:, s, P * j:P * j + P],
                                                wv[:, s, :], start=(s == 0), stop=(s == 1))
                    elif kind == "xT":
                        wait(pe, xn_ready, b + 1)
                        for q in range(4):
                            t, k = 2 * i + q // 2, q % 2
                            ins = pe.transpose(pM[:, P * q:P * q + P], xn[:, t, P * k:P * k + P],
                                               ident[:, :])
                    elif kind == "q":
                        for k in range(KD):
                            ins = pe.matmul(pM[:, :], wq[:, k, P * i:P * i + P], xT[:, k, :],
                                            start=(k == 0), stop=(k == KD - 1))
                    elif kind == "m_turn":
                        wait(pe, m_ready, G * b + i + 1)
                        for t in range(TB):
                            ins = pe.transpose(pM[:, 64 * t:64 * t + 64].bitcast(BF16),
                                               max_parts[:, t, :, :].rearrange("p h v -> p (h v)"),
                                               ident_h[:, :])
                    elif kind == "o_turn":
                        wait(pe, ot_ready, G * b + i + 1)
                        for t in range(TB):
                            ins = pe.transpose(pM[:, P * t:P * t + P], ot[:, P * t:P * t + P], ident[:, :])
                    elif kind == "oT":
                        for t in range(TB):
                            ins = pe.transpose(pM[:, P * t:P * t + P], o[:, t, P * i:P * i + P], ident[:, :])
                    elif kind == "y":
                        for q in range(2):
                            t = 2 * i + q
                            for k in range(KD):
                                ins = pe.matmul(pM[:, D * q:D * q + D], oT[:, k, P * t:P * t + P],
                                                wo[:, k, :], start=(k == 0), stop=(k == KD - 1))
                    ins.then_inc(filled, 1)

                def scores_by_token(b, hg, u):
                    U = 16 * (G * b + hg) + u
                    t, h, slot = u // G, G * hg + u % G, u % 2
                    if u == 0 and hg == 0:
                        wait(pe, k_loaded, N_LOAD * (b + 1))
                        wait(pe, q_loaded, N_LOAD * (b + 1))
                    wait(pe, max_done, U - 1)
                    par = b % 2
                    for half in range(2):
                        ins = pe.matmul(
                            pS1[:, slot, 512 * half:512 * half + 512],
                            qs[0:KR, bass.ds(par, 1), h, P * t:P * t + P].rearrange("r a n -> r (a n)"),
                            ks[0:KR, bass.ds(par, 1), h, 512 * half:512 * half + 512
                               ].rearrange("r a n -> r (a n)"), start=True, stop=True)
                    ins.then_inc(s1_done, 1)

                def scores_by_context(b, hg, j, i, steps):
                    n = G * (JT * (G * b + hg) + j) + i
                    if j == 0 and i == 0:
                        wait(pe, emptied, steps)
                    wait(pe, exp_done, n - 1)
                    par, h = b % 2, G * hg + i
                    pe.matmul(pS2[:, i % 2, :],
                              ks[0:KR, bass.ds(par, 1), h, P * j:P * j + P].rearrange("r a n -> r (a n)"),
                              qs[0:KR, bass.ds(par, 1), h, :].rearrange("r a n -> r (a n)"),
                              start=True, stop=True).then_inc(s2_done, 1)

                def weighted_values(b, hg, j):
                    n = G * b + hg
                    wait(pe, exp_done, G * (JT * n + j + 1))
                    if j == 0:
                        wait(pe, ot_ready, n)
                        wait(pe, placed, n + 1)
                    for i in range(G):
                        ins = pe.matmul(pO[XV * i:XV * i + XV, :], v1[:, hg, j, i, :], pt[:, j % 2, i, :],
                                        start=(j == 0), stop=(j == JT - 1))
                    ins.then_inc(av_done, 1)

                pe.wait_ge(s_id, 3)
                pe.wait_ge(s_w, 64)
                pe.wait_ge(s_z, 3)
                for n, (kind, i) in enumerate(PREPARE):
                    small(0, kind, i, n)
                for u in range(16):
                    scores_by_token(0, 0, u)
                small(0, "m_turn", 0, START - 1)
                for u in range(4):
                    scores_by_token(0, 1, u)

                def batch(b, start, first, last):
                    n = 0
                    for hg in range(G):
                        for j in range(JT):
                            units = score_units(hg, j, last)
                            for i in range(G):
                                scores_by_context(b, hg, j, i, start + n)
                                if i == 1:
                                    for ahead, g, u in units[:1]:
                                        scores_by_token(b + ahead, g, u)
                                    if j:
                                        weighted_values(b, hg, j - 1)
                                    elif hg:
                                        weighted_values(b, hg - 1, JT - 1)
                                    elif not first:
                                        weighted_values(b - 1, G - 1, JT - 1)
                            for ahead, g, u in units[1:]:
                                scores_by_token(b + ahead, g, u)
                            for kind, i in small_steps(hg, j, first, last):
                                small(batch_of(b, kind, i, hg), kind, i, start + n)
                                n += 1
                    return start + n

                batch(0, START, True, False)
                with pe.Fori(1, B - 1) as b:
                    batch(b, steps_before(b), False, False)
                n = batch(B - 1, steps_before(B - 1), False, True)
                weighted_values(B - 1, G - 1, JT - 1)
                for q, (kind, i) in enumerate(FINISH):
                    small(B - 1, kind, i, n + q)

            @block.scalar
            def _(act):
                act.wait_ge(s_var, 1)
                nc.scalar.activation(rstd[:, :], rstd[:, :], ACT.Sqrt).then_inc(s_std, 1)
                act.wait_ge(s_id, 2)
                nc.scalar.copy(ident_h[:, :], ident[:, :]).then_inc(s_id, 1)

                def small(b, kind, i, n):
                    if kind in ("y", "o_turn"):
                        return
                    wait(act, filled, n + 1)
                    if kind == "cT":
                        nc.scalar.copy(cT[:, :, 2 * P * i:2 * P * i + 2 * P].rearrange("c s (j n) -> c j s n", j=2),
                                       pM[0:CS, :].rearrange("c (j s n) -> c j s n", j=2, s=2)
                                       ).then_inc(emptied, 1)
                    elif kind == "xT":
                        nc.scalar.copy(xT[:, :, 2 * P * i:2 * P * i + 2 * P].rearrange("c k (t n) -> c t k n", t=2),
                                       pM[:, :].rearrange("c (t k n) -> c t k n", t=2, k=2)
                                       ).then_inc(emptied, 1)
                    elif kind == "k":
                        wait(act, stored[1 + i // 2], 48 * b)
                        nc.scalar.copy(parts[:, slot(b, i // 2), 0, i % 2, :].rearrange("p a n -> p (a n)"),
                                       pM[:, :]).then_inc(head_done, 1)
                    elif kind == "q":
                        wait(act, stored[0], 48 * (b + 1))
                        act.wait_ge(s_aug, 3)
                        nc.scalar.activation(parts[:, slot(b, 2), 0, i, :].rearrange("p a n -> p (a n)"), pM[:, :],
                                             ACT.Copy, scale=q_scale[:, bass.ds(b, 1)]).then_inc(head_done, 1)
                    elif kind == "v":
                        if i == 0:
                            wait(act, placed, G * b)
                        nc.scalar.copy(v_new[:, :, 2 * i:2 * i + 2, :].rearrange("p g j c -> p j g c"),
                                       pM[:, :].rearrange("p (j g c) -> p j g c", j=2, g=G)
                                       ).then_inc(emptied, 1)
                    elif kind == "oT":
                        nc.scalar.copy(oT[:, i, :], pM[:, :]).then_inc(emptied, 1)
                    elif kind == "m_turn":
                        bb, g = (b + 1, 0) if i == G else (b, i)
                        act.wait_ge(s_id, 3)
                        for q in range(G):
                            ins = nc.scalar.copy(
                                qs[AUG:KR, bass.ds(bb % 2, 1), G * g + q, :].rearrange("r a n -> r (a n)"),
                                pM[XV * q:XV * q + 4, 0:TB * 64].bitcast(BF16))
                        ins.then_inc(emptied, 1)

                def exponentials(b, hg, j):
                    n = JT * (G * b + hg) + j
                    wait(act, av_done, n - 1)
                    if j == 0:
                        wait(act, placed, G * b + hg + 1)
                    for i in range(G):
                        wait(act, s2_done, G * n + i + 1)
                        nc.scalar.activation(pt[:, j % 2, i, :], pS2[:, i % 2, :], ACT.Exp,
                                             bias=bias[:, hg, j:j + 1]).then_inc(exp_done, 1)

                def values_copy(n):
                    wait(act, av_done, JT * n)
                    nc.scalar.copy(ot[:, :], pO[:, :]).then_inc(ot_ready, 1)

                for n, (kind, i) in enumerate(PREPARE):
                    small(0, kind, i, n)
                small(0, "m_turn", 0, START - 1)

                def batch(b, start, first, last):
                    n = 0
                    for hg in range(G):
                        for j in range(JT):
                            exponentials(b, hg, j)
                            if j == 0 and (hg or not first):
                                values_copy(G * b + hg)
                            for kind, i in small_steps(hg, j, first, last):
                                small(batch_of(b, kind, i, hg), kind, i, start + n)
                                n += 1
                    return start + n

                batch(0, START, True, False)
                with act.Fori(1, B - 1) as b:
                    batch(b, steps_before(b), False, False)
                n = batch(B - 1, steps_before(B - 1), False, True)
                values_copy(NG)
                for q, (kind, i) in enumerate(FINISH):
                    small(B - 1, kind, i, n + q)

            @block.vector
            def _(dve):
                own = Chain(dve, s_dve)
                for t in range(T):
                    own.did(nc.vector.bn_stats(stats[:, t, :], xr[:, t, :]))
                own.wait()
                for t in range(T):
                    own.did(nc.vector.bn_aggr(mv[:, t, :], stats[:, t, :]))
                own.wait()
                nc.vector.tensor_scalar(rstd[:, :], mv[:, :, 1], LN_EPS, None, ALU.add).then_inc(s_var, 1)
                dve.wait_ge(s_mask, 32)
                own.did(nc.vector.tensor_reduce(any_on[:, :], m_row, AX_X, ALU.max))
                own.wait()
                own.did(nc.vector.tensor_scalar(big[:, :], any_on[:, :], MASKED, None, ALU.mult))
                own.did(nc.vector.tensor_scalar(q_scale[:, :], any_on[:, :], XD ** -0.5, None, ALU.mult))
                dve.wait_ge(s_row, 3)
                own.did(nc.vector.tensor_scalar(other_rows[:, :], last_row[:, :], -1.0, 1.0, ALU.mult, ALU.add))
                own.wait()
                for b in range(B):
                    own.did(nc.vector.tensor_scalar(aug_f[AUG:KR, b], m_row[AUG:KR, b], -1.0,
                                                    big[AUG:KR, b:b + 1], ALU.add, ALU.mult))
                own.wait()
                nc.vector.tensor_scalar(q_aug[:, :], q_aug[:, :], last_row[:, :], None, ALU.add).then_inc(s_aug, 1)
                for b in range(0, B, 2):
                    nc.vector.tensor_scalar(k_aug[AUG:KR, b:b + 2], aug_f[AUG:KR, b:b + 2], last_row[AUG:KR, :],
                                            other_rows[AUG:KR, :], ALU.mult, ALU.add).then_inc(s_aug, 1)
                dve.wait_ge(s_std, 1)
                own.did(nc.vector.reciprocal(rstd[:, :], rstd[:, :]))
                own.wait()

                def normalise(b):
                    for t in range(TB):
                        ins = nc.vector.tensor_scalar(
                            xn[:, t, :], xr[:, bass.ds(TB * b + t, 1), :].rearrange("p a d -> p (a d)"),
                            mv[:, bass.ds(TB * b + t, 1), 0], rstd[:, bass.ds(TB * b + t, 1)],
                            ALU.subtract, ALU.mult)
                    ins.then_inc(xn_ready, 1)

                def maximum(b, hg, u):
                    U = 16 * (G * b + hg) + u
                    wait(dve, s1_done, U + 1)
                    nc.vector.tensor_reduce(neg_max[:, hg % 2, u // G, u % G:u % G + 1], pS1[:, u % 2, :],
                                            AX_X, ALU.max, negate=True).then_inc(max_done, 1)

                def place(b, hg):
                    wait(dve, av_done, JT * (G * (b - 1) + hg + 1))
                    nc.vector.tensor_copy(v1[:, hg, :, :, 0:XD],
                                          v_new[:, hg].rearrange("p j (i d) -> p j i d", i=G))
                    nc.vector.tensor_scalar(bias[:, hg, :], m_col[:, bass.ds(b, 1), :].rearrange("p a j -> p (a j)"),
                                            -1.0, big[:, bass.ds(b, 1)], ALU.add, ALU.mult).then_inc(placed, 1)

                def split_max(b, hg, own, steps):
                    wait(dve, max_done, 16 * (G * b + hg + 1))
                    wait(dve, filled, steps)
                    nm = neg_max[:, hg % 2]
                    own.did(nc.vector.tensor_copy(max_parts[:, :, :, 0], nm))
                    own.wait()
                    own.did(nc.vector.tensor_tensor(max_rest[:, :, :], nm, max_parts[:, :, :, 0], ALU.subtract))
                    own.wait()
                    own.did(nc.vector.tensor_copy(max_parts[:, :, :, 1], max_rest[:, :, :]))
                    own.wait()
                    nc.vector.tensor_tensor(max_parts[:, :, :, 2], max_rest[:, :, :], max_parts[:, :, :, 1],
                                            ALU.subtract).then_inc(m_ready, 1)

                def small(b, kind, i, n, own):
                    if kind in ("k", "q"):
                        s, m = (slot(b, i // 2), i % 2) if kind == "k" else (slot(b, 2), i)
                        part = [parts[:, s, c, m, :].rearrange("p a n -> p (a n)") for c in range(3)]
                        nth = 6 * b + (i if kind == "k" else 4 + i)
                        wait(dve, head_done, nth + 1)
                        wait(dve, split_done, nth)
                        if kind == "k":
                            nc.vector.tensor_tensor(rest[:, :], pM[:, :], part[0], ALU.subtract
                                                    ).then_inc(emptied, 1)
                        else:
                            nc.vector.scalar_tensor_tensor(rest[:, :], pM[:, :], q_scale[:, bass.ds(b, 1)],
                                                           part[0], ALU.mult, ALU.subtract).then_inc(emptied, 1)
                        wait(dve, emptied, n + 1)
                        own.did(nc.vector.tensor_copy(part[1], rest[:, :]))
                        own.wait()
                        nc.vector.tensor_tensor(part[2], rest[:, :], part[1], ALU.subtract).then_inc(split_done, 1)
                    elif kind == "o_turn":
                        wait(dve, filled, n + 1)
                        turned = pM[:, :].rearrange("p (t h v) -> p t h v", t=TB, h=G)
                        own.did(nc.vector.reciprocal(rz[:, :, :], turned[:, :, :, XD]))
                        own.wait()
                        nc.vector.tensor_tensor(
                            o[:, :, G * XD * i:G * XD * i + G * XD].rearrange("p t (h d) -> p t h d", h=G),
                            turned[:, :, :, 0:XD], rz[:, :, :].unsqueeze(3).broadcast_to([P, TB, G, XD]),
                            ALU.mult).then_inc(emptied, 1)
                    elif kind == "y":
                        wait(dve, filled, n + 1)
                        xt = xr[:, bass.ds(TB * b + 2 * i, 2), :]
                        nc.vector.tensor_tensor(xt, xt, pM[:, :].rearrange("p (t d) -> p t d", t=2),
                                                ALU.add).then_inc(emptied, 1)

                normalise(0)
                dve.wait_ge(s_z, 1)
                for n, (kind, i) in enumerate(PREPARE):
                    small(0, kind, i, n, own)
                wait(dve, emptied, len(PREPARE))
                dve.wait_ge(s_z, 3)
                for hg in range(G):
                    place(0, hg)
                for u in range(16):
                    maximum(0, 0, u)
                split_max(0, 0, own, 0)
                for u in range(4):
                    maximum(0, 1, u)
                before = own.n

                def batch(b, start, first, last, own):
                    n = 0
                    for hg in range(G):
                        for j in range(JT):
                            if j == 6 and (hg < G - 1 or not last):
                                if hg < G - 1:
                                    split_max(b, hg + 1, own, start + n)
                                else:
                                    split_max(b + 1, 0, own, start + n)
                            for ahead, g, u in score_units(hg, j, last):
                                maximum(b + ahead, g, u)
                            for kind, i in small_steps(hg, j, first, last):
                                small(batch_of(b, kind, i, hg), kind, i, start + n, own)
                                n += 1
                            if (hg, j) == (0, 7) and not last:
                                normalise(b + 1)
                            if (hg, j) == (0, 2) and not first:
                                place(b, G - 1)
                            if (hg, j) == (2, 5) and not last:
                                wait(dve, emptied, start + n)
                                place(b + 1, 0)
                                place(b + 1, 1)
                            if (hg, j) == (3, 2) and not last:
                                place(b + 1, 2)
                    return start + n

                def owned(b):
                    return Chain(dve, s_dve, before + OWN_FIRST + OWN_MIDDLE * (b - 1))

                own = Chain(dve, s_dve, before)
                batch(0, START, True, False, own)
                assert own.n == OWN_FIRST, own.n
                with dve.Fori(1, B - 1) as b:
                    own = owned(b)
                    batch(b, steps_before(b), False, False, own)
                    assert own.n == OWN_MIDDLE, own.n
                own = owned(B - 1)
                n = batch(B - 1, steps_before(B - 1), False, True, own)
                for q, (kind, i) in enumerate(FINISH):
                    small(B - 1, kind, i, n + q, own)


E_, FH = 8, 512
TE = T * E_
KH = FH // P
R = B * L + P
SLOTS = 2 * T + E_


def experts(nc, gate_w, w1, b1, ln1_g, ln1_b, w2, b2, ln_g, ln_b, x_rows, y_rows, xr, out):
    with ExitStack() as ctx:
        def sb(name, shape, dt=F32):
            return ctx.enter_context(nc.sbuf_tensor("c_" + name, shape, dt))

        def ps(name, shape, dt=F32):
            return ctx.enter_context(nc.psum_tensor("c_" + name, shape, dt))

        def sem(name):
            return ctx.enter_context(nc.semaphore("c_" + name))

        ident = sb("ident", [P, P])
        earlier = sb("earlier", [P, P])
        ones = sb("ones", [P, P])
        half = sb("half", [P, 1])
        w1_sb = sb("w1", [P, E_, KD, FH])
        w2_sb = sb("w2", [P, E_, KH, D])
        b1_sb = sb("b1", [P, E_, FH])
        b2_sb = sb("b2", [P, E_, D])
        gb = sb("gb", [P, 2, E_, KH])
        lng = sb("lng", [P, D])
        lnb = sb("lnb", [P, D])
        gate = sb("gate", [P, KD, 32])
        f = sb("f", [P, T, D])
        stats = sb("stats", [P, T, 6])
        mv = sb("mv", [P, T, 2])
        rstd = sb("rstd", [P, T])
        fT = sb("fT", [P, KD, B * L])
        lgT = sb("lgT", [P, 512])
        g1 = sb("g1", [P, T, E_])
        g2 = sb("g2", [P, T, E_])
        eq = sb("eq", [P, T, E_])
        sel = sb("sel", [P, 2, T, E_])
        both = sb("both", [P, T, E_])
        rank = sb("rank", [P, T, E_])
        tot = sb("tot", [P, 2, T, E_])
        order = sb("order", [P, E_])
        order_i = sb("order_i", [P, E_], I32)
        base = sb("base", [P, E_])
        base_i = sb("base_i", [P, E_], I32)
        slot_i = sb("slot_i", [P, SLOTS], I32)
        lane_i = sb("lane_i", [P, 1], I32)
        lane = sb("lane", [P, 1])
        slot = sb("slot", [P, SLOTS])
        top = sb("top", [P, 2, T])
        tmp = sb("tmp", [P, T])
        pos = sb("pos", [P, 2, T])
        pos_i = sb("pos_i", [P, 2, T], I32)
        n_e = sb("n_e", [P, E_])
        pad_i = sb("pad_i", [P, E_], I32)
        tiles_i = sb("tiles_i", [P, E_], I32)
        ends = sb("ends", [P, 2, E_])
        over = sb("over", [P, SLOTS, E_])
        s_exp = sb("s_exp", [P, SLOTS])
        s_row = sb("s_row", [P, SLOTS])
        s_tab = sb("s_tab", [P, 2, SLOTS], I32)
        y_base = sb("y_base", [P, E_])
        y_pos = sb("y_pos", [P, 2, T], I32)
        zrow = sb("zrow", [P, D])
        xs = sb("xs", [P, 4, D])
        xsT = sb("xsT", [P, 2, KD, P])
        h = sb("h", [P, 2, FH])
        hst = sb("hst", [P, 2, 6])
        hmv = sb("hmv", [P, 2, 2])
        hrs = sb("hrs", [P, 2, 1])
        hT = sb("hT", [P, 2, KH, P])
        gbn = sb("gbn", [P, 2, 2, KH])
        ys = sb("ys", [P, 2, D])
        y = sb("y", [P, 4, 2, D])
        acc = sb("acc", [P, T, D])

        pX = [ps("pX0", [P, 512]), ps("pX1", [P, 512])]
        pH = [ps("pH0", [P, 512]), ps("pH1", [P, 512])]
        pT = [ps("pT0", [P, 512]), ps("pT1", [P, 512])]
        pY = [ps("pY0", [P, 512]), ps("pY1", [P, 512])]

        s_gate, s_w1, s_w2, s_par, s_ln = sem("gate"), sem("w1"), sem("w2"), sem("par"), sem("ln")
        s_id, s_k, s_gz, s_dve = sem("ident"), sem("consts"), sem("gate0"), sem("dve")
        s_var, s_rstd, f_ready = sem("var"), sem("rstd"), sem("f")
        t_done, t_copied, lg_done, lg_copied = sem("t_done"), sem("t_copied"), sem("lg"), sem("lg_copied")
        lt_done, g_ready, g_exp, both_ready, rank_done = sem("lt"), sem("g"), sem("gexp"), sem("both"), sem("rank")
        pad_ready, pos_ready, sent, padded, tab_ready = sem("pad"), sem("pos"), sem("sent"), sem("padded"), sem("tab")
        def two(name):
            return [sem(name + "0"), sem(name + "1")]

        xs_in, xs_t, xsT_ready = [sem(f"xs_in{j}") for j in range(4)], two("xs_t"), two("xsT")
        h_done, h_read, h_var, h_rstd, h_norm = two("h"), two("h_read"), two("h_var"), two("h_rstd"), two("h_norm")
        h_t, hT_ready, gb_now = two("h_t"), two("hT"), two("gb_now")
        y_done, y_ready, y_out = two("y"), two("ys"), two("y_out")
        y_in = [sem(f"y_in{i}") for i in range(4)]
        a_done, a_stats, a_std, o_ready, o_out = sem("a"), sem("a_st"), sem("a_std"), sem("o"), sem("o_out")

        OWN_TILE = 2
        ROUNDS = SLOTS // 4

        def at(i, j):
            return i + j // 4, j % 4

        def nth(i, j):
            return 2 * i + j // 2

        def slot_steps(engine, step):
            for j in range(4):
                step(0, j)
            with engine.Fori(1, ROUNDS - 1) as i:
                for j in range(4):
                    step(i, j)
            for j in range(4):
                step(ROUNDS - 1, j)

        def exists(i, j):
            return not isinstance(i, int) or 0 <= 4 * i + j < SLOTS

        with nc.Block() as block:

            @block.sync
            def _(sp):
                sp.wait_ge(s_gz, 1)
                sp.dma_start(gate[:, :, 0:E_], gate_w.rearrange("(k p) e -> p k e", p=P)).then_inc(s_gate, 16)
                for k in range(KD):
                    sp.dma_start(w1_sb[:, :, k, :], w1[:, P * k:P * k + P, :].rearrange("e p h -> p e h")
                                 ).then_inc(s_w1, 16)
                sp.dma_start(b1_sb[:, :, :].rearrange("p e h -> p (e h)"),
                             b1.rearrange("e h -> (e h)").unsqueeze(0).broadcast_to([P, E_ * FH])).then_inc(s_par, 16)
                with nc.allow_non_contiguous_dma(reason="two vectors of each expert, by hidden unit"):
                    for i, v in enumerate((ln1_g, ln1_b)):
                        sp.dma_start(gb[:, i], v.rearrange("e (c p) -> p e c", p=P)).then_inc(s_par, 16)
                for k in range(KH):
                    sp.dma_start(w2_sb[:, :, k, :], w2[:, P * k:P * k + P, :].rearrange("e p d -> p e d")
                                 ).then_inc(s_w2, 16)
                sp.dma_start(b2_sb[:, :, :].rearrange("p e h -> p (e h)"),
                             b2.rearrange("e h -> (e h)").unsqueeze(0).broadcast_to([P, E_ * D])).then_inc(s_par, 16)
                for t, v in ((lng, ln_g), (lnb, ln_b)):
                    sp.dma_start(t[:, :], v.unsqueeze(0).broadcast_to([P, D])).then_inc(s_ln, 16)

                sp.wait_ge(tab_ready, 1)
                sp.wait_ge(sent, 16 * 2 * T)
                sp.wait_ge(padded, 16 * E_)

                def fetch(i, j):
                    if not isinstance(i, int):
                        wait(sp, xs_t[j % 2], nth(i - 1, j) + 1)
                    row = sp.value_load(s_tab[0:1, 1, bass.ds(4 * i + j, 1)], min_val=0, max_val=E_ * R - P)
                    sp.dma_start(xs[:, j, :], x_rows[bass.ds(row, P), :]).then_inc(xs_in[j], 16)

                for j in range(4):
                    fetch(0, j)
                with sp.Fori(1, ROUNDS) as i:
                    for j in range(4):
                        fetch(i, j)

                for t in range(T):
                    wait(sp, o_ready, t + 1)
                    sp.dma_start(out[t // TB, P * (t % TB):P * (t % TB) + P, :], acc[:, t, :]).then_inc(o_out, 16)
                sp.wait_ge(o_out, 16 * T)

            @block.gpsimd
            def _(pool):
                pool.memset(gate[:, :, :], 0.0).then_inc(s_gz, 1)
                pool.memset(half[:, :], -0.5).then_inc(s_k, 1)
                pool.wait_ge(s_k, 1)
                pool.wait_ge(s_var, 1)
                nc.gpsimd.tensor_tensor(rstd[:, :], rstd[:, :], half[:, :].broadcast_to([P, T]), ALU.pow
                                        ).then_inc(s_rstd, 1)
                make_identity(pool, ident[:, :], s_id)
                pool.memset(ones[:, :], 1.0).then_inc(s_k, 1)
                pool.memset(earlier[:, :], 1.0).then_inc(s_k, 1)
                pool.wait_ge(s_k, 3)
                pool.affine_select(out=earlier[:, :], in_=earlier[:, :], compare_op=ALU.is_gt, fill=0.0,
                                   base=0, pattern=[[1, P]], channel_multiplier=-1).then_inc(s_k, 1)
                pool.iota(order_i[:, :], pattern=[[-1, E_]], base=E_, channel_multiplier=0).then_inc(s_k, 1)
                pool.iota(base_i[:, :], pattern=[[R, E_]], base=0, channel_multiplier=0).then_inc(s_k, 1)
                pool.iota(slot_i[:, :], pattern=[[1, SLOTS]], base=0, channel_multiplier=0).then_inc(s_k, 1)
                pool.iota(lane_i[:, :], pattern=[[0, 1]], base=0, channel_multiplier=1).then_inc(s_k, 1)
                pool.memset(zrow[:, :], 0.0).then_inc(s_k, 1)
                pool.wait_ge(s_k, 9)

                pool.wait_ge(pos_ready, 1)
                for k in range(2):
                    for t in range(T):
                        pool.indirect_dma_start(
                            out=x_rows, out_offset=bass.IndirectOffsetOnAxis(
                                ap=pos_i[:, k, t:t + 1].bitcast(U32), axis=0),
                            in_=f[:, t, :], in_offset=None).then_inc(sent, 16)
                for e in range(E_):
                    pool.indirect_dma_start(
                        out=x_rows, out_offset=bass.IndirectOffsetOnAxis(
                            ap=pad_i[:, e:e + 1].bitcast(U32), axis=0),
                        in_=zrow[:, :], in_offset=None).then_inc(padded, 16)

                def power(i, j):
                    par = j % 2
                    wait(pool, h_var[par], nth(i, j) + 1)
                    nc.gpsimd.tensor_tensor(hrs[:, par, :], hrs[:, par, :], half[:, :], ALU.pow).then_inc(h_rstd[par], 1)

                slot_steps(pool, power)

                for par in range(2):
                    pool.wait_ge(y_out[par], 16 * (SLOTS // 2))
                for t in range(T):
                    if t >= 4:
                        pool.wait_ge(a_done, t - 3)
                    for k in range(2):
                        pool.indirect_dma_start(
                            out=y[:, t % 4, k, :], out_offset=None, in_=y_rows,
                            in_offset=bass.IndirectOffsetOnAxis(ap=y_pos[:, k, t:t + 1].bitcast(U32), axis=0)
                        ).then_inc(y_in[t % 4], 16)

            @block.tensor
            def _(pe):
                pe.wait_ge(s_id, 2)
                for n in range(2 * T // 4):
                    wait(pe, f_ready, 2 * n + 2)
                    if n >= 2:
                        wait(pe, t_copied, n - 1)
                    for q in range(4):
                        t, k = 2 * n + q // 2, q % 2
                        ins = pe.transpose(pX[n % 2][:, P * q:P * q + P], f[:, t, P * k:P * k + P], ident[:, :])
                    ins.then_inc(t_done, 1)
                pe.wait_ge(s_gate, 16)
                pe.wait_ge(t_copied, T // 2)
                for k in range(KD):
                    for q in range(B):
                        ins = pe.matmul(pH[0][32 * q:32 * q + 32, :], gate[:, k, :], fT[:, k, L * q:L * q + L],
                                        start=(k == 0), stop=(k == KD - 1))
                ins.then_inc(lg_done, 1)
                pe.wait_ge(lg_copied, 1)
                for c in range(TB):
                    ins = pe.transpose(pH[1][:, P * c:P * c + P], lgT[:, P * c:P * c + P], ident[:, :])
                ins.then_inc(lt_done, 1)
                pe.wait_ge(both_ready, 1)
                pe.wait_ge(s_k, 4)
                sel_2d = both[:, :, :].rearrange("p t e -> p (t e)")
                pe.matmul(pT[0][:, 0:TE], earlier[:, :], sel_2d, start=True, stop=True).then_inc(rank_done, 1)
                pe.matmul(pT[1][:, 0:TE], ones[:, :], sel_2d, start=True, stop=True).then_inc(rank_done, 1)

                pe.wait_ge(tab_ready, 1)
                pe.wait_ge(s_w1, 16 * KD)
                pe.wait_ge(s_w2, 16 * KH)

                def x_transposes(i, j):
                    par = j % 2
                    wait(pe, xs_in[j], 16 * (i + 1))
                    wait(pe, xsT_ready[par], nth(i, j))
                    for k in range(KD):
                        ins = pe.transpose(pX[par][:, P * k:P * k + P], xs[:, j, P * k:P * k + P], ident[:, :])
                    ins.then_inc(xs_t[par], 1)

                def up(i, j):
                    par = j % 2
                    e = pe.value_load(s_tab[0:1, 0, bass.ds(4 * i + j, 1)], min_val=0, max_val=E_ - 1)
                    wait(pe, xsT_ready[par], nth(i, j) + 1)
                    wait(pe, h_read[par], nth(i, j))
                    for k in range(KD):
                        ins = pe.matmul(pH[par][:, :], xsT[:, par, k, :],
                                        w1_sb[:, bass.ds(e, 1), k, :].rearrange("p a h -> p (a h)"),
                                        start=(k == 0), stop=(k == KD - 1))
                    ins.then_inc(h_done[par], 1)

                def h_transposes(i, j):
                    par = j % 2
                    wait(pe, h_norm[par], nth(i, j) + 1)
                    wait(pe, hT_ready[par], nth(i, j))
                    for k in range(KH):
                        ins = pe.transpose(pT[par][:, P * k:P * k + P], h[:, par, P * k:P * k + P], ident[:, :])
                    ins.then_inc(h_t[par], 1)

                def down(i, j):
                    par = j % 2
                    e = pe.value_load(s_tab[0:1, 0, bass.ds(4 * i + j, 1)], min_val=0, max_val=E_ - 1)
                    wait(pe, hT_ready[par], nth(i, j) + 1)
                    wait(pe, y_ready[par], nth(i, j))
                    for k in range(KH):
                        ins = pe.matmul(pY[par][:, 0:D], hT[:, par, k, :],
                                        w2_sb[:, bass.ds(e, 1), k, :].rearrange("p a d -> p (a d)"),
                                        start=(k == 0), stop=(k == KH - 1))
                    ins.then_inc(y_done[par], 1)

                x_transposes(0, 0)
                x_transposes(0, 1)
                up(0, 0)

                def step(i, j):
                    if exists(i, j + 1):
                        up(*at(i, j + 1))
                    h_transposes(i, j)
                    if exists(i, j + 2):
                        x_transposes(*at(i, j + 2))
                    if exists(i, j - 1):
                        down(*at(i, j - 1))

                slot_steps(pe, step)
                down(ROUNDS - 1, 3)

            @block.scalar
            def _(act):
                for n in range(T // 2):
                    wait(act, t_done, n + 1)
                    nc.scalar.copy(fT[:, :, 2 * P * n:2 * P * n + 2 * P].rearrange("p k (t n) -> p t k n", t=2),
                                   pX[n % 2][:, :].rearrange("p (t k n) -> p t k n", t=2, k=2)
                                   ).then_inc(t_copied, 1)
                act.wait_ge(lg_done, 1)
                nc.scalar.copy(lgT[:, :], pH[0][:, :]).then_inc(lg_copied, 1)
                act.wait_ge(g_ready, 1)
                nc.scalar.activation(g1[:, :, :], g1[:, :, :], ACT.Exp).then_inc(g_exp, 1)
                act.wait_ge(s_par, 64)

                def x_copy(i, j):
                    par = j % 2
                    wait(act, xs_t[par], nth(i, j) + 1)
                    wait(act, h_done[par], nth(i, j))
                    nc.scalar.copy(xsT[:, par], pX[par][:, 0:D].rearrange("p (k n) -> p k n", k=KD)
                                   ).then_inc(xsT_ready[par], 1)

                def gelu(i, j):
                    par = j % 2
                    wait(act, gb_now[par], nth(i, j) + 1)
                    wait(act, y_done[par], nth(i, j))
                    wait(act, h_t[par], nth(i, j) + 1)
                    for k in range(KH):
                        ins = nc.scalar.activation(hT[:, par, k, :], pT[par][:, P * k:P * k + P], ACT.Gelu,
                                                   bias=gbn[:, par, 1, k:k + 1], scale=gbn[:, par, 0, k:k + 1])
                    ins.then_inc(hT_ready[par], 1)

                def store(i, j):
                    par = j % 2
                    wait(act, y_ready[par], nth(i, j) + 1)
                    act.dma_start(y_rows[bass.ds(P * (4 * i + j), P), :], ys[:, par, :]).then_inc(y_out[par], 16)

                x_copy(0, 0)
                x_copy(0, 1)

                def step(i, j):
                    if exists(i, j + 2):
                        x_copy(*at(i, j + 2))
                    gelu(i, j)
                    if exists(i, j - 1):
                        store(*at(i, j - 1))

                slot_steps(act, step)
                store(ROUNDS - 1, 3)

                for t in range(T):
                    act.wait_ge(a_stats, t + 1)
                    nc.scalar.activation(rstd[:, t:t + 1], rstd[:, t:t + 1], ACT.Sqrt).then_inc(a_std, 1)

            @block.vector
            def _(dve):
                own = Chain(dve, s_dve)

                def did(ins):
                    own.did(ins)
                    own.wait()

                for t in range(T):
                    own.did(nc.vector.bn_stats(stats[:, t, :], xr[:, t, :]))
                own.wait()
                for t in range(T):
                    own.did(nc.vector.bn_aggr(mv[:, t, :], stats[:, t, :]))
                own.wait()
                nc.vector.tensor_scalar(rstd[:, :], mv[:, :, 1], LN_EPS, None, ALU.add).then_inc(s_var, 1)
                dve.wait_ge(s_rstd, 1)
                for t in range(T):
                    nc.vector.tensor_scalar(f[:, t, :], xr[:, t, :], mv[:, t, 0:1], rstd[:, t:t + 1],
                                            ALU.subtract, ALU.mult).then_inc(f_ready, 1)
                dve.wait_ge(s_k, 9)
                own.did(nc.vector.tensor_copy(order[:, :], order_i[:, :]))
                own.did(nc.vector.tensor_copy(base[:, :], base_i[:, :]))
                own.did(nc.vector.tensor_copy(slot[:, :], slot_i[:, :]))
                own.did(nc.vector.tensor_copy(lane[:, :], lane_i[:, :]))

                dve.wait_ge(lt_done, 1)
                did(nc.vector.tensor_copy(
                    g1[:, :, :].rearrange("p (q c) e -> p c q e", q=B),
                    pH[1][:, :].rearrange("p (c q e) -> p c q e", c=TB, q=B)[:, :, :, 0:E_]))
                did(nc.vector.tensor_reduce(tmp[:, :], g1[:, :, :], AX_X, ALU.max))
                nc.vector.tensor_tensor(g1[:, :, :], g1[:, :, :], tmp[:, :].unsqueeze(2).broadcast_to([P, T, E_]),
                                        ALU.subtract).then_inc(g_ready, 1)
                dve.wait_ge(g_exp, 1)
                g = g1
                for c in range(2):
                    did(nc.vector.tensor_reduce(top[:, c, :], g[:, :, :], AX_X, ALU.max))
                    did(nc.vector.tensor_tensor(eq[:, :, :], g[:, :, :],
                                                top[:, c, :].unsqueeze(2).broadcast_to([P, T, E_]), ALU.is_equal))
                    did(nc.vector.tensor_tensor(eq[:, :, :], eq[:, :, :],
                                                order[:, :].unsqueeze(1).broadcast_to([P, T, E_]), ALU.mult))
                    did(nc.vector.tensor_reduce(tmp[:, :], eq[:, :, :], AX_X, ALU.max))
                    did(nc.vector.tensor_tensor(sel[:, c], eq[:, :, :],
                                                tmp[:, :].unsqueeze(2).broadcast_to([P, T, E_]), ALU.is_equal))
                    if c == 0:
                        did(nc.vector.scalar_tensor_tensor(
                            g2[:, :, :].rearrange("p t e -> p (t e)"), sel[:, 0].rearrange("p t e -> p (t e)"),
                            -2.0, g1[:, :, :].rearrange("p t e -> p (t e)"), ALU.mult, ALU.add))
                        g = g2
                nc.vector.tensor_tensor(both[:, :, :], sel[:, 0], sel[:, 1], ALU.add).then_inc(both_ready, 1)
                did(nc.vector.tensor_tensor(tmp[:, :], top[:, 0, :], top[:, 1, :], ALU.add))
                did(nc.vector.reciprocal(tmp[:, :], tmp[:, :]))
                own.did(nc.vector.tensor_tensor(top[:, :, :], top[:, :, :],
                                                tmp[:, :].unsqueeze(1).broadcast_to([P, 2, T]), ALU.mult))
                dve.wait_ge(rank_done, 2)
                did(nc.vector.tensor_copy(tot[:, 0].rearrange("p t e -> p (t e)"), pT[1][:, 0:TE]))
                cur = 0
                for step in (1, 2, 4, 8):
                    nc.vector.tensor_copy(tot[:, 1 - cur, 0:step, :], tot[:, cur, 0:step, :])
                    did(nc.vector.tensor_tensor(tot[:, 1 - cur, step:T, :], tot[:, cur, step:T, :],
                                                tot[:, cur, 0:T - step, :], ALU.add))
                    cur = 1 - cur
                own.did(nc.vector.tensor_copy(n_e[:, :], tot[:, cur, T - 1, :]))
                did(nc.vector.tensor_tensor(rank[:, 0, :], pT[0][:, 0:E_], base[:, :], ALU.add))
                did(nc.vector.tensor_tensor(rank[:, 1:T, :].rearrange("p t e -> p (t e)"), pT[0][:, E_:TE],
                                            tot[:, cur, 0:T - 1, :].rearrange("p t e -> p (t e)"), ALU.add))
                did(nc.vector.tensor_tensor(rank[:, 1:T, :], rank[:, 1:T, :],
                                            base[:, :].unsqueeze(1).broadcast_to([P, T - 1, E_]), ALU.add))
                for c in range(2):
                    did(nc.vector.tensor_tensor(eq[:, :, :], sel[:, c], rank[:, :, :], ALU.mult))
                    did(nc.vector.tensor_reduce(pos[:, c, :], eq[:, :, :], AX_X, ALU.add))
                own.did(nc.vector.tensor_tensor(eq[:, 0, :], n_e[:, :], base[:, :], ALU.add))
                own.wait()
                own.did(nc.vector.tensor_scalar(pad_i[:, :], eq[:, 0, :], lane[:, :], None, ALU.add))
                own.wait()
                nc.vector.tensor_copy(pos_i[:, :, :], pos[:, :, :]).then_inc(pos_ready, 1)
                did(nc.vector.tensor_scalar(tiles_i[:, :], n_e[:, :], float(P - 1), None, ALU.add))
                did(nc.vector.tensor_scalar(tiles_i[:, :], tiles_i[:, :], 7, None, ALU.logical_shift_right))
                did(nc.vector.tensor_copy(ends[:, 0, :], tiles_i[:, :]))
                cur = 0
                for step in (1, 2, 4):
                    nc.vector.tensor_copy(ends[:, 1 - cur, 0:step], ends[:, cur, 0:step])
                    did(nc.vector.tensor_tensor(ends[:, 1 - cur, step:E_], ends[:, cur, step:E_],
                                                ends[:, cur, 0:E_ - step], ALU.add))
                    cur = 1 - cur
                end = ends[:, cur, :]
                did(nc.vector.tensor_scalar(tmp[:, 0:1], end[:, E_ - 1:E_], -1.0, None, ALU.add))
                did(nc.vector.tensor_scalar(slot[:, :], slot[:, :], tmp[:, 0:1], None, ALU.min))
                did(nc.vector.tensor_tensor(over[:, :, :], slot[:, :].unsqueeze(2).broadcast_to([P, SLOTS, E_]),
                                            end.unsqueeze(1).broadcast_to([P, SLOTS, E_]), ALU.is_ge))
                did(nc.vector.tensor_reduce(s_exp[:, :], over[:, :, :], AX_X, ALU.add))
                own.did(nc.vector.tensor_scalar(n_e[:, :], tiles_i[:, :], 1.0, None, ALU.mult))
                own.wait()
                did(nc.vector.tensor_tensor(over[:, :, :], over[:, :, :],
                                            n_e[:, :].unsqueeze(1).broadcast_to([P, SLOTS, E_]), ALU.mult))
                did(nc.vector.tensor_reduce(s_row[:, :], over[:, :, :], AX_X, ALU.add))
                did(nc.vector.tensor_tensor(s_row[:, :], slot[:, :], s_row[:, :], ALU.subtract))
                did(nc.vector.tensor_scalar(s_row[:, :], s_row[:, :], float(P), None, ALU.mult))
                did(nc.vector.scalar_tensor_tensor(s_row[:, :], s_exp[:, :], float(R), s_row[:, :],
                                                   ALU.mult, ALU.add))
                own.did(nc.vector.tensor_tensor(y_base[:, :], end, n_e[:, :], ALU.subtract))
                own.wait()
                did(nc.vector.scalar_tensor_tensor(y_base[:, :], y_base[:, :], float(P), base[:, :],
                                                   ALU.mult, ALU.subtract))
                did(nc.vector.tensor_tensor(rank[:, :, :], rank[:, :, :],
                                            y_base[:, :].unsqueeze(1).broadcast_to([P, T, E_]), ALU.add))
                for c in range(2):
                    did(nc.vector.tensor_tensor(eq[:, :, :], sel[:, c], rank[:, :, :], ALU.mult))
                    did(nc.vector.tensor_reduce(pos[:, c, :], eq[:, :, :], AX_X, ALU.add))
                own.did(nc.vector.tensor_copy(y_pos[:, :, :], pos[:, :, :]))
                own.did(nc.vector.tensor_copy(s_tab[:, 0, :], s_exp[:, :]))
                own.wait()
                nc.vector.tensor_copy(s_tab[:, 1, :], s_row[:, :]).then_inc(tab_ready, 1)
                dve.wait_ge(tab_ready, 1)
                dve.wait_ge(s_par, 64)

                def first(i, j, own):
                    par = j % 2
                    e = dve.value_load(s_tab[0:1, 0, bass.ds(4 * i + j, 1)], min_val=0, max_val=E_ - 1)
                    wait(dve, h_done[par], nth(i, j) + 1)
                    wait(dve, h_t[par], nth(i, j))
                    nc.vector.tensor_tensor(h[:, par, :], pH[par][:, :],
                                            b1_sb[:, bass.ds(e, 1), :].rearrange("p a h -> p (a h)"),
                                            ALU.add).then_inc(h_read[par], 1)
                    wait(dve, h_read[par], nth(i, j) + 1)
                    own.did(nc.vector.bn_stats(hst[:, par, :], h[:, par, :]))
                    wait(dve, hT_ready[par], nth(i, j))
                    own.wait()
                    nc.vector.tensor_scalar(gbn[:, par, :, :], gb[:, :, bass.ds(e, 1), :].rearrange("p g a k -> p g (a k)"),
                                            1.0, None, ALU.mult).then_inc(gb_now[par], 1)
                    own.did(nc.vector.bn_aggr(hmv[:, par, :], hst[:, par, :]))
                    own.wait()
                    nc.vector.tensor_scalar(hrs[:, par, :], hmv[:, par, 1:2], LN_EPS, None, ALU.add
                                            ).then_inc(h_var[par], 1)

                def second(i, j):
                    par = j % 2
                    wait(dve, h_rstd[par], nth(i, j) + 1)
                    nc.vector.tensor_scalar(h[:, par, :], h[:, par, :], hmv[:, par, 0:1], hrs[:, par, :],
                                            ALU.subtract, ALU.mult).then_inc(h_norm[par], 1)

                def third(i, j):
                    par = j % 2
                    e = dve.value_load(s_tab[0:1, 0, bass.ds(4 * i + j, 1)], min_val=0, max_val=E_ - 1)
                    wait(dve, y_done[par], nth(i, j) + 1)
                    wait(dve, y_out[par], 16 * nth(i, j))
                    nc.vector.tensor_tensor(ys[:, par, :], pY[par][:, 0:D],
                                            b2_sb[:, bass.ds(e, 1), :].rearrange("p a d -> p (a d)"),
                                            ALU.add).then_inc(y_ready[par], 1)

                before = own.n
                first(0, 0, own)
                second(0, 0)

                def step(i, j):
                    own = Chain(dve, s_dve, before + OWN_TILE * (4 * i + j + 1))
                    if exists(i, j + 1):
                        first(*at(i, j + 1), own)
                        second(*at(i, j + 1))
                    if exists(i, j - 1):
                        third(*at(i, j - 1))

                slot_steps(dve, step)
                third(ROUNDS - 1, 3)

                dve.wait_ge(s_ln, 32)
                own = Chain(dve, s_dve, before + OWN_TILE * SLOTS)

                def gather(t):
                    wait(dve, y_in[t % 4], 32 * (t // 4 + 1))
                    a = acc[:, t, :]
                    own.did(nc.vector.scalar_tensor_tensor(a, y[:, t % 4, 0, :], top[:, 0, t:t + 1], f[:, t, :],
                                                           ALU.mult, ALU.add))
                    own.wait()
                    nc.vector.scalar_tensor_tensor(a, y[:, t % 4, 1, :], top[:, 1, t:t + 1], a,
                                                   ALU.mult, ALU.add).then_inc(a_done, 1)
                    wait(dve, a_done, t + 1)
                    own.did(nc.vector.bn_stats(stats[:, t, :], a))
                    own.wait()
                    own.did(nc.vector.bn_aggr(mv[:, t, :], stats[:, t, :]))
                    own.wait()
                    nc.vector.tensor_scalar(rstd[:, t:t + 1], mv[:, t, 1:2], LN_EPS, None, ALU.add
                                            ).then_inc(a_stats, 1)

                def finish(t):
                    a = acc[:, t, :]
                    wait(dve, a_std, t + 1)
                    own.did(nc.vector.reciprocal(rstd[:, t:t + 1], rstd[:, t:t + 1]))
                    own.wait()
                    own.did(nc.vector.tensor_scalar(a, a, mv[:, t, 0:1], rstd[:, t:t + 1], ALU.subtract, ALU.mult))
                    own.wait()
                    own.did(nc.vector.tensor_tensor(a, a, lng[:, :], ALU.mult))
                    own.did(nc.vector.tensor_tensor(xr[:, t, :], xr[:, t, :], lnb[:, :], ALU.add))
                    own.wait()
                    nc.vector.tensor_tensor(a, a, xr[:, t, :], ALU.add).then_inc(o_ready, 1)

                for t in range(T):
                    gather(t)
                    if t:
                        finish(t - 1)
                finish(T - 1)


def decoder_layer(nc, x, ctx_in, mask, a_wq, a_wk, a_wv, a_wo, a_kq, a_kk, x_wq, x_wk, x_wv, x_wo,
                  gate_w, w1, b1, ln1_g, ln1_b, w2, b2, ln_g, ln_b, out):
    k_scr = nc.dram_tensor("k_scr", (B, 3, D, M), BF16).ap()
    q_scr = nc.dram_tensor("q_scr", (B, 3, D, L), BF16).ap()
    aug_scr = nc.dram_tensor("aug_scr", (B, 4, M), BF16).ap()
    x_rows = nc.dram_tensor("x_rows", (E_ * R, D), F32).ap()
    y_rows = nc.dram_tensor("y_rows", (SLOTS * P, D), F32).ap()
    with nc.sbuf_tensor("xr", [P, T, D], F32) as xr:
        linear_attention(nc, x, a_wq, a_wk, a_wv, a_wo, a_kq, a_kk, xr)
        cross_attention(nc, ctx_in, mask, x_wq, x_wk, x_wv, x_wo, k_scr, q_scr, aug_scr, xr)
        experts(nc, gate_w, w1, b1, ln1_g, ln1_b, w2, b2, ln_g, ln_b, x_rows, y_rows, xr, out)


_INS = ['x', 'ctx_768', 'mask_BxS2_bf1', 'L0_attn_Wq', 'L0_attn_Wk', 'L0_attn_Wv', 'L0_attn_Wo',
        'L0_attn_Kq', 'L0_attn_Kk', 'L0_xattn_Wq', 'L0_xattn_Wk', 'L0_xattn_Wv', 'L0_xattn_Wo',
        'L0_ffn_gate_w', 'L0_ffn_w1', 'L0_ffn_b1', 'L0_ffn_ln1_g', 'L0_ffn_ln1_b', 'L0_ffn_w2',
        'L0_ffn_b2', 'L0_ffn_ln_g', 'L0_ffn_ln_b']
_OUTS = [((B, L, D), 'float32')]


def kernel(**inputs):
    import numpy as _np
    import concourse.bacc as _bacc
    from concourse import mybir as _mybir
    from concourse.bass_utils import run_bass_kernel_spmd as _run

    nc = _bacc.Bacc("TRN2", target_bir_lowering=False, num_devices=1)
    arrays, args = {}, []
    for name in _INS:
        a = _np.ascontiguousarray(inputs[name])
        if a.dtype.kind == "b":
            a = a.view(_np.uint8)
        arrays[f"in_{name}_dram"] = a
        args.append(nc.dram_tensor(f"in_{name}_dram", a.shape, _mybir.dt.from_np(a.dtype), kind="ExternalInput").ap())
    for i, (shape, dtype) in enumerate(_OUTS):
        dt = _mybir.dt.from_np(_np.dtype(dtype))
        args.append(nc.dram_tensor(f"out_{i}_dram", shape, dt, kind="ExternalOutput").ap())
    decoder_layer(nc, *args)
    r = _run(nc, [arrays], core_ids=[0])
    got = tuple(r.results[0][f"out_{i}_dram"] for i in range(len(_OUTS)))
    return got[0]
```

```python
from contextlib import ExitStack

import concourse.bass as bass
from concourse import mybir

P = 128
F32 = mybir.dt.float32
BF16 = mybir.dt.bfloat16
I32 = mybir.dt.int32
U32 = mybir.dt.uint32
U8 = mybir.dt.uint8
ALU = mybir.AluOpType
ACT = mybir.ActivationFunctionType
AX_X = mybir.AxisListType.X

B, L, D = 4, 512, 256
T = B * L // P
TB = L // P
KD = D // P
H, HD = 16, 64
F2 = 2 * HD
VW = 96
G = 4
LN_EPS = 1e-5
FEAT_EPS = 1e-12


def wait(eng, sem, value):
    if not isinstance(value, int) or value > 0:
        eng.wait_ge(sem, value)


class Chain:

    def __init__(self, eng, sem, base=0):
        self.eng, self.sem, self.base, self.n = eng, sem, base, 0

    def did(self, ins):
        ins.then_inc(self.sem, 1)
        self.n += 1

    def wait(self):
        wait(self.eng, self.sem, self.base + self.n)


def make_identity(pool, ident, sem):
    pool.memset(ident, 0.0).then_inc(sem, 1)
    pool.wait_ge(sem, 1)
    pool.affine_select(out=ident, in_=ident, compare_op=ALU.not_equal, fill=1.0, base=0,
                       pattern=[[-1, P]], channel_multiplier=1).then_inc(sem, 1)


def linear_attention(nc, x, Wq, Wk, Wv, Wo, Kq, Kk, xr):
    with ExitStack() as ctx:
        def sb(name, shape, dt=F32):
            return ctx.enter_context(nc.sbuf_tensor(name, shape, dt))

        def ps(name, shape, dt=F32):
            return ctx.enter_context(nc.psum_tensor(name, shape, dt))

        def sem(name):
            return ctx.enter_context(nc.semaphore("a_" + name))

        ident = sb("a_ident", [P, P])
        causal = sb("a_causal", [P, P])
        w_raw = sb("w_raw", [P, 2, KD, H * HD])
        k_diag = sb("k_diag", [P, 2, H // 2, P])
        w_t = sb("w_t", [P, 2, 4, P])
        w_feat = sb("w_feat", [P, 2, KD, H * HD])
        wv = sb("wv", [P, KD, H * HD])
        wo = sb("wo", [P, H // 2, D])
        stats = sb("a_stats", [P, T, 6])
        mv = sb("a_mv", [P, T, 2])
        rstd = sb("a_rstd", [P, T])
        xn = sb("a_xn", [P, D])
        xT = sb("a_xT", [P, 2, KD, P])
        hi = sb("hi", [P, 2, H])
        lo = sb("lo", [P, 2, H])
        fsum = sb("fsum", [P, 2, 2 * H])
        feat = [sb("kf", [P, 2, H, F2]), sb("qf", [P, 2, H, F2])]
        v1 = sb("v1", [P, 2, H, VW])
        fT = [sb("kfT", [P, 2, G, P]), sb("qfT", [P, 2, G, P])]
        am = sb("am", [P, 2, G, P])
        state = sb("state", [P, H, VW])
        z = sb("z", [P, G])
        rz = sb("rz", [P, G])
        o_sb = sb("o_sb", [P, H * HD])
        oT = sb("oT", [P, H // 2, P])

        pP = ps("pP", [P, 1024])
        pT = [ps("pT0", [P, 512]), ps("pT1", [P, 512])]
        pA = ps("pA", [P, G, P])
        pO = ps("pO", [P, 512])
        pD = ps("pD", [P, 512])
        pW = ps("pW", [P, 512])
        o_ps = pO[:, 0:G * VW].rearrange("p (h v) -> p h v", h=G)
        d_ps = pD[:, 0:G * VW].rearrange("p (h v) -> p h v", h=G)
        y_ps = pW[:, 0:D]
        x_ps = pW[:, D:2 * D]

        s_x, s_w, s_kd, s_wv, s_wo = sem("x"), sem("w"), sem("kd"), sem("wv"), sem("wo")
        s_id, s_cz, s_kz, s_vz = sem("ident"), sem("causal"), sem("kdiag0"), sem("vzero")
        s_dve = sem("dve")
        s_var, s_std = sem("var"), sem("std")
        w_tr, w_ev, w_mm, w_cp = sem("w_tr"), sem("w_ev"), sem("w_mm"), sem("w_cp")
        xn_ready, x_tr, xT_ready = sem("xn"), sem("x_tr"), sem("xT")
        proj = [sem("k_proj"), sem("q_proj")]
        v_proj, v_copied = sem("v_proj"), sem("v_copied")
        shifted = [sem("k_shifted"), sem("q_shifted")]
        expd = [sem("k_exp"), sem("q_exp")]
        summed = [sem("k_sum"), sem("q_sum")]
        scaled = [sem("k_scaled"), sem("q_scaled")]
        f_ready = [sem("k_feat"), sem("q_feat")]
        f_tr = [sem("k_tr"), sem("q_tr")]
        fT_ready = [sem("kT"), sem("qT")]
        a_done, a_masked = sem("a_done"), sem("a_masked")
        d_done, s_upd = sem("d_done"), sem("state")
        o_done, o_norm = sem("o_done"), sem("o_norm")
        o_tr, oT_ready = sem("o_tr"), sem("oT")
        y_done, x1_done = sem("y_done"), sem("x1")

        ROUNDS = 8
        DVE_BATCH = 72

        with nc.Block() as block:

            @block.sync
            def _(sp):
                sp.dma_start(xr[:, :, :], x.rearrange("b (c p) d -> p (b c) d", p=P)).then_inc(s_x, 16)
                for m, w in enumerate((Wk, Wq)):
                    sp.dma_start(w_raw[:, m], w.rearrange("(k p) n -> p k n", p=P)).then_inc(s_w, 16)
                sp.wait_ge(s_kz, 1)
                for m, kk in enumerate((Kk, Kq)):
                    pairs = kk.rearrange("(j two) d f -> two d j f", two=2)
                    for s in range(2):
                        sp.dma_start(k_diag[HD * s:HD * s + HD, m, :, HD * s:HD * s + HD],
                                     pairs[s]).then_inc(s_kd, 16)
                sp.dma_start(wv[:, :, :], Wv.rearrange("(k p) n -> p k n", p=P)).then_inc(s_wv, 16)
                sp.dma_start(wo[:, :, :], Wo.rearrange("(k p) n -> p k n", p=P)).then_inc(s_wo, 16)

            @block.gpsimd
            def _(pool):
                pool.memset(k_diag[:, :, :, :], 0.0).then_inc(s_kz, 1)
                make_identity(pool, ident[:, :], s_id)
                pool.memset(causal[:, :], 1.0).then_inc(s_cz, 1)
                pool.wait_ge(s_cz, 1)
                pool.affine_select(out=causal[:, :], in_=causal[:, :], compare_op=ALU.is_ge, fill=0.0,
                                   base=0, pattern=[[1, P]], channel_multiplier=-1).then_inc(s_cz, 1)
                pool.memset(v1[:, :, :, HD:VW], 0.0).then_inc(s_vz, 1)
                pool.wait_ge(s_vz, 1)
                pool.memset(v1[:, :, :, HD:HD + 1], 1.0).then_inc(s_vz, 1)

                def scale(m, t, par):
                    wait(pool, summed[m], t + 1)
                    e = feat[m][:, par].rearrange("p h (s f) -> p (h s) f", s=2)
                    nc.gpsimd.tensor_tensor(e, e, fsum[:, m].unsqueeze(2).broadcast_to([P, 2 * H, HD]),
                                            ALU.mult).then_inc(scaled[m], 1)

                scale(0, 0, 0)
                scale(1, 0, 0)
                scale(0, 1, 1)

                def batch(b, last):
                    for c in range(TB):
                        if not (last and c == TB - 1):
                            scale(1, TB * b + c + 1, (c + 1) % 2)
                        if not (last and c >= TB - 2):
                            scale(0, TB * b + c + 2, c % 2)

                batch(0, False)
                with pool.Fori(1, B - 1) as b:
                    batch(b, False)
                batch(B - 1, True)

            @block.tensor
            def _(pe):
                pe.wait_ge(s_id, 2)
                pe.wait_ge(s_w, 32)

                def w_transposes(r):
                    m, j = r // 4, 2 * (r % 4)
                    if r >= 2:
                        wait(pe, w_ev, r - 1)
                    for i in range(4):
                        col = P * (j + i // 2)
                        ins = pe.transpose(pT[r % 2][:, P * i:P * i + P],
                                           w_raw[:, m, i % 2, col:col + P], ident[:, :])
                    ins.then_inc(w_tr, 1)

                def w_products(r):
                    m, j = r // 4, 2 * (r % 4)
                    wait(pe, w_ev, r + 1)
                    if r >= 2:
                        wait(pe, w_cp, r - 1)
                    out = (pP[:, 0:512], pP[:, 512:1024])[r % 2]
                    for i in range(4):
                        ins = pe.matmul(out[:, P * i:P * i + P], w_t[:, r % 2, i, :],
                                        k_diag[:, m, j + i // 2, :], start=True, stop=True)
                    ins.then_inc(w_mm, 1)

                w_transposes(0)
                pe.wait_ge(s_kd, 64)
                for r in range(ROUNDS):
                    if r + 1 < ROUNDS:
                        w_transposes(r + 1)
                    w_products(r)
                pe.wait_ge(w_cp, ROUNDS)

                def x_transposes(t):
                    wait(pe, xn_ready, t + 1)
                    wait(pe, x1_done, t - 2)
                    for k in range(KD):
                        ins = pe.transpose(x_ps[:, P * k:P * k + P], xn[:, P * k:P * k + P], ident[:, :])
                    ins.then_inc(x_tr, 1)

                def project(w, half, par, done):
                    for k in range(KD):
                        ins = pe.matmul(pP[:, 512 * half:512 * half + 512], xT[:, par, k, :],
                                        w[:, k, 512 * half:512 * half + 512],
                                        start=(k == 0), stop=(k == KD - 1))
                    ins.then_inc(done, 1)

                def project_k(t, half, par):
                    wait(pe, xT_ready, t + 1)
                    wait(pe, v_copied, 2 * t - 1 + half)
                    project(w_feat[:, 0], half, par, proj[0])

                def project_q(t, half, par):
                    wait(pe, shifted[0], 2 * t + half + 1)
                    project(w_feat[:, 1], half, par, proj[1])

                def project_v(t, half, par):
                    wait(pe, shifted[1], 2 * t + half + 1)
                    project(wv, half, par, v_proj)

                def transposes(t, g, par):
                    for m in (1, 0):
                        if g == 0:
                            wait(pe, f_ready[m], t + 1)
                            wait(pe, oT_ready, 2 * t)
                        wait(pe, fT_ready[m], 4 * t + g)
                        for h in range(G):
                            ins = pe.transpose(pT[m][:, P * h:P * h + P], feat[m][:, par, G * g + h, :],
                                               ident[:, :])
                        ins.then_inc(f_tr[m], 1)

                def chunk_scores(t, g):
                    wait(pe, fT_ready[0], 4 * t + g + 1)
                    wait(pe, fT_ready[1], 4 * t + g + 1)
                    wait(pe, a_masked, 4 * t + g)
                    for h in range(G):
                        ins = pe.matmul(pA[:, h, :], fT[0][:, g % 2, h, :], fT[1][:, g % 2, h, :],
                                        start=True, stop=True)
                    ins.then_inc(a_done, 1)

                def state_delta(b, c, g, par):
                    wait(pe, v_copied, 2 * (TB * b + c) + 2)
                    wait(pe, s_upd, 12 * b + 4 * c + g)
                    for h in range(G):
                        ins = pe.matmul(d_ps[:, h, :], feat[0][:, par, G * g + h, :],
                                        v1[:, par, G * g + h, :], start=True, stop=True)
                    ins.then_inc(d_done, 1)

                def outputs(b, c, g, par):
                    t = TB * b + c
                    wait(pe, v_copied, 2 * t + 2)
                    wait(pe, o_norm, 4 * t + g)
                    if c:
                        wait(pe, s_upd, 12 * b + 4 * (c - 1) + g + 1)
                    wait(pe, a_masked, 4 * t + g + 1)
                    for h in range(G):
                        if c:
                            pe.matmul(o_ps[:, h, :], fT[1][:, g % 2, h, :], state[:, G * g + h, :],
                                      start=True, stop=False)
                        ins = pe.matmul(o_ps[:, h, :], am[:, g % 2, h, :], v1[:, par, G * g + h, :],
                                        start=(c == 0), stop=True)
                    ins.then_inc(o_done, 1)

                def o_transposes(t):
                    wait(pe, o_norm, 4 * t + 4)
                    for half in range(2):
                        wait(pe, fT_ready[half], 4 * t + 4)
                        for j in range(4):
                            col = P * (4 * half + j)
                            ins = pe.transpose(pT[half][:, P * j:P * j + P], o_sb[:, col:col + P],
                                               ident[:, :])
                        ins.then_inc(o_tr, 1)

                def out_product(t, xT_count):
                    wait(pe, oT_ready, 2 * t + 2)
                    wait(pe, xT_ready, xT_count)
                    wait(pe, x1_done, t)
                    for j in range(H // 2):
                        ins = pe.matmul(y_ps, oT[:, j, :], wo[:, j, :], start=(j == 0), stop=(j == H // 2 - 1))
                    ins.then_inc(y_done, 1)

                x_transposes(0)
                for half in range(2):
                    project_k(0, half, 0)
                for half in range(2):
                    project_q(0, half, 0)
                pe.wait_ge(s_wv, 16)
                for half in range(2):
                    project_v(0, half, 0)
                x_transposes(1)
                for half in range(2):
                    project_k(1, half, 1)
                transposes(0, 0, 0)
                chunk_scores(0, 0)
                pe.wait_ge(s_wo, 16)

                def batch(b, last):
                    for c in range(TB):
                        t, par = TB * b + c, c % 2
                        has1, has2 = not (last and c == TB - 1), not (last and c >= TB - 2)
                        for g in range(G):
                            if g == G - 1 and has2:
                                x_transposes(t + 2)
                            if g < G - 1:
                                transposes(t, g + 1, par)
                            if has1:
                                if g < 2:
                                    project_q(t + 1, g, 1 - par)
                                else:
                                    project_v(t + 1, g - 2, 1 - par)
                            if g < G - 1:
                                chunk_scores(t, g + 1)
                            if c < TB - 1:
                                state_delta(b, c, g, par)
                            outputs(b, c, g, par)
                        if has2:
                            project_k(t + 2, 0, par)
                        o_transposes(t)
                        if has2:
                            project_k(t + 2, 1, par)
                        if has1:
                            transposes(t + 1, 0, 1 - par)
                        out_product(t, t + 3 if has2 else T)
                        if has1:
                            chunk_scores(t + 1, 0)

                batch(0, False)
                with pe.Fori(1, B - 1) as b:
                    batch(b, False)
                batch(B - 1, True)

            @block.scalar
            def _(act):
                act.wait_ge(s_var, 1)
                nc.scalar.activation(rstd[:, :], rstd[:, :], ACT.Sqrt).then_inc(s_std, 1)
                for r in range(ROUNDS):
                    wait(act, w_tr, r + 1)
                    if r >= 2:
                        wait(act, w_mm, r - 1)
                    nc.scalar.copy(w_t[:, r % 2], pT[r % 2][:, :].rearrange("p (i n) -> p i n", i=4)
                                   ).then_inc(w_ev, 1)

                def x_copy(t, par):
                    wait(act, x_tr, t + 1)
                    wait(act, v_proj, 2 * (t - 1))
                    nc.scalar.copy(xT[:, par], x_ps.rearrange("p (k n) -> p k n", k=KD)).then_inc(xT_ready, 1)

                def exponentials(m, t, half, par):
                    wait(act, shifted[m], 2 * t + half + 1)
                    e = feat[m][:, par, 8 * half:8 * half + 8, :]
                    nc.scalar.activation(e, e, ACT.Exp).then_inc(expd[m], 1)

                def v_copy(t, half, par):
                    wait(act, v_proj, 2 * t + half + 1)
                    wait(act, o_done, 4 * (t - 1))
                    wait(act, s_vz, 2)
                    nc.scalar.copy(v1[:, par, 8 * half:8 * half + 8, 0:HD],
                                   pP[:, 512 * half:512 * half + 512].rearrange("p (h d) -> p h d", h=H // 2)
                                   ).then_inc(v_copied, 1)

                def f_copies(t, g):
                    for m in (1, 0):
                        wait(act, f_tr[m], 4 * t + g + 1)
                        wait(act, o_done, 4 * t + g - 1)
                        nc.scalar.copy(fT[m][:, g % 2], pT[m][:, :].rearrange("p (h n) -> p h n", h=G)
                                       ).then_inc(fT_ready[m], 1)

                x_copy(0, 0)
                for m in range(2):
                    for half in range(2):
                        exponentials(m, 0, half, 0)
                for half in range(2):
                    v_copy(0, half, 0)
                x_copy(1, 1)
                for half in range(2):
                    exponentials(0, 1, half, 1)
                f_copies(0, 0)

                def batch(b, last):
                    for c in range(TB):
                        t, par = TB * b + c, c % 2
                        has1, has2 = not (last and c == TB - 1), not (last and c >= TB - 2)
                        f_copies(t, 1)
                        f_copies(t, 2)
                        if has1:
                            exponentials(1, t + 1, 0, 1 - par)
                            exponentials(1, t + 1, 1, 1 - par)
                        f_copies(t, 3)
                        if has1:
                            v_copy(t + 1, 0, 1 - par)
                        if has2:
                            x_copy(t + 2, par)
                        if has1:
                            v_copy(t + 1, 1, 1 - par)
                        for half in range(2):
                            wait(act, o_tr, 2 * t + half + 1)
                            wait(act, y_done, t)
                            nc.scalar.copy(oT[:, 4 * half:4 * half + 4, :],
                                           pT[half][:, :].rearrange("p (j n) -> p j n", j=4)
                                           ).then_inc(oT_ready, 1)
                        if has2:
                            exponentials(0, t + 2, 0, par)
                        if has1:
                            f_copies(t + 1, 0)
                        if has2:
                            exponentials(0, t + 2, 1, par)

                batch(0, False)
                with act.Fori(1, B - 1) as b:
                    batch(b, False)
                batch(B - 1, True)

            @block.vector
            def _(dve):
                own = Chain(dve, s_dve)
                dve.wait_ge(s_x, 16)
                for t in range(T):
                    own.did(nc.vector.bn_stats(stats[:, t, :], xr[:, t, :]))
                own.wait()
                for t in range(T):
                    own.did(nc.vector.bn_aggr(mv[:, t, :], stats[:, t, :]))
                own.wait()
                nc.vector.tensor_scalar(rstd[:, :], mv[:, :, 1], LN_EPS, None, ALU.add).then_inc(s_var, 1)
                dve.wait_ge(s_std, 1)
                own.did(nc.vector.reciprocal(rstd[:, :], rstd[:, :]))
                own.wait()

                def normalise(t):
                    wait(dve, x_tr, t)
                    nc.vector.tensor_scalar(xn[:, :], xr[:, bass.ds(t, 1), :].rearrange("p a d -> p (a d)"),
                                            mv[:, bass.ds(t, 1), 0], rstd[:, bass.ds(t, 1)],
                                            ALU.subtract, ALU.mult).then_inc(xn_ready, 1)

                normalise(0)
                for r in range(ROUNDS):
                    wait(dve, w_mm, r + 1)
                    m, col = r // 4, 2 * P * (r % 4)
                    nc.vector.tensor_copy(
                        w_feat[:, m, :, col:col + 2 * P].rearrange("p k (j n) -> p j k n", j=2),
                        pP[:, 512 * (r % 2):512 * (r % 2) + 512].rearrange("p (j k n) -> p j k n", j=2, k=KD)
                    ).then_inc(w_cp, 1)

                def shift(m, t, half, par, own):
                    hs = slice(8 * half, 8 * half + 8)
                    f = pP[:, 512 * half:512 * half + 512].rearrange("p (h f) -> p h f", h=H // 2)
                    wait(dve, proj[m], 2 * t + half + 1)
                    wait(dve, o_done, 4 * (t - 1))
                    own.did(nc.vector.tensor_reduce(hi[:, m, hs], f, AX_X, ALU.max))
                    own.did(nc.vector.tensor_reduce(lo[:, m, hs], f, AX_X, ALU.min))
                    own.wait()
                    nc.vector.tensor_tensor(feat[m][:, par, hs, 0:HD], f,
                                            hi[:, m, hs].unsqueeze(2).broadcast_to([P, H // 2, HD]), ALU.subtract)
                    nc.vector.tensor_tensor(feat[m][:, par, hs, HD:F2],
                                            lo[:, m, hs].unsqueeze(2).broadcast_to([P, H // 2, HD]), f,
                                            ALU.subtract).then_inc(shifted[m], 1)

                def denominators(m, t, par, own):
                    wait(dve, expd[m], 2 * t + 2)
                    wait(dve, scaled[m], t)
                    own.did(nc.vector.tensor_reduce(
                        fsum[:, m], feat[m][:, par].rearrange("p h (s f) -> p (h s) f", s=2), AX_X, ALU.add))
                    own.wait()
                    nc.vector.reciprocal(fsum[:, m], fsum[:, m]).then_inc(summed[m], 1)

                def clamp(m, t, par):
                    wait(dve, scaled[m], t + 1)
                    nc.vector.tensor_scalar(feat[m][:, par], feat[m][:, par], FEAT_EPS, None,
                                            ALU.max).then_inc(f_ready[m], 1)

                def mask(t, g):
                    wait(dve, a_done, 4 * t + g + 1)
                    wait(dve, o_done, 4 * t + g - 1)
                    nc.vector.tensor_tensor(am[:, g % 2], pA[:, :, :],
                                            causal[:, :].unsqueeze(1).broadcast_to([P, G, P]),
                                            ALU.mult).then_inc(a_masked, 1)

                def update(b, c, g):
                    wait(dve, d_done, 12 * b + 4 * c + g + 1)
                    wait(dve, o_done, 4 * (TB * b + c) + g + 1)
                    st = state[:, G * g:G * g + G, :]
                    if c == 0:
                        nc.vector.tensor_copy(st, d_ps).then_inc(s_upd, 1)
                    else:
                        nc.vector.tensor_tensor(st, st, d_ps, ALU.add).then_inc(s_upd, 1)

                def normalise_o(t, g, own):
                    wait(dve, o_done, 4 * t + g + 1)
                    if g == 0:
                        wait(dve, o_tr, 2 * t)
                    own.did(nc.vector.tensor_scalar(z[:, :], o_ps[:, :, HD], FEAT_EPS, None, ALU.add))
                    own.wait()
                    own.did(nc.vector.reciprocal(rz[:, :], z[:, :]))
                    own.wait()
                    nc.vector.tensor_tensor(
                        o_sb[:, 256 * g:256 * g + 256].rearrange("p (h d) -> p h d", h=G),
                        o_ps[:, :, 0:HD], rz[:, :].unsqueeze(2).broadcast_to([P, G, HD]),
                        ALU.mult).then_inc(o_norm, 1)

                def residual(t):
                    wait(dve, y_done, t + 1)
                    xt = xr[:, bass.ds(t, 1), :].rearrange("p a d -> p (a d)")
                    nc.vector.tensor_tensor(xt, xt, y_ps, ALU.add).then_inc(x1_done, 1)

                for m in range(2):
                    for half in range(2):
                        shift(m, 0, half, 0, own)
                    if m == 0:
                        denominators(0, 0, 0, own)
                        normalise(1)
                denominators(1, 0, 0, own)
                for half in range(2):
                    shift(0, 1, half, 1, own)
                clamp(0, 0, 0)
                clamp(1, 0, 0)
                denominators(0, 1, 1, own)
                dve.wait_ge(s_cz, 2)
                mask(0, 0)
                before = own.n

                def batch(b, last):
                    own = Chain(dve, s_dve, DVE_BATCH * b + before)
                    for c in range(TB):
                        t, par = TB * b + c, c % 2
                        has1, has2 = not (last and c == TB - 1), not (last and c >= TB - 2)
                        for g in range(G):
                            if g == 1 and has1:
                                shift(1, t + 1, 1, 1 - par, own)
                            if g == 2 and has1:
                                denominators(1, t + 1, 1 - par, own)
                            if g < G - 1:
                                mask(t, g + 1)
                            if g == 0 and has1:
                                shift(1, t + 1, 0, 1 - par, own)
                            if g == 1 and has1:
                                clamp(0, t + 1, 1 - par)
                            if c < TB - 1:
                                update(b, c, g)
                            normalise_o(t, g, own)
                            if g == 0 and has2:
                                normalise(t + 2)
                            if g == 2 and has1:
                                clamp(1, t + 1, 1 - par)
                        if has2:
                            shift(0, t + 2, 0, par, own)
                            shift(0, t + 2, 1, par, own)
                            denominators(0, t + 2, par, own)
                        residual(t)
                        if has1:
                            mask(t + 1, 0)
                    assert last or own.n == DVE_BATCH, own.n

                batch(0, False)
                with dve.Fori(1, B - 1) as b:
                    batch(b, False)
                batch(B - 1, True)


CD = 192
CS = CD // 2
M = 1024
JT = M // P
XH, XD = 16, 16
XV = 32
PAIRS = ((0, 0), (0, 1), (1, 0), (1, 1), (0, 2), (2, 0))
AUG = XD * len(PAIRS)
KR = AUG + 4
MASKED = 1e30
NG = B * G


def cross_attention(nc, ctx_in, mask, Wq, Wk, Wv, Wo, k_scr, q_scr, aug_scr, xr):
    with ExitStack() as ctx:
        def sb(name, shape, dt=F32):
            return ctx.enter_context(nc.sbuf_tensor(name, shape, dt))

        def ps(name, shape, dt=F32):
            return ctx.enter_context(nc.psum_tensor(name, shape, dt))

        def sem(name):
            return ctx.enter_context(nc.semaphore("b_" + name))

        ident = sb("b_ident", [P, P])
        ident_h = sb("b_ident_h", [P, P], BF16)
        wq = sb("b_wq", [P, KD, D])
        wo = sb("b_wo", [P, KD, D])
        wk = sb("b_wk", [CS, 2, D])
        wv = sb("b_wv", [CS, 2, D])
        m_col = sb("m_col", [P, B, JT], U8)
        any_on = sb("any_on", [P, B])
        big = sb("big", [P, B])
        q_scale = sb("q_scale", [P, B])
        bias = sb("bias", [P, G, JT])
        last_row = sb("last_row", [P, 1])
        other_rows = sb("other_rows", [P, 1])
        q_aug = sb("q_aug", [P, L], BF16)
        mv = sb("b_mv", [P, T, 2])
        rstd = sb("b_rstd", [P, T])
        xn = sb("b_xn", [P, TB, D])
        xT = sb("b_xT", [P, KD, L])
        cx = sb("cx", [P, JT, CD])
        cT = sb("cT", [CS, 2, M])
        rest = sb("rest", [P, 512])
        zero = sb("b_zero", [P, 1])
        parts = sb("parts", [P, 2, 3, 2, 512], BF16)
        ks = sb("ks", [P, 2, XH, M], BF16)
        qs = sb("qs", [P, 2, XH, L], BF16)
        v_new = sb("v_new", [P, G, JT, G * XD])
        v1 = sb("b_v1", [P, G, JT, G, XV])
        neg_max = sb("neg_max", [P, 2, TB, G])
        max_rest = sb("max_rest", [P, TB, G])
        max_parts = sb("max_parts", [P, TB, G, XV], BF16)
        pt = sb("pt", [P, 2, G, L])
        ot = sb("ot", [P, L])
        rz = sb("b_rz", [P, TB, G])
        o = sb("b_o", [P, TB, D])
        oT = xT
        stats = ot[:, 0:6 * T].rearrange("p (t s) -> p t s", t=T)
        m_row = qs[:, 1, 0:4, :].rearrange("p h n -> p (h n)").bitcast(U8).rearrange("p (b m) -> p b m", b=B)
        aug_f = pt[:, :, :, :].rearrange("p s i n -> p (s i n)").rearrange("p (b m) -> p b m", b=B)
        k_aug = ks[:, 1, 0:B, :]

        pS1 = ps("pS1", [P, 2, M])
        pS2 = ps("pS2", [P, 2, L])
        pO = ps("b_pO", [P, L])
        pM = ps("pM", [P, 512])

        s_wk, s_scale, s_w, s_mask, s_cx, s_id = sem("wk"), sem("scale"), sem("w"), sem("mask"), sem("cx"), sem("ident")
        s_dve, s_act = sem("dve"), sem("act")
        s_z, s_row, s_var, s_std, s_aug = sem("zero"), sem("row"), sem("var"), sem("std"), sem("aug")
        xn_ready = sem("xn")
        filled, emptied = sem("filled"), sem("emptied")
        head_done, rounded, split_done = sem("head"), sem("rounded"), sem("split")
        stored = [sem("k0_stored"), sem("k1_stored"), sem("q_stored")]
        aug_stored = sem("aug_stored")
        k_loaded, q_loaded = sem("k_loaded"), sem("q_loaded")
        placed = sem("placed")
        s1_done, max_done = sem("s1"), sem("max")
        m_ready = sem("m_ready")
        s2_done, exp_done, av_done, ot_ready = sem("s2"), sem("exp"), sem("av"), sem("ot")

        N_LOAD = 16 * (len(PAIRS) + 1)

        def small_steps(hg, j, first, last):
            plan = {(0, 2): [("o_turn", 3)] * (not first)}
            for g in range(1, G):
                plan[g, 2] = [("o_turn", g - 1)]
            if not first:
                plan[0, 3], plan[0, 4] = [("oT", 0)], [("oT", 1)]
                plan[0, 5], plan[0, 6] = [("y", 0)], [("y", 1)]
            for g in range(G):
                plan[g, 6] = plan.get((g, 6), []) + [("m_turn", g + 1)] * (g < G - 1 or not last)
            if not last:
                plan[0, 0], plan[0, 1], plan[0, 7], plan[1, 0] = [[("cT", i)] for i in range(4)]
                plan[1, 1], plan[1, 3], plan[1, 4] = [("k", 0)], [("k", 2)], [("k", 3)]
                plan[1, 2] = plan[1, 2] + [("k", 1)]
                plan[1, 5], plan[1, 6] = [("xT", 0)], [("xT", 1)] + plan[1, 6]
                plan[1, 7], plan[2, 0] = [("q", 0)], [("q", 1)]
                plan[2, 1], plan[2, 3], plan[2, 4], plan[2, 5] = [[("v", i)] for i in range(4)]
            return plan.get((hg, j), [])

        PREPARE = [("cT", i) for i in range(4)] + [("k", i) for i in range(4)] + \
            [("xT", 0), ("xT", 1), ("q", 0), ("q", 1)] + [("v", i) for i in range(4)]
        free_banks = [pM, pO, pS2[:, 0, :], pS2[:, 1, :]]

        def prepare_wait(n):
            kind, i = PREPARE[n]
            return n - i
        FINISH = [("o_turn", 3), ("oT", 0), ("oT", 1), ("y", 0), ("y", 1)]

        OWN_FIRST, OWN_MIDDLE = 15, 16

        def slot(b, n):
            return bass.ds((3 * b + n) % 2, 1)

        def batch_of(b, kind, i, hg):
            if kind in ("cT", "k", "v", "xT", "q"):
                return b + 1
            return b - 1 if kind in ("oT", "y") or (kind == "o_turn" and i > hg) else b

        def steps_of(first, last):
            return sum(len(small_steps(g, j, first, last)) for g in range(G) for j in range(JT))

        START = len(PREPARE) + 1
        FIRST, MIDDLE = steps_of(True, False), steps_of(False, False)

        def steps_before(b):
            return (b - 1) * MIDDLE + (START + FIRST)

        def score_units(hg, j, last):
            ahead, u = (hg + 1, 2 * j + 4) if j < 6 else (hg + 2, 2 * j - 12)
            if ahead >= G and last:
                return []
            return [(ahead // G, ahead % G, u), (ahead // G, ahead % G, u + 1)]

        with nc.Block() as block:

            @block.sync
            def _(sp):
                def load_cx(b):
                    sp.dma_start(cx[:, :, :], ctx_in[b].rearrange("(j p) c -> p j c", p=P)).then_inc(s_cx, 16)

                def stack_k(b):
                    for half in range(2):
                        n = 3 * b + half
                        wait(sp, split_done, 2 * (n + 1))
                        for c in range(3):
                            sp.dma_start(k_scr[b, c].rearrange("(m p) n -> p m n", p=P)[:, :, 512 * half:512 * half + 512],
                                         parts[:, n % 2, c]).then_inc(stored[half], 16)
                    for half in range(2):
                        wait(sp, stored[half], 48 * (b + 1))
                    wait(sp, s2_done, G * JT * G * (b - 1))
                    for s, pair in enumerate(PAIRS):
                        sp.dma_start(ks[XD * s:XD * s + XD, b % 2],
                                     k_scr[b, pair[1]].rearrange("(h d) n -> d h n", d=XD)).then_inc(k_loaded, 16)
                    if isinstance(b, int) and b == 0:
                        sp.wait_ge(s_aug, 3)
                        for bb in range(B):
                            sp.dma_start(aug_scr[bb], k_aug[AUG:KR, bb]).then_inc(aug_stored, 16)
                        sp.wait_ge(aug_stored, 16 * B)
                    sp.dma_start(ks[AUG:KR, b % 2],
                                 aug_scr[b].unsqueeze(1).broadcast_to([4, XH, M])).then_inc(k_loaded, 16)

                def stack_q(b):
                    n = 3 * b + 2
                    wait(sp, split_done, 2 * (n + 1))
                    for c in range(3):
                        sp.dma_start(q_scr[b, c].rearrange("(m p) n -> p m n", p=P),
                                     parts[:, n % 2, c]).then_inc(stored[2], 16)
                    wait(sp, stored[2], 48 * (b + 1))
                    for s, pair in enumerate(PAIRS):
                        sp.dma_start(qs[XD * s:XD * s + XD, b % 2],
                                     q_scr[b, pair[0]].rearrange("(h d) n -> d h n", d=XD)).then_inc(q_loaded, 16)
                    sp.dma_start(qs[AUG:KR, b % 2],
                                 q_aug[AUG:KR, :].unsqueeze(1).broadcast_to([4, XH, L])).then_inc(q_loaded, 16)

                load_cx(0)
                for w, src in ((wk, Wk), (wv, Wv)):
                    sp.dma_start(w[:, :, :], src.rearrange("(s p) n -> p s n", p=CS)).then_inc(s_wk, 16)
                flat = mask.rearrange("b m -> (b m)").unsqueeze(0)
                sp.dma_start(m_row.rearrange("p b m -> p (b m)"),
                             flat.broadcast_to([P, B * M])).then_inc(s_mask, 16)
                with nc.allow_non_contiguous_dma(reason="4096 bytes of the mask"):
                    sp.dma_start(m_col[:, :, :], mask.rearrange("b (j p) -> p b j", p=P)).then_inc(s_mask, 16)
                for w, src in ((wq, Wq), (wo, Wo)):
                    sp.dma_start(w[:, :, :], src.rearrange("(k p) n -> p k n", p=P)).then_inc(s_w, 16)
                wait(sp, filled, 4)
                load_cx(1)
                stack_k(0)
                stack_q(0)
                for b in range(1, B):
                    n = sum(len(small_steps(0, j, b == 1, False)) for j in range(JT)) + 1
                    if b + 1 < B:
                        wait(sp, filled, n + (START if b == 1 else steps_before(b - 1)))
                        load_cx(b + 1)
                    stack_k(b)
                    stack_q(b)

            @block.gpsimd
            def _(pool):
                make_identity(pool, ident[:, :], s_id)
                pool.memset(last_row[:, :], 0.0).then_inc(s_row, 1)
                pool.wait_ge(s_row, 1)
                pool.affine_select(out=last_row[:, :], in_=last_row[:, :], compare_op=ALU.not_equal, fill=1.0,
                                   base=-(KR - 1), pattern=[[0, 1]], channel_multiplier=1).then_inc(s_row, 1)
                pool.memset(q_aug[:, :], 0.0).then_inc(s_row, 1)
                pool.memset(max_parts[:, :, :, :], 0.0).then_inc(s_z, 1)
                pool.memset(v1[:, :, :, :, XD:XV], 0.0).then_inc(s_z, 1)
                pool.wait_ge(s_z, 2)
                pool.memset(v1[:, :, :, :, XD:XD + 1], 1.0).then_inc(s_z, 1)
                pool.memset(zero[:, :], 0.0).then_inc(s_z, 1)
                pool.wait_ge(s_z, 4)

                def split(b, kind, i, n):
                    s, m = (slot(b, i // 2), i % 2) if kind == "k" else (slot(b, 2), i)
                    part = [parts[:, s, c, m, :].rearrange("p a n -> p (a n)") for c in range(3)]
                    wait(pool, emptied, n + 1)
                    nc.gpsimd.tensor_tensor(part[1], rest[:, :], zero[:, :].broadcast_to([P, 512]), ALU.add
                                            ).then_inc(rounded, 1)
                    wait(pool, rounded, 6 * (b - 1) + (i if kind == "k" else 4 + i) + 1)
                    nc.gpsimd.tensor_tensor(part[2], rest[:, :], part[1], ALU.subtract).then_inc(split_done, 1)

                def batch(b, start, first):
                    n = 0
                    for hg in range(G):
                        for j in range(JT):
                            for kind, i in small_steps(hg, j, first, False):
                                if kind in ("k", "q"):
                                    split(batch_of(b, kind, i, hg), kind, i, start + n)
                                n += 1

                batch(0, START, True)
                with pool.Fori(1, B - 1) as b:
                    batch(b, steps_before(b), False)

            @block.tensor
            def _(pe):
                def small(b, kind, i, n, pM=pM, before=None):
                    wait(pe, emptied, n if before is None else before)
                    if kind == "cT":
                        wait(pe, s_cx, 16 * (b + 1))
                        for q in range(4):
                            j, s = 2 * i + q // 2, q % 2
                            ins = pe.transpose(pM[0:CS, P * q:P * q + P], cx[:, j, CS * s:CS * s + CS],
                                               ident[:, :])
                    elif kind == "k":
                        pe.wait_ge(s_wk, 32)
                        half, m = i // 2, i % 2
                        for s in range(2):
                            ins = pe.matmul(pM[:, :], wk[:, s, P * m:P * m + P],
                                            cT[:, s, 512 * half:512 * half + 512],
                                            start=(s == 0), stop=(s == 1))
                    elif kind == "v":
                        for q in range(2):
                            j = 2 * i + q
                            for s in range(2):
                                ins = pe.matmul(pM[:, D * q:D * q + D], cT[:, s, P * j:P * j + P],
                                                wv[:, s, :], start=(s == 0), stop=(s == 1))
                    elif kind == "xT":
                        wait(pe, xn_ready, b + 1)
                        for q in range(4):
                            t, k = 2 * i + q // 2, q % 2
                            ins = pe.transpose(pM[:, P * q:P * q + P], xn[:, t, P * k:P * k + P],
                                               ident[:, :])
                    elif kind == "q":
                        pe.wait_ge(s_w, 32)
                        for k in range(KD):
                            ins = pe.matmul(pM[:, :], wq[:, k, P * i:P * i + P], xT[:, k, :],
                                            start=(k == 0), stop=(k == KD - 1))
                    elif kind == "m_turn":
                        wait(pe, m_ready, G * b + i + 1)
                        for t in range(TB):
                            ins = pe.transpose(pM[:, 64 * t:64 * t + 64].bitcast(BF16),
                                               max_parts[:, t, :, :].rearrange("p h v -> p (h v)"),
                                               ident_h[:, :])
                    elif kind == "o_turn":
                        wait(pe, ot_ready, G * b + i + 1)
                        for t in range(TB):
                            ins = pe.transpose(pM[:, P * t:P * t + P], ot[:, P * t:P * t + P], ident[:, :])
                    elif kind == "oT":
                        for t in range(TB):
                            ins = pe.transpose(pM[:, P * t:P * t + P], o[:, t, P * i:P * i + P], ident[:, :])
                    elif kind == "y":
                        for q in range(2):
                            t = 2 * i + q
                            for k in range(KD):
                                ins = pe.matmul(pM[:, D * q:D * q + D], oT[:, k, P * t:P * t + P],
                                                wo[:, k, :], start=(k == 0), stop=(k == KD - 1))
                    ins.then_inc(filled, 1)

                def scores_by_token(b, hg, u):
                    U = 16 * (G * b + hg) + u
                    t, h, slot = u // G, G * hg + u % G, u % 2
                    if u == 0 and hg == 0:
                        wait(pe, k_loaded, N_LOAD * (b + 1))
                        wait(pe, q_loaded, N_LOAD * (b + 1))
                    wait(pe, max_done, U - 1)
                    par = b % 2
                    for half in range(2):
                        ins = pe.matmul(
                            pS1[:, slot, 512 * half:512 * half + 512],
                            qs[0:KR, bass.ds(par, 1), h, P * t:P * t + P].rearrange("r a n -> r (a n)"),
                            ks[0:KR, bass.ds(par, 1), h, 512 * half:512 * half + 512
                               ].rearrange("r a n -> r (a n)"), start=True, stop=True)
                    ins.then_inc(s1_done, 1)

                def scores_by_context(b, hg, j, i, steps):
                    n = G * (JT * (G * b + hg) + j) + i
                    if j == 0 and i == 0:
                        wait(pe, emptied, steps)
                    wait(pe, exp_done, n - 1)
                    par, h = b % 2, G * hg + i
                    pe.matmul(pS2[:, i % 2, :],
                              ks[0:KR, bass.ds(par, 1), h, P * j:P * j + P].rearrange("r a n -> r (a n)"),
                              qs[0:KR, bass.ds(par, 1), h, :].rearrange("r a n -> r (a n)"),
                              start=True, stop=True).then_inc(s2_done, 1)

                def weighted_values(b, hg, j):
                    n = G * b + hg
                    wait(pe, exp_done, G * (JT * n + j + 1))
                    if j == 0:
                        wait(pe, ot_ready, n)
                        wait(pe, placed, n + 1)
                    for i in range(G):
                        ins = pe.matmul(pO[XV * i:XV * i + XV, :], v1[:, hg, j, i, :], pt[:, j % 2, i, :],
                                        start=(j == 0), stop=(j == JT - 1))
                    ins.then_inc(av_done, 1)

                pe.wait_ge(s_id, 3)
                for n, (kind, i) in enumerate(PREPARE):
                    small(0, kind, i, n, free_banks[i], prepare_wait(n))
                pe.wait_ge(s_z, 3)
                for u in range(16):
                    scores_by_token(0, 0, u)
                small(0, "m_turn", 0, START - 1)
                for u in range(4):
                    scores_by_token(0, 1, u)

                def batch(b, start, first, last):
                    n = 0
                    for hg in range(G):
                        for j in range(JT):
                            units = score_units(hg, j, last)
                            for i in range(G):
                                scores_by_context(b, hg, j, i, start + n)
                                if i == 1:
                                    for ahead, g, u in units[:1]:
                                        scores_by_token(b + ahead, g, u)
                                    if j:
                                        weighted_values(b, hg, j - 1)
                                    elif hg:
                                        weighted_values(b, hg - 1, JT - 1)
                                    elif not first:
                                        weighted_values(b - 1, G - 1, JT - 1)
                                    for kind, k in small_steps(hg, j, first, last)[:-1]:
                                        small(batch_of(b, kind, k, hg), kind, k, start + n)
                                        n += 1
                            for ahead, g, u in units[1:]:
                                scores_by_token(b + ahead, g, u)
                            for kind, i in small_steps(hg, j, first, last)[-1:]:
                                small(batch_of(b, kind, i, hg), kind, i, start + n)
                                n += 1
                    return start + n

                batch(0, START, True, False)
                with pe.Fori(1, B - 1) as b:
                    batch(b, steps_before(b), False, False)
                n = batch(B - 1, steps_before(B - 1), False, True)
                weighted_values(B - 1, G - 1, JT - 1)
                for q, (kind, i) in enumerate(FINISH):
                    small(B - 1, kind, i, n + q)

            @block.scalar
            def _(act):
                act.wait_ge(s_id, 2)
                nc.scalar.copy(ident_h[:, :], ident[:, :]).then_inc(s_id, 1)
                act.wait_ge(s_var, 1)
                nc.scalar.activation(rstd[:, :], rstd[:, :], ACT.Sqrt).then_inc(s_std, 1)

                def small(b, kind, i, n, pM=pM):
                    if kind in ("y", "o_turn"):
                        return
                    wait(act, filled, n + 1)
                    if kind == "cT":
                        nc.scalar.copy(cT[:, :, 2 * P * i:2 * P * i + 2 * P].rearrange("c s (j n) -> c j s n", j=2),
                                       pM[0:CS, :].rearrange("c (j s n) -> c j s n", j=2, s=2)
                                       ).then_inc(emptied, 1)
                    elif kind == "xT":
                        nc.scalar.copy(xT[:, :, 2 * P * i:2 * P * i + 2 * P].rearrange("c k (t n) -> c t k n", t=2),
                                       pM[:, :].rearrange("c (t k n) -> c t k n", t=2, k=2)
                                       ).then_inc(emptied, 1)
                    elif kind == "k":
                        wait(act, stored[1 + i // 2], 48 * b)
                        nc.scalar.copy(parts[:, slot(b, i // 2), 0, i % 2, :].rearrange("p a n -> p (a n)"),
                                       pM[:, :]).then_inc(head_done, 1)
                    elif kind == "q":
                        wait(act, stored[0], 48 * (b + 1))
                        act.wait_ge(s_scale, 1)
                        nc.scalar.activation(parts[:, slot(b, 2), 0, i, :].rearrange("p a n -> p (a n)"), pM[:, :],
                                             ACT.Copy, scale=q_scale[:, bass.ds(b, 1)]).then_inc(head_done, 1)
                    elif kind == "v":
                        if i == 0:
                            wait(act, placed, G * b)
                        nc.scalar.copy(v_new[:, :, 2 * i:2 * i + 2, :].rearrange("p g j c -> p j g c"),
                                       pM[:, :].rearrange("p (j g c) -> p j g c", j=2, g=G)
                                       ).then_inc(emptied, 1)
                    elif kind == "oT":
                        nc.scalar.copy(oT[:, i, :], pM[:, :]).then_inc(emptied, 1)
                    elif kind == "m_turn":
                        bb, g = (b + 1, 0) if i == G else (b, i)
                        act.wait_ge(s_id, 3)
                        for q in range(G):
                            ins = nc.scalar.copy(
                                qs[AUG:KR, bass.ds(bb % 2, 1), G * g + q, :].rearrange("r a n -> r (a n)"),
                                pM[XV * q:XV * q + 4, 0:TB * 64].bitcast(BF16))
                        ins.then_inc(emptied, 1)

                def exponentials(b, hg, j, between=None):
                    n = JT * (G * b + hg) + j
                    wait(act, av_done, n - 1)
                    if j == 0:
                        wait(act, placed, G * b + hg + 1)
                    for i in range(G):
                        wait(act, s2_done, G * n + i + 1)
                        nc.scalar.activation(pt[:, j % 2, i, :], pS2[:, i % 2, :], ACT.Exp,
                                             bias=bias[:, hg, j:j + 1]).then_inc(exp_done, 1)
                        if i == 1:
                            between()

                def values_copy(n):
                    wait(act, av_done, JT * n)
                    nc.scalar.copy(ot[:, :], pO[:, :]).then_inc(ot_ready, 1)

                for n, (kind, i) in enumerate(PREPARE):
                    small(0, kind, i, n, free_banks[i])
                small(0, "m_turn", 0, START - 1)

                def batch(b, start, first, last):
                    n = 0
                    for hg in range(G):
                        for j in range(JT):
                            def between():
                                nonlocal n
                                if j == 0 and (hg or not first):
                                    values_copy(G * b + hg)
                                for kind, i in small_steps(hg, j, first, last)[:-1]:
                                    small(batch_of(b, kind, i, hg), kind, i, start + n)
                                    n += 1

                            exponentials(b, hg, j, between)
                            for kind, i in small_steps(hg, j, first, last)[-1:]:
                                small(batch_of(b, kind, i, hg), kind, i, start + n)
                                n += 1
                    return start + n

                batch(0, START, True, False)
                with act.Fori(1, B - 1) as b:
                    batch(b, steps_before(b), False, False)
                n = batch(B - 1, steps_before(B - 1), False, True)
                values_copy(NG)
                for q, (kind, i) in enumerate(FINISH):
                    small(B - 1, kind, i, n + q)

            @block.vector
            def _(dve):
                own = Chain(dve, s_dve)

                def small(b, kind, i, n, own, pM=pM, first_batch=False):
                    if kind in ("k", "q"):
                        s, m = (slot(b, i // 2), i % 2) if kind == "k" else (slot(b, 2), i)
                        head = parts[:, s, 0, m, :].rearrange("p a n -> p (a n)")
                        nth = 6 * b + (i if kind == "k" else 4 + i)
                        wait(dve, head_done, nth + 1)
                        wait(dve, split_done, nth)
                        if kind == "k":
                            nc.vector.tensor_tensor(rest[:, :], pM[:, :], head, ALU.subtract
                                                    ).then_inc(emptied, 1)
                        else:
                            nc.vector.scalar_tensor_tensor(rest[:, :], pM[:, :], q_scale[:, bass.ds(b, 1)],
                                                           head, ALU.mult, ALU.subtract).then_inc(emptied, 1)
                        if first_batch:
                            part = [parts[:, s, c, m, :].rearrange("p a n -> p (a n)") for c in range(3)]
                            wait(dve, emptied, n + 1)
                            own.did(nc.vector.tensor_copy(part[1], rest[:, :]))
                            own.wait()
                            nc.vector.tensor_tensor(part[2], rest[:, :], part[1], ALU.subtract).then_inc(split_done, 1)
                    elif kind == "o_turn":
                        wait(dve, filled, n + 1)
                        turned = pM[:, :].rearrange("p (t h v) -> p t h v", t=TB, h=G)
                        own.did(nc.vector.reciprocal(rz[:, :, :], turned[:, :, :, XD]))
                        own.wait()
                        nc.vector.tensor_tensor(
                            o[:, :, G * XD * i:G * XD * i + G * XD].rearrange("p t (h d) -> p t h d", h=G),
                            turned[:, :, :, 0:XD], rz[:, :, :].unsqueeze(3).broadcast_to([P, TB, G, XD]),
                            ALU.mult).then_inc(emptied, 1)
                    elif kind == "y":
                        wait(dve, filled, n + 1)
                        xt = xr[:, bass.ds(TB * b + 2 * i, 2), :]
                        nc.vector.tensor_tensor(xt, xt, pM[:, :].rearrange("p (t d) -> p t d", t=2),
                                                ALU.add).then_inc(emptied, 1)

                def normalise(b):
                    for t in range(TB):
                        ins = nc.vector.tensor_scalar(
                            xn[:, t, :], xr[:, bass.ds(TB * b + t, 1), :].rearrange("p a d -> p (a d)"),
                            mv[:, bass.ds(TB * b + t, 1), 0], rstd[:, bass.ds(TB * b + t, 1)],
                            ALU.subtract, ALU.mult)
                    ins.then_inc(xn_ready, 1)

                for t in range(T):
                    own.did(nc.vector.bn_stats(stats[:, t, :], xr[:, t, :]))
                own.wait()
                for t in range(T):
                    own.did(nc.vector.bn_aggr(mv[:, t, :], stats[:, t, :]))
                own.wait()
                nc.vector.tensor_scalar(rstd[:, :], mv[:, :, 1], LN_EPS, None, ALU.add).then_inc(s_var, 1)
                dve.wait_ge(s_std, 1)
                own.did(nc.vector.reciprocal(rstd[:, :], rstd[:, :]))
                own.wait()
                normalise(0)

                def prepare(kinds):
                    for n, (kind, i) in enumerate(PREPARE):
                        if kind in kinds:
                            small(0, kind, i, n, own, free_banks[i], first_batch=True)

                prepare(("k",))
                dve.wait_ge(s_mask, 32)
                own.did(nc.vector.tensor_reduce(any_on[:, :], m_row, AX_X, ALU.max))
                own.wait()
                nc.vector.tensor_scalar(q_scale[:, :], any_on[:, :], XD ** -0.5, None, ALU.mult).then_inc(s_scale, 1)
                own.did(nc.vector.tensor_scalar(big[:, :], any_on[:, :], MASKED, None, ALU.mult))
                dve.wait_ge(s_scale, 1)
                prepare(("q",))
                dve.wait_ge(s_row, 3)
                own.did(nc.vector.tensor_scalar(other_rows[:, :], last_row[:, :], -1.0, 1.0, ALU.mult, ALU.add))
                own.wait()
                for b in range(B):
                    own.did(nc.vector.tensor_scalar(aug_f[AUG:KR, b], m_row[AUG:KR, b], -1.0,
                                                    big[AUG:KR, b:b + 1], ALU.add, ALU.mult))
                own.wait()
                nc.vector.tensor_scalar(q_aug[:, :], q_aug[:, :], last_row[:, :], None, ALU.add).then_inc(s_aug, 1)
                for b in range(0, B, 2):
                    nc.vector.tensor_scalar(k_aug[AUG:KR, b:b + 2], aug_f[AUG:KR, b:b + 2], last_row[AUG:KR, :],
                                            other_rows[AUG:KR, :], ALU.mult, ALU.add).then_inc(s_aug, 1)

                def maximum(b, hg, u):
                    U = 16 * (G * b + hg) + u
                    wait(dve, s1_done, U + 1)
                    nc.vector.tensor_reduce(neg_max[:, hg % 2, u // G, u % G:u % G + 1], pS1[:, u % 2, :],
                                            AX_X, ALU.max, negate=True).then_inc(max_done, 1)

                def place(b, hg):
                    wait(dve, av_done, JT * (G * (b - 1) + hg + 1))
                    nc.vector.tensor_copy(v1[:, hg, :, :, 0:XD],
                                          v_new[:, hg].rearrange("p j (i d) -> p j i d", i=G))
                    nc.vector.tensor_scalar(bias[:, hg, :], m_col[:, bass.ds(b, 1), :].rearrange("p a j -> p (a j)"),
                                            -1.0, big[:, bass.ds(b, 1)], ALU.add, ALU.mult).then_inc(placed, 1)

                def split_max(b, hg, own, steps):
                    wait(dve, max_done, 16 * (G * b + hg + 1))
                    wait(dve, filled, steps)
                    nm = neg_max[:, hg % 2]
                    own.did(nc.vector.tensor_copy(max_parts[:, :, :, 0], nm))
                    own.wait()
                    own.did(nc.vector.tensor_tensor(max_rest[:, :, :], nm, max_parts[:, :, :, 0], ALU.subtract))
                    own.wait()
                    own.did(nc.vector.tensor_copy(max_parts[:, :, :, 1], max_rest[:, :, :]))
                    own.wait()
                    nc.vector.tensor_tensor(max_parts[:, :, :, 2], max_rest[:, :, :], max_parts[:, :, :, 1],
                                            ALU.subtract).then_inc(m_ready, 1)

                dve.wait_ge(s_z, 1)
                wait(dve, emptied, len(PREPARE))
                dve.wait_ge(s_z, 3)
                for hg in range(G):
                    place(0, hg)
                for u in range(16):
                    maximum(0, 0, u)
                split_max(0, 0, own, 0)
                for u in range(4):
                    maximum(0, 1, u)
                before = own.n

                def batch(b, start, first, last, own):
                    n = 0
                    for hg in range(G):
                        for j in range(JT):
                            if j == 6 and (hg < G - 1 or not last):
                                if hg < G - 1:
                                    split_max(b, hg + 1, own, start + n)
                                else:
                                    split_max(b + 1, 0, own, start + n)
                            units = score_units(hg, j, last)
                            for ahead, g, u in units[:1]:
                                maximum(b + ahead, g, u)
                            for kind, i in small_steps(hg, j, first, last)[:-1]:
                                small(batch_of(b, kind, i, hg), kind, i, start + n, own)
                                n += 1
                            for ahead, g, u in units[1:]:
                                maximum(b + ahead, g, u)
                            for kind, i in small_steps(hg, j, first, last)[-1:]:
                                small(batch_of(b, kind, i, hg), kind, i, start + n, own)
                                n += 1
                            if (hg, j) == (0, 7) and not last:
                                normalise(b + 1)
                            if (hg, j) == (0, 2) and not first:
                                place(b, G - 1)
                            if (hg, j) == (2, 5) and not last:
                                wait(dve, emptied, start + n)
                                place(b + 1, 0)
                                place(b + 1, 1)
                            if (hg, j) == (3, 2) and not last:
                                place(b + 1, 2)
                    return start + n

                def owned(b):
                    return Chain(dve, s_dve, before + OWN_FIRST + OWN_MIDDLE * (b - 1))

                own = Chain(dve, s_dve, before)
                batch(0, START, True, False, own)
                assert own.n == OWN_FIRST, own.n
                with dve.Fori(1, B - 1) as b:
                    own = owned(b)
                    batch(b, steps_before(b), False, False, own)
                    assert own.n == OWN_MIDDLE, own.n
                own = owned(B - 1)
                n = batch(B - 1, steps_before(B - 1), False, True, own)
                for q, (kind, i) in enumerate(FINISH):
                    small(B - 1, kind, i, n + q, own)


E_, FH = 8, 512
TE = T * E_
KH = FH // P
R = B * L + P
SLOTS = 2 * T + E_


def experts(nc, gate_w, w1, b1, ln1_g, ln1_b, w2, b2, ln_g, ln_b, x_rows, y_rows, xr, out):
    with ExitStack() as ctx:
        def sb(name, shape, dt=F32):
            return ctx.enter_context(nc.sbuf_tensor("c_" + name, shape, dt))

        def ps(name, shape, dt=F32):
            return ctx.enter_context(nc.psum_tensor("c_" + name, shape, dt))

        def sem(name):
            return ctx.enter_context(nc.semaphore("c_" + name))

        ident = sb("ident", [P, P])
        earlier = sb("earlier", [P, P])
        ones = sb("ones", [P, P])
        half = sb("half", [P, 1])
        w1_sb = sb("w1", [P, E_, KD, FH])
        w2_sb = sb("w2", [P, E_, KH, D])
        b1_sb = sb("b1", [P, E_, FH])
        b2_sb = sb("b2", [P, E_, D])
        gb = sb("gb", [P, 2, E_, KH])
        lng = sb("lng", [P, D])
        lnb = sb("lnb", [P, D])
        gate = sb("gate", [P, KD, 32])
        f = sb("f", [P, T, D])
        stats = sb("stats", [P, T, 6])
        mv = sb("mv", [P, T, 2])
        rstd = sb("rstd", [P, T])
        fT = sb("fT", [P, KD, B * L])
        lgT = sb("lgT", [P, 512])
        g1 = sb("g1", [P, T, E_])
        g2 = sb("g2", [P, T, E_])
        eq = sb("eq", [P, T, E_])
        sel = sb("sel", [P, 2, T, E_])
        both = sb("both", [P, T, E_])
        rank = sb("rank", [P, T, E_])
        tot = sb("tot", [P, 2, T, E_])
        order = sb("order", [P, E_])
        order_i = sb("order_i", [P, E_], I32)
        base = sb("base", [P, E_])
        base_i = sb("base_i", [P, E_], I32)
        slot_i = sb("slot_i", [P, SLOTS], I32)
        lane_i = sb("lane_i", [P, 1], I32)
        lane = sb("lane", [P, 1])
        slot = sb("slot", [P, SLOTS])
        top = sb("top", [P, 2, T])
        tmp = sb("tmp", [P, T])
        pos = sb("pos", [P, 2, T])
        pos_i = sb("pos_i", [P, 2, T], I32)
        n_e = sb("n_e", [P, E_])
        pad_i = sb("pad_i", [P, E_], I32)
        tiles_i = sb("tiles_i", [P, E_], I32)
        ends = sb("ends", [P, 2, E_])
        over = sb("over", [P, SLOTS, E_])
        s_exp = sb("s_exp", [P, SLOTS])
        s_row = sb("s_row", [P, SLOTS])
        s_tab = sb("s_tab", [P, 2, SLOTS], I32)
        y_base = sb("y_base", [P, E_])
        y_pos = sb("y_pos", [P, 2, T], I32)
        zrow = sb("zrow", [P, D])
        xs = sb("xs", [P, 4, D])
        xsT = sb("xsT", [P, 2, KD, P])
        h = sb("h", [P, 2, FH])
        hst = sb("hst", [P, 2, 6])
        hmv = sb("hmv", [P, 2, 2])
        hrs = sb("hrs", [P, 2, 1])
        hT = sb("hT", [P, 2, KH, P])
        gbn = sb("gbn", [P, 2, 2, KH])
        ys = sb("ys", [P, 2, D])
        y = sb("y", [P, 4, 2, D])
        acc = sb("acc", [P, T, D])

        pX = [ps("pX0", [P, 512]), ps("pX1", [P, 512])]
        pH = [ps("pH0", [P, 512]), ps("pH1", [P, 512])]
        pT = [ps("pT0", [P, 512]), ps("pT1", [P, 512])]
        pY = [ps("pY0", [P, 512]), ps("pY1", [P, 512])]

        s_gate, s_w1, s_w2, s_par, s_ln = sem("gate"), sem("w1"), sem("w2"), sem("par"), sem("ln")
        s_id, s_k, s_gz, s_dve = sem("ident"), sem("consts"), sem("gate0"), sem("dve")
        s_var, s_rstd, f_ready = sem("var"), sem("rstd"), sem("f")
        t_done, t_copied, lg_done, lg_copied = sem("t_done"), sem("t_copied"), sem("lg"), sem("lg_copied")
        lt_done, g_ready, g_exp, both_ready, rank_done = sem("lt"), sem("g"), sem("gexp"), sem("both"), sem("rank")
        pad_ready, pos_ready, sent, padded, tab_ready = sem("pad"), sem("pos"), sem("sent"), sem("padded"), sem("tab")
        def two(name):
            return [sem(name + "0"), sem(name + "1")]

        xs_in, xs_t, xsT_ready = [sem(f"xs_in{j}") for j in range(4)], two("xs_t"), two("xsT")
        h_done, h_read, h_var, h_rstd, h_norm = two("h"), two("h_read"), two("h_var"), two("h_rstd"), two("h_norm")
        h_t, hT_ready, gb_now = two("h_t"), two("hT"), two("gb_now")
        y_done, y_ready, y_out = two("y"), two("ys"), two("y_out")
        y_in = [sem(f"y_in{i}") for i in range(4)]
        a_done, a_stats, a_std, o_ready, o_out = sem("a"), sem("a_st"), sem("a_std"), sem("o"), sem("o_out")

        OWN_TILE = 2
        ROUNDS = SLOTS // 4

        def at(i, j):
            return i + j // 4, j % 4

        def nth(i, j):
            return 2 * i + j // 2

        def slot_steps(engine, step):
            for j in range(4):
                step(0, j)
            with engine.Fori(1, ROUNDS - 1) as i:
                for j in range(4):
                    step(i, j)
            for j in range(4):
                step(ROUNDS - 1, j)

        def exists(i, j):
            return not isinstance(i, int) or 0 <= 4 * i + j < SLOTS

        with nc.Block() as block:

            @block.sync
            def _(sp):
                sp.wait_ge(s_gz, 1)
                sp.dma_start(gate[:, :, 0:E_], gate_w.rearrange("(k p) e -> p k e", p=P)).then_inc(s_gate, 16)
                for k in range(KD):
                    sp.dma_start(w1_sb[:, :, k, :], w1[:, P * k:P * k + P, :].rearrange("e p h -> p e h")
                                 ).then_inc(s_w1, 16)
                sp.dma_start(b1_sb[:, :, :].rearrange("p e h -> p (e h)"),
                             b1.rearrange("e h -> (e h)").unsqueeze(0).broadcast_to([P, E_ * FH])).then_inc(s_par, 16)
                with nc.allow_non_contiguous_dma(reason="two vectors of each expert, by hidden unit"):
                    for i, v in enumerate((ln1_g, ln1_b)):
                        sp.dma_start(gb[:, i], v.rearrange("e (c p) -> p e c", p=P)).then_inc(s_par, 16)
                for k in range(KH):
                    sp.dma_start(w2_sb[:, :, k, :], w2[:, P * k:P * k + P, :].rearrange("e p d -> p e d")
                                 ).then_inc(s_w2, 16)
                sp.dma_start(b2_sb[:, :, :].rearrange("p e h -> p (e h)"),
                             b2.rearrange("e h -> (e h)").unsqueeze(0).broadcast_to([P, E_ * D])).then_inc(s_par, 16)
                for t, v in ((lng, ln_g), (lnb, ln_b)):
                    sp.dma_start(t[:, :], v.unsqueeze(0).broadcast_to([P, D])).then_inc(s_ln, 16)

                sp.wait_ge(tab_ready, 1)
                sp.wait_ge(sent, 16 * 2 * T)
                sp.wait_ge(padded, 16 * E_)

                def fetch(i, j):
                    if not isinstance(i, int):
                        wait(sp, xs_t[j % 2], nth(i - 1, j) + 1)
                    row = sp.value_load(s_tab[0:1, 1, bass.ds(4 * i + j, 1)], min_val=0, max_val=E_ * R - P)
                    sp.dma_start(xs[:, j, :], x_rows[bass.ds(row, P), :]).then_inc(xs_in[j], 16)

                for j in range(4):
                    fetch(0, j)
                with sp.Fori(1, ROUNDS) as i:
                    for j in range(4):
                        fetch(i, j)

                for t in range(T):
                    wait(sp, o_ready, t + 1)
                    sp.dma_start(out[t // TB, P * (t % TB):P * (t % TB) + P, :], acc[:, t, :]).then_inc(o_out, 16)
                sp.wait_ge(o_out, 16 * T)

            @block.gpsimd
            def _(pool):
                pool.memset(gate[:, :, :], 0.0).then_inc(s_gz, 1)
                pool.memset(half[:, :], -0.5).then_inc(s_k, 1)
                pool.wait_ge(s_k, 1)
                pool.wait_ge(s_var, 1)
                nc.gpsimd.tensor_tensor(rstd[:, :], rstd[:, :], half[:, :].broadcast_to([P, T]), ALU.pow
                                        ).then_inc(s_rstd, 1)
                make_identity(pool, ident[:, :], s_id)
                pool.memset(ones[:, :], 1.0).then_inc(s_k, 1)
                pool.memset(earlier[:, :], 1.0).then_inc(s_k, 1)
                pool.wait_ge(s_k, 3)
                pool.affine_select(out=earlier[:, :], in_=earlier[:, :], compare_op=ALU.is_gt, fill=0.0,
                                   base=0, pattern=[[1, P]], channel_multiplier=-1).then_inc(s_k, 1)
                pool.iota(order_i[:, :], pattern=[[-1, E_]], base=E_, channel_multiplier=0).then_inc(s_k, 1)
                pool.iota(base_i[:, :], pattern=[[R, E_]], base=0, channel_multiplier=0).then_inc(s_k, 1)
                pool.iota(slot_i[:, :], pattern=[[1, SLOTS]], base=0, channel_multiplier=0).then_inc(s_k, 1)
                pool.iota(lane_i[:, :], pattern=[[0, 1]], base=0, channel_multiplier=1).then_inc(s_k, 1)
                pool.memset(zrow[:, :], 0.0).then_inc(s_k, 1)
                pool.wait_ge(s_k, 9)

                pool.wait_ge(pos_ready, 1)
                for k in range(2):
                    for t in range(T):
                        pool.indirect_dma_start(
                            out=x_rows, out_offset=bass.IndirectOffsetOnAxis(
                                ap=pos_i[:, k, t:t + 1].bitcast(U32), axis=0),
                            in_=f[:, t, :], in_offset=None).then_inc(sent, 16)
                for e in range(E_):
                    pool.indirect_dma_start(
                        out=x_rows, out_offset=bass.IndirectOffsetOnAxis(
                            ap=pad_i[:, e:e + 1].bitcast(U32), axis=0),
                        in_=zrow[:, :], in_offset=None).then_inc(padded, 16)

                def power(i, j):
                    par = j % 2
                    wait(pool, h_var[par], nth(i, j) + 1)
                    nc.gpsimd.tensor_tensor(hrs[:, par, :], hrs[:, par, :], half[:, :], ALU.pow).then_inc(h_rstd[par], 1)

                slot_steps(pool, power)

                for par in range(2):
                    pool.wait_ge(y_out[par], 16 * (SLOTS // 2))
                for t in range(T):
                    if t >= 4:
                        pool.wait_ge(a_done, t - 3)
                    for k in range(2):
                        pool.indirect_dma_start(
                            out=y[:, t % 4, k, :], out_offset=None, in_=y_rows,
                            in_offset=bass.IndirectOffsetOnAxis(ap=y_pos[:, k, t:t + 1].bitcast(U32), axis=0)
                        ).then_inc(y_in[t % 4], 16)

            @block.tensor
            def _(pe):
                pe.wait_ge(s_id, 2)
                for n in range(2 * T // 4):
                    wait(pe, f_ready, 2 * n + 2)
                    if n >= 2:
                        wait(pe, t_copied, n - 1)
                    for q in range(4):
                        t, k = 2 * n + q // 2, q % 2
                        ins = pe.transpose(pX[n % 2][:, P * q:P * q + P], f[:, t, P * k:P * k + P], ident[:, :])
                    ins.then_inc(t_done, 1)
                pe.wait_ge(s_gate, 16)
                pe.wait_ge(t_copied, T // 2)
                for k in range(KD):
                    for q in range(B):
                        ins = pe.matmul(pH[0][32 * q:32 * q + 32, :], gate[:, k, :], fT[:, k, L * q:L * q + L],
                                        start=(k == 0), stop=(k == KD - 1))
                ins.then_inc(lg_done, 1)
                pe.wait_ge(lg_copied, 1)
                for c in range(TB):
                    ins = pe.transpose(pH[1][:, P * c:P * c + P], lgT[:, P * c:P * c + P], ident[:, :])
                ins.then_inc(lt_done, 1)
                pe.wait_ge(both_ready, 1)
                pe.wait_ge(s_k, 4)
                sel_2d = both[:, :, :].rearrange("p t e -> p (t e)")
                pe.matmul(pT[0][:, 0:TE], earlier[:, :], sel_2d, start=True, stop=True).then_inc(rank_done, 1)
                pe.matmul(pT[1][:, 0:TE], ones[:, :], sel_2d, start=True, stop=True).then_inc(rank_done, 1)

                pe.wait_ge(tab_ready, 1)
                pe.wait_ge(s_w1, 16 * KD)
                pe.wait_ge(s_w2, 16 * KH)

                def x_transposes(i, j):
                    par = j % 2
                    wait(pe, xs_in[j], 16 * (i + 1))
                    wait(pe, xsT_ready[par], nth(i, j))
                    for k in range(KD):
                        ins = pe.transpose(pX[par][:, P * k:P * k + P], xs[:, j, P * k:P * k + P], ident[:, :])
                    ins.then_inc(xs_t[par], 1)

                def up(i, j):
                    par = j % 2
                    e = pe.value_load(s_tab[0:1, 0, bass.ds(4 * i + j, 1)], min_val=0, max_val=E_ - 1)
                    wait(pe, xsT_ready[par], nth(i, j) + 1)
                    wait(pe, h_read[par], nth(i, j))
                    for k in range(KD):
                        ins = pe.matmul(pH[par][:, :], xsT[:, par, k, :],
                                        w1_sb[:, bass.ds(e, 1), k, :].rearrange("p a h -> p (a h)"),
                                        start=(k == 0), stop=(k == KD - 1))
                    ins.then_inc(h_done[par], 1)

                def h_transposes(i, j):
                    par = j % 2
                    wait(pe, h_norm[par], nth(i, j) + 1)
                    wait(pe, hT_ready[par], nth(i, j))
                    for k in range(KH):
                        ins = pe.transpose(pT[par][:, P * k:P * k + P], h[:, par, P * k:P * k + P], ident[:, :])
                    ins.then_inc(h_t[par], 1)

                def down(i, j):
                    par = j % 2
                    e = pe.value_load(s_tab[0:1, 0, bass.ds(4 * i + j, 1)], min_val=0, max_val=E_ - 1)
                    wait(pe, hT_ready[par], nth(i, j) + 1)
                    wait(pe, y_ready[par], nth(i, j))
                    for k in range(KH):
                        ins = pe.matmul(pY[par][:, 0:D], hT[:, par, k, :],
                                        w2_sb[:, bass.ds(e, 1), k, :].rearrange("p a d -> p (a d)"),
                                        start=(k == 0), stop=(k == KH - 1))
                    ins.then_inc(y_done[par], 1)

                x_transposes(0, 0)
                x_transposes(0, 1)
                up(0, 0)

                def step(i, j):
                    if exists(i, j + 1):
                        up(*at(i, j + 1))
                    h_transposes(i, j)
                    if exists(i, j + 2):
                        x_transposes(*at(i, j + 2))
                    if exists(i, j - 1):
                        down(*at(i, j - 1))

                slot_steps(pe, step)
                down(ROUNDS - 1, 3)

            @block.scalar
            def _(act):
                for n in range(T // 2):
                    wait(act, t_done, n + 1)
                    nc.scalar.copy(fT[:, :, 2 * P * n:2 * P * n + 2 * P].rearrange("p k (t n) -> p t k n", t=2),
                                   pX[n % 2][:, :].rearrange("p (t k n) -> p t k n", t=2, k=2)
                                   ).then_inc(t_copied, 1)
                act.wait_ge(lg_done, 1)
                nc.scalar.copy(lgT[:, :], pH[0][:, :]).then_inc(lg_copied, 1)
                act.wait_ge(g_ready, 1)
                nc.scalar.activation(g1[:, :, :], g1[:, :, :], ACT.Exp).then_inc(g_exp, 1)
                act.wait_ge(s_par, 64)

                def x_copy(i, j):
                    par = j % 2
                    wait(act, xs_t[par], nth(i, j) + 1)
                    wait(act, h_done[par], nth(i, j))
                    nc.scalar.copy(xsT[:, par], pX[par][:, 0:D].rearrange("p (k n) -> p k n", k=KD)
                                   ).then_inc(xsT_ready[par], 1)

                def gelu(i, j):
                    par = j % 2
                    wait(act, gb_now[par], nth(i, j) + 1)
                    wait(act, y_done[par], nth(i, j))
                    wait(act, h_t[par], nth(i, j) + 1)
                    for k in range(KH):
                        ins = nc.scalar.activation(hT[:, par, k, :], pT[par][:, P * k:P * k + P], ACT.Gelu,
                                                   bias=gbn[:, par, 1, k:k + 1], scale=gbn[:, par, 0, k:k + 1])
                    ins.then_inc(hT_ready[par], 1)

                def store(i, j):
                    par = j % 2
                    wait(act, y_ready[par], nth(i, j) + 1)
                    act.dma_start(y_rows[bass.ds(P * (4 * i + j), P), :], ys[:, par, :]).then_inc(y_out[par], 16)

                x_copy(0, 0)
                x_copy(0, 1)

                def step(i, j):
                    if exists(i, j + 2):
                        x_copy(*at(i, j + 2))
                    gelu(i, j)
                    if exists(i, j - 1):
                        store(*at(i, j - 1))

                slot_steps(act, step)
                store(ROUNDS - 1, 3)

                for t in range(T):
                    act.wait_ge(a_stats, t + 1)
                    nc.scalar.activation(rstd[:, t:t + 1], rstd[:, t:t + 1], ACT.Sqrt).then_inc(a_std, 1)

            @block.vector
            def _(dve):
                own = Chain(dve, s_dve)

                def did(ins):
                    own.did(ins)
                    own.wait()

                for t in range(T):
                    own.did(nc.vector.bn_stats(stats[:, t, :], xr[:, t, :]))
                own.wait()
                for t in range(T):
                    own.did(nc.vector.bn_aggr(mv[:, t, :], stats[:, t, :]))
                own.wait()
                nc.vector.tensor_scalar(rstd[:, :], mv[:, :, 1], LN_EPS, None, ALU.add).then_inc(s_var, 1)
                dve.wait_ge(s_rstd, 1)
                for t in range(T):
                    nc.vector.tensor_scalar(f[:, t, :], xr[:, t, :], mv[:, t, 0:1], rstd[:, t:t + 1],
                                            ALU.subtract, ALU.mult).then_inc(f_ready, 1)
                dve.wait_ge(s_k, 9)
                own.did(nc.vector.tensor_copy(order[:, :], order_i[:, :]))
                own.did(nc.vector.tensor_copy(base[:, :], base_i[:, :]))
                own.did(nc.vector.tensor_copy(slot[:, :], slot_i[:, :]))
                own.did(nc.vector.tensor_copy(lane[:, :], lane_i[:, :]))

                dve.wait_ge(lt_done, 1)
                did(nc.vector.tensor_copy(
                    g1[:, :, :].rearrange("p (q c) e -> p c q e", q=B),
                    pH[1][:, :].rearrange("p (c q e) -> p c q e", c=TB, q=B)[:, :, :, 0:E_]))
                did(nc.vector.tensor_reduce(tmp[:, :], g1[:, :, :], AX_X, ALU.max))
                nc.vector.tensor_tensor(g1[:, :, :], g1[:, :, :], tmp[:, :].unsqueeze(2).broadcast_to([P, T, E_]),
                                        ALU.subtract).then_inc(g_ready, 1)
                dve.wait_ge(g_exp, 1)
                g = g1
                for c in range(2):
                    did(nc.vector.tensor_reduce(top[:, c, :], g[:, :, :], AX_X, ALU.max))
                    did(nc.vector.tensor_tensor(eq[:, :, :], g[:, :, :],
                                                top[:, c, :].unsqueeze(2).broadcast_to([P, T, E_]), ALU.is_equal))
                    did(nc.vector.tensor_tensor(eq[:, :, :], eq[:, :, :],
                                                order[:, :].unsqueeze(1).broadcast_to([P, T, E_]), ALU.mult))
                    did(nc.vector.tensor_reduce(tmp[:, :], eq[:, :, :], AX_X, ALU.max))
                    did(nc.vector.tensor_tensor(sel[:, c], eq[:, :, :],
                                                tmp[:, :].unsqueeze(2).broadcast_to([P, T, E_]), ALU.is_equal))
                    if c == 0:
                        did(nc.vector.scalar_tensor_tensor(
                            g2[:, :, :].rearrange("p t e -> p (t e)"), sel[:, 0].rearrange("p t e -> p (t e)"),
                            -2.0, g1[:, :, :].rearrange("p t e -> p (t e)"), ALU.mult, ALU.add))
                        g = g2
                nc.vector.tensor_tensor(both[:, :, :], sel[:, 0], sel[:, 1], ALU.add).then_inc(both_ready, 1)
                did(nc.vector.tensor_tensor(tmp[:, :], top[:, 0, :], top[:, 1, :], ALU.add))
                did(nc.vector.reciprocal(tmp[:, :], tmp[:, :]))
                own.did(nc.vector.tensor_tensor(top[:, :, :], top[:, :, :],
                                                tmp[:, :].unsqueeze(1).broadcast_to([P, 2, T]), ALU.mult))
                dve.wait_ge(rank_done, 2)
                did(nc.vector.tensor_copy(tot[:, 0].rearrange("p t e -> p (t e)"), pT[1][:, 0:TE]))
                cur = 0
                for step in (1, 2, 4, 8):
                    nc.vector.tensor_copy(tot[:, 1 - cur, 0:step, :], tot[:, cur, 0:step, :])
                    did(nc.vector.tensor_tensor(tot[:, 1 - cur, step:T, :], tot[:, cur, step:T, :],
                                                tot[:, cur, 0:T - step, :], ALU.add))
                    cur = 1 - cur
                own.did(nc.vector.tensor_copy(n_e[:, :], tot[:, cur, T - 1, :]))
                did(nc.vector.tensor_tensor(rank[:, 0, :], pT[0][:, 0:E_], base[:, :], ALU.add))
                did(nc.vector.tensor_tensor(rank[:, 1:T, :].rearrange("p t e -> p (t e)"), pT[0][:, E_:TE],
                                            tot[:, cur, 0:T - 1, :].rearrange("p t e -> p (t e)"), ALU.add))
                did(nc.vector.tensor_tensor(rank[:, 1:T, :], rank[:, 1:T, :],
                                            base[:, :].unsqueeze(1).broadcast_to([P, T - 1, E_]), ALU.add))
                for c in range(2):
                    did(nc.vector.tensor_tensor(eq[:, :, :], sel[:, c], rank[:, :, :], ALU.mult))
                    did(nc.vector.tensor_reduce(pos[:, c, :], eq[:, :, :], AX_X, ALU.add))
                own.did(nc.vector.tensor_tensor(eq[:, 0, :], n_e[:, :], base[:, :], ALU.add))
                own.wait()
                own.did(nc.vector.tensor_scalar(pad_i[:, :], eq[:, 0, :], lane[:, :], None, ALU.add))
                own.wait()
                nc.vector.tensor_copy(pos_i[:, :, :], pos[:, :, :]).then_inc(pos_ready, 1)
                did(nc.vector.tensor_scalar(tiles_i[:, :], n_e[:, :], float(P - 1), None, ALU.add))
                did(nc.vector.tensor_scalar(tiles_i[:, :], tiles_i[:, :], 7, None, ALU.logical_shift_right))
                did(nc.vector.tensor_copy(ends[:, 0, :], tiles_i[:, :]))
                cur = 0
                for step in (1, 2, 4):
                    nc.vector.tensor_copy(ends[:, 1 - cur, 0:step], ends[:, cur, 0:step])
                    did(nc.vector.tensor_tensor(ends[:, 1 - cur, step:E_], ends[:, cur, step:E_],
                                                ends[:, cur, 0:E_ - step], ALU.add))
                    cur = 1 - cur
                end = ends[:, cur, :]
                did(nc.vector.tensor_scalar(tmp[:, 0:1], end[:, E_ - 1:E_], -1.0, None, ALU.add))
                did(nc.vector.tensor_scalar(slot[:, :], slot[:, :], tmp[:, 0:1], None, ALU.min))
                did(nc.vector.tensor_tensor(over[:, :, :], slot[:, :].unsqueeze(2).broadcast_to([P, SLOTS, E_]),
                                            end.unsqueeze(1).broadcast_to([P, SLOTS, E_]), ALU.is_ge))
                did(nc.vector.tensor_reduce(s_exp[:, :], over[:, :, :], AX_X, ALU.add))
                own.did(nc.vector.tensor_scalar(n_e[:, :], tiles_i[:, :], 1.0, None, ALU.mult))
                own.wait()
                did(nc.vector.tensor_tensor(over[:, :, :], over[:, :, :],
                                            n_e[:, :].unsqueeze(1).broadcast_to([P, SLOTS, E_]), ALU.mult))
                did(nc.vector.tensor_reduce(s_row[:, :], over[:, :, :], AX_X, ALU.add))
                did(nc.vector.tensor_tensor(s_row[:, :], slot[:, :], s_row[:, :], ALU.subtract))
                did(nc.vector.tensor_scalar(s_row[:, :], s_row[:, :], float(P), None, ALU.mult))
                did(nc.vector.scalar_tensor_tensor(s_row[:, :], s_exp[:, :], float(R), s_row[:, :],
                                                   ALU.mult, ALU.add))
                own.did(nc.vector.tensor_tensor(y_base[:, :], end, n_e[:, :], ALU.subtract))
                own.wait()
                did(nc.vector.scalar_tensor_tensor(y_base[:, :], y_base[:, :], float(P), base[:, :],
                                                   ALU.mult, ALU.subtract))
                did(nc.vector.tensor_tensor(rank[:, :, :], rank[:, :, :],
                                            y_base[:, :].unsqueeze(1).broadcast_to([P, T, E_]), ALU.add))
                for c in range(2):
                    did(nc.vector.tensor_tensor(eq[:, :, :], sel[:, c], rank[:, :, :], ALU.mult))
                    did(nc.vector.tensor_reduce(pos[:, c, :], eq[:, :, :], AX_X, ALU.add))
                own.did(nc.vector.tensor_copy(y_pos[:, :, :], pos[:, :, :]))
                own.did(nc.vector.tensor_copy(s_tab[:, 0, :], s_exp[:, :]))
                own.wait()
                nc.vector.tensor_copy(s_tab[:, 1, :], s_row[:, :]).then_inc(tab_ready, 1)
                dve.wait_ge(tab_ready, 1)
                dve.wait_ge(s_par, 64)

                def first(i, j, own):
                    par = j % 2
                    e = dve.value_load(s_tab[0:1, 0, bass.ds(4 * i + j, 1)], min_val=0, max_val=E_ - 1)
                    wait(dve, h_done[par], nth(i, j) + 1)
                    wait(dve, h_t[par], nth(i, j))
                    nc.vector.tensor_tensor(h[:, par, :], pH[par][:, :],
                                            b1_sb[:, bass.ds(e, 1), :].rearrange("p a h -> p (a h)"),
                                            ALU.add).then_inc(h_read[par], 1)
                    wait(dve, h_read[par], nth(i, j) + 1)
                    own.did(nc.vector.bn_stats(hst[:, par, :], h[:, par, :]))
                    wait(dve, hT_ready[par], nth(i, j))
                    own.wait()
                    nc.vector.tensor_scalar(gbn[:, par, :, :], gb[:, :, bass.ds(e, 1), :].rearrange("p g a k -> p g (a k)"),
                                            1.0, None, ALU.mult).then_inc(gb_now[par], 1)
                    own.did(nc.vector.bn_aggr(hmv[:, par, :], hst[:, par, :]))
                    own.wait()
                    nc.vector.tensor_scalar(hrs[:, par, :], hmv[:, par, 1:2], LN_EPS, None, ALU.add
                                            ).then_inc(h_var[par], 1)

                def second(i, j):
                    par = j % 2
                    wait(dve, h_rstd[par], nth(i, j) + 1)
                    nc.vector.tensor_scalar(h[:, par, :], h[:, par, :], hmv[:, par, 0:1], hrs[:, par, :],
                                            ALU.subtract, ALU.mult).then_inc(h_norm[par], 1)

                def third(i, j):
                    par = j % 2
                    e = dve.value_load(s_tab[0:1, 0, bass.ds(4 * i + j, 1)], min_val=0, max_val=E_ - 1)
                    wait(dve, y_done[par], nth(i, j) + 1)
                    wait(dve, y_out[par], 16 * nth(i, j))
                    nc.vector.tensor_tensor(ys[:, par, :], pY[par][:, 0:D],
                                            b2_sb[:, bass.ds(e, 1), :].rearrange("p a d -> p (a d)"),
                                            ALU.add).then_inc(y_ready[par], 1)

                before = own.n
                first(0, 0, own)
                second(0, 0)

                def step(i, j):
                    own = Chain(dve, s_dve, before + OWN_TILE * (4 * i + j + 1))
                    if exists(i, j + 1):
                        first(*at(i, j + 1), own)
                        second(*at(i, j + 1))
                    if exists(i, j - 1):
                        third(*at(i, j - 1))

                slot_steps(dve, step)
                third(ROUNDS - 1, 3)

                dve.wait_ge(s_ln, 32)
                own = Chain(dve, s_dve, before + OWN_TILE * SLOTS)

                def gather(t):
                    wait(dve, y_in[t % 4], 32 * (t // 4 + 1))
                    a = acc[:, t, :]
                    own.did(nc.vector.scalar_tensor_tensor(a, y[:, t % 4, 0, :], top[:, 0, t:t + 1], f[:, t, :],
                                                           ALU.mult, ALU.add))
                    own.wait()
                    nc.vector.scalar_tensor_tensor(a, y[:, t % 4, 1, :], top[:, 1, t:t + 1], a,
                                                   ALU.mult, ALU.add).then_inc(a_done, 1)
                    wait(dve, a_done, t + 1)
                    own.did(nc.vector.bn_stats(stats[:, t, :], a))
                    own.wait()
                    own.did(nc.vector.bn_aggr(mv[:, t, :], stats[:, t, :]))
                    own.wait()
                    nc.vector.tensor_scalar(rstd[:, t:t + 1], mv[:, t, 1:2], LN_EPS, None, ALU.add
                                            ).then_inc(a_stats, 1)

                def finish(t):
                    a = acc[:, t, :]
                    wait(dve, a_std, t + 1)
                    own.did(nc.vector.reciprocal(rstd[:, t:t + 1], rstd[:, t:t + 1]))
                    own.wait()
                    own.did(nc.vector.tensor_scalar(a, a, mv[:, t, 0:1], rstd[:, t:t + 1], ALU.subtract, ALU.mult))
                    own.wait()
                    own.did(nc.vector.tensor_tensor(a, a, lng[:, :], ALU.mult))
                    own.did(nc.vector.tensor_tensor(xr[:, t, :], xr[:, t, :], lnb[:, :], ALU.add))
                    own.wait()
                    nc.vector.tensor_tensor(a, a, xr[:, t, :], ALU.add).then_inc(o_ready, 1)

                for t in range(T):
                    gather(t)
                    if t:
                        finish(t - 1)
                finish(T - 1)


def decoder_layer(nc, x, ctx_in, mask, a_wq, a_wk, a_wv, a_wo, a_kq, a_kk, x_wq, x_wk, x_wv, x_wo,
                  gate_w, w1, b1, ln1_g, ln1_b, w2, b2, ln_g, ln_b, out):
    k_scr = nc.dram_tensor("k_scr", (B, 3, D, M), BF16).ap()
    q_scr = nc.dram_tensor("q_scr", (B, 3, D, L), BF16).ap()
    aug_scr = nc.dram_tensor("aug_scr", (B, 4, M), BF16).ap()
    x_rows = nc.dram_tensor("x_rows", (E_ * R, D), F32).ap()
    y_rows = nc.dram_tensor("y_rows", (SLOTS * P, D), F32).ap()
    with nc.sbuf_tensor("xr", [P, T, D], F32) as xr:
        linear_attention(nc, x, a_wq, a_wk, a_wv, a_wo, a_kq, a_kk, xr)
        cross_attention(nc, ctx_in, mask, x_wq, x_wk, x_wv, x_wo, k_scr, q_scr, aug_scr, xr)
        experts(nc, gate_w, w1, b1, ln1_g, ln1_b, w2, b2, ln_g, ln_b, x_rows, y_rows, xr, out)


_INS = ['x', 'ctx_768', 'mask_BxS2_bf1', 'L0_attn_Wq', 'L0_attn_Wk', 'L0_attn_Wv', 'L0_attn_Wo',
        'L0_attn_Kq', 'L0_attn_Kk', 'L0_xattn_Wq', 'L0_xattn_Wk', 'L0_xattn_Wv', 'L0_xattn_Wo',
        'L0_ffn_gate_w', 'L0_ffn_w1', 'L0_ffn_b1', 'L0_ffn_ln1_g', 'L0_ffn_ln1_b', 'L0_ffn_w2',
        'L0_ffn_b2', 'L0_ffn_ln_g', 'L0_ffn_ln_b']
_OUTS = [((B, L, D), 'float32')]


def kernel(**inputs):
    import numpy as _np
    import concourse.bacc as _bacc
    from concourse import mybir as _mybir
    from concourse.bass_utils import run_bass_kernel_spmd as _run

    nc = _bacc.Bacc("TRN2", target_bir_lowering=False, num_devices=1)
    arrays, args = {}, []
    for name in _INS:
        a = _np.ascontiguousarray(inputs[name])
        if a.dtype.kind == "b":
            a = a.view(_np.uint8)
        arrays[f"in_{name}_dram"] = a
        args.append(nc.dram_tensor(f"in_{name}_dram", a.shape, _mybir.dt.from_np(a.dtype), kind="ExternalInput").ap())
    for i, (shape, dtype) in enumerate(_OUTS):
        dt = _mybir.dt.from_np(_np.dtype(dtype))
        args.append(nc.dram_tensor(f"out_{i}_dram", shape, dt, kind="ExternalOutput").ap())
    decoder_layer(nc, *args)
    r = _run(nc, [arrays], core_ids=[0])
    got = tuple(r.results[0][f"out_{i}_dram"] for i in range(len(_OUTS)))
    return got[0]
```

```python
from contextlib import ExitStack

import concourse.bass as bass
from concourse import mybir

P = 128
F32 = mybir.dt.float32
BF16 = mybir.dt.bfloat16
I32 = mybir.dt.int32
U32 = mybir.dt.uint32
U8 = mybir.dt.uint8
ALU = mybir.AluOpType
ACT = mybir.ActivationFunctionType
AX_X = mybir.AxisListType.X

B, L, D = 4, 512, 256
T = B * L // P
TB = L // P
KD = D // P
H, HD = 16, 64
F2 = 2 * HD
VW = 96
G = 4
LN_EPS = 1e-5
FEAT_EPS = 1e-12


def wait(eng, sem, value):
    if not isinstance(value, int) or value > 0:
        eng.wait_ge(sem, value)


class Chain:

    def __init__(self, eng, sem, base=0):
        self.eng, self.sem, self.base, self.n = eng, sem, base, 0

    def did(self, ins):
        ins.then_inc(self.sem, 1)
        self.n += 1

    def wait(self):
        wait(self.eng, self.sem, self.base + self.n)


def make_identity(pool, ident, sem):
    pool.memset(ident, 0.0).then_inc(sem, 1)
    pool.wait_ge(sem, 1)
    pool.affine_select(out=ident, in_=ident, compare_op=ALU.not_equal, fill=1.0, base=0,
                       pattern=[[-1, P]], channel_multiplier=1).then_inc(sem, 1)


def linear_attention(nc, x, Wq, Wk, Wv, Wo, Kq, Kk, xr):
    with ExitStack() as ctx:
        def sb(name, shape, dt=F32):
            return ctx.enter_context(nc.sbuf_tensor(name, shape, dt))

        def ps(name, shape, dt=F32):
            return ctx.enter_context(nc.psum_tensor(name, shape, dt))

        def sem(name):
            return ctx.enter_context(nc.semaphore("a_" + name))

        ident = sb("a_ident", [P, P])
        causal = sb("a_causal", [P, P])
        w_raw = sb("w_raw", [P, 2, KD, H * HD])
        k_diag = sb("k_diag", [P, 2, H // 2, P])
        w_t = sb("w_t", [P, 2, 4, P])
        w_feat = sb("w_feat", [P, 2, KD, H * HD])
        wv = sb("wv", [P, KD, H * HD])
        wo = sb("wo", [P, H // 2, D])
        stats = sb("a_stats", [P, T, 6])
        mv = sb("a_mv", [P, T, 2])
        rstd = sb("a_rstd", [P, T])
        xn = sb("a_xn", [P, D])
        xT = sb("a_xT", [P, 2, KD, P])
        hi = sb("hi", [P, 2, H])
        lo = sb("lo", [P, 2, H])
        fsum = sb("fsum", [P, 2, 2 * H])
        feat = [sb("kf", [P, 2, H, F2]), sb("qf", [P, 2, H, F2])]
        v1 = sb("v1", [P, 2, H, VW])
        fT = [sb("kfT", [P, 2, G, P]), sb("qfT", [P, 2, G, P])]
        am = sb("am", [P, 2, G, P])
        state = sb("state", [P, H, VW])
        z = sb("z", [P, G])
        rz = sb("rz", [P, G])
        o_sb = sb("o_sb", [P, H * HD])
        oT = sb("oT", [P, H // 2, P])

        pP = ps("pP", [P, 1024])
        pT = [ps("pT0", [P, 512]), ps("pT1", [P, 512])]
        pA = ps("pA", [P, G, P])
        pO = ps("pO", [P, 512])
        pD = ps("pD", [P, 512])
        pW = ps("pW", [P, 512])
        o_ps = pO[:, 0:G * VW].rearrange("p (h v) -> p h v", h=G)
        d_ps = pD[:, 0:G * VW].rearrange("p (h v) -> p h v", h=G)
        y_ps = pW[:, 0:D]
        x_ps = pW[:, D:2 * D]

        s_x = [sem(f"x_batch{b}") for b in range(B)]
        s_w, s_kd, s_wv, s_wo = [sem("wk"), sem("wq")], [sem("kk"), sem("kq")], sem("wv"), sem("wo")
        s_id, s_cz, s_kz, s_vz = sem("ident"), sem("causal"), sem("kdiag0"), sem("vzero")
        s_dve = sem("dve")
        s_var, s_std = sem("var"), sem("std")
        w_tr, w_ev, w_mm, w_cp = sem("w_tr"), sem("w_ev"), sem("w_mm"), sem("w_cp")
        xn_ready, x_tr, xT_ready = sem("xn"), sem("x_tr"), sem("xT")
        proj = [sem("k_proj"), sem("q_proj")]
        v_proj, v_copied = sem("v_proj"), sem("v_copied")
        shifted = [sem("k_shifted"), sem("q_shifted")]
        expd = [sem("k_exp"), sem("q_exp")]
        summed = [sem("k_sum"), sem("q_sum")]
        scaled = [sem("k_scaled"), sem("q_scaled")]
        f_ready = [sem("k_feat"), sem("q_feat")]
        f_tr = [sem("k_tr"), sem("q_tr")]
        fT_ready = [sem("kT"), sem("qT")]
        a_done, a_masked = sem("a_done"), sem("a_masked")
        d_done, s_upd = sem("d_done"), sem("state")
        o_done, o_norm = sem("o_done"), sem("o_norm")
        o_tr, oT_ready = sem("o_tr"), sem("oT")
        y_done, x1_done = sem("y_done"), sem("x1")

        ROUNDS = 8
        DVE_BATCH = 72

        with nc.Block() as block:

            @block.sync
            def _(sp):
                sp.wait_ge(s_kz, 1)
                for m, (w, kk) in enumerate(((Wk, Kk), (Wq, Kq))):
                    sp.dma_start(w_raw[:, m], w.rearrange("(k p) n -> p k n", p=P)).then_inc(s_w[m], 16)
                    pairs = kk.rearrange("(j two) d f -> two d j f", two=2)
                    for s in range(2):
                        sp.dma_start(k_diag[HD * s:HD * s + HD, m, :, HD * s:HD * s + HD],
                                     pairs[s]).then_inc(s_kd[m], 16)
                    for b in range(2 * m, 2 * m + 2):
                        sp.dma_start(xr[:, TB * b:TB * b + TB, :], x[b].rearrange("(c p) d -> p c d", p=P)
                                     ).then_inc(s_x[b], 16)
                sp.dma_start(wv[:, :, :], Wv.rearrange("(k p) n -> p k n", p=P)).then_inc(s_wv, 16)
                sp.dma_start(wo[:, :, :], Wo.rearrange("(k p) n -> p k n", p=P)).then_inc(s_wo, 16)

            @block.gpsimd
            def _(pool):
                pool.memset(k_diag[:, :, :, :], 0.0).then_inc(s_kz, 1)
                make_identity(pool, ident[:, :], s_id)
                pool.memset(causal[:, :], 1.0).then_inc(s_cz, 1)
                pool.wait_ge(s_cz, 1)
                pool.affine_select(out=causal[:, :], in_=causal[:, :], compare_op=ALU.is_ge, fill=0.0,
                                   base=0, pattern=[[1, P]], channel_multiplier=-1).then_inc(s_cz, 1)
                pool.memset(v1[:, :, :, HD:VW], 0.0).then_inc(s_vz, 1)
                pool.wait_ge(s_vz, 1)
                pool.memset(v1[:, :, :, HD:HD + 1], 1.0).then_inc(s_vz, 1)

                def scale(m, t, par):
                    wait(pool, summed[m], t + 1)
                    e = feat[m][:, par].rearrange("p h (s f) -> p (h s) f", s=2)
                    nc.gpsimd.tensor_tensor(e, e, fsum[:, m].unsqueeze(2).broadcast_to([P, 2 * H, HD]),
                                            ALU.mult).then_inc(scaled[m], 1)

                scale(0, 0, 0)
                scale(1, 0, 0)
                scale(0, 1, 1)

                def batch(b, last):
                    for c in range(TB):
                        if not (last and c == TB - 1):
                            scale(1, TB * b + c + 1, (c + 1) % 2)
                        if not (last and c >= TB - 2):
                            scale(0, TB * b + c + 2, c % 2)

                batch(0, False)
                with pool.Fori(1, B - 1) as b:
                    batch(b, False)
                batch(B - 1, True)

            @block.tensor
            def _(pe):
                pe.wait_ge(s_id, 2)
                def w_transposes(r):
                    m, j = r // 4, 2 * (r % 4)
                    pe.wait_ge(s_w[m], 16)
                    if r >= 2:
                        wait(pe, w_ev, r - 1)
                    for i in range(4):
                        col = P * (j + i // 2)
                        ins = pe.transpose(pT[r % 2][:, P * i:P * i + P],
                                           w_raw[:, m, i % 2, col:col + P], ident[:, :])
                    ins.then_inc(w_tr, 1)

                def w_products(r):
                    m, j = r // 4, 2 * (r % 4)
                    pe.wait_ge(s_kd[m], 32)
                    wait(pe, w_ev, r + 1)
                    if r >= 2:
                        wait(pe, w_cp, r - 1)
                    out = (pP[:, 0:512], pP[:, 512:1024])[r % 2]
                    for i in range(4):
                        ins = pe.matmul(out[:, P * i:P * i + P], w_t[:, r % 2, i, :],
                                        k_diag[:, m, j + i // 2, :], start=True, stop=True)
                    ins.then_inc(w_mm, 1)

                w_transposes(0)
                for r in range(ROUNDS):
                    if r + 1 < ROUNDS:
                        w_transposes(r + 1)
                    w_products(r)
                pe.wait_ge(w_cp, ROUNDS)

                def x_transposes(t):
                    wait(pe, xn_ready, t + 1)
                    wait(pe, x1_done, t - 2)
                    for k in range(KD):
                        ins = pe.transpose(x_ps[:, P * k:P * k + P], xn[:, P * k:P * k + P], ident[:, :])
                    ins.then_inc(x_tr, 1)

                def project(w, half, par, done):
                    for k in range(KD):
                        ins = pe.matmul(pP[:, 512 * half:512 * half + 512], xT[:, par, k, :],
                                        w[:, k, 512 * half:512 * half + 512],
                                        start=(k == 0), stop=(k == KD - 1))
                    ins.then_inc(done, 1)

                def project_k(t, half, par):
                    wait(pe, xT_ready, t + 1)
                    wait(pe, v_copied, 2 * t - 1 + half)
                    project(w_feat[:, 0], half, par, proj[0])

                def project_q(t, half, par):
                    wait(pe, shifted[0], 2 * t + half + 1)
                    project(w_feat[:, 1], half, par, proj[1])

                def project_v(t, half, par):
                    wait(pe, shifted[1], 2 * t + half + 1)
                    project(wv, half, par, v_proj)

                def transposes(t, g, par):
                    for m in (1, 0):
                        if g == 0:
                            wait(pe, f_ready[m], t + 1)
                            wait(pe, oT_ready, 2 * t)
                        wait(pe, fT_ready[m], 4 * t + g)
                        for h in range(G):
                            ins = pe.transpose(pT[m][:, P * h:P * h + P], feat[m][:, par, G * g + h, :],
                                               ident[:, :])
                        ins.then_inc(f_tr[m], 1)

                def chunk_scores(t, g):
                    wait(pe, fT_ready[0], 4 * t + g + 1)
                    wait(pe, fT_ready[1], 4 * t + g + 1)
                    wait(pe, a_masked, 4 * t + g)
                    for h in range(G):
                        ins = pe.matmul(pA[:, h, :], fT[0][:, g % 2, h, :], fT[1][:, g % 2, h, :],
                                        start=True, stop=True)
                    ins.then_inc(a_done, 1)

                def state_delta(b, c, g, par):
                    wait(pe, v_copied, 2 * (TB * b + c) + 2)
                    wait(pe, s_upd, 12 * b + 4 * c + g)
                    for h in range(G):
                        ins = pe.matmul(d_ps[:, h, :], feat[0][:, par, G * g + h, :],
                                        v1[:, par, G * g + h, :], start=True, stop=True)
                    ins.then_inc(d_done, 1)

                def outputs(b, c, g, par):
                    t = TB * b + c
                    wait(pe, v_copied, 2 * t + 2)
                    wait(pe, o_norm, 4 * t + g)
                    if c:
                        wait(pe, s_upd, 12 * b + 4 * (c - 1) + g + 1)
                    wait(pe, a_masked, 4 * t + g + 1)
                    for h in range(G):
                        if c:
                            pe.matmul(o_ps[:, h, :], fT[1][:, g % 2, h, :], state[:, G * g + h, :],
                                      start=True, stop=False)
                        ins = pe.matmul(o_ps[:, h, :], am[:, g % 2, h, :], v1[:, par, G * g + h, :],
                                        start=(c == 0), stop=True)
                    ins.then_inc(o_done, 1)

                def o_transposes(t):
                    wait(pe, o_norm, 4 * t + 4)
                    for half in range(2):
                        wait(pe, fT_ready[half], 4 * t + 4)
                        for j in range(4):
                            col = P * (4 * half + j)
                            ins = pe.transpose(pT[half][:, P * j:P * j + P], o_sb[:, col:col + P],
                                               ident[:, :])
                        ins.then_inc(o_tr, 1)

                def out_product(t, xT_count):
                    wait(pe, oT_ready, 2 * t + 2)
                    wait(pe, xT_ready, xT_count)
                    wait(pe, x1_done, t)
                    for j in range(H // 2):
                        ins = pe.matmul(y_ps, oT[:, j, :], wo[:, j, :], start=(j == 0), stop=(j == H // 2 - 1))
                    ins.then_inc(y_done, 1)

                x_transposes(0)
                for half in range(2):
                    project_k(0, half, 0)
                for half in range(2):
                    project_q(0, half, 0)
                pe.wait_ge(s_wv, 16)
                for half in range(2):
                    project_v(0, half, 0)
                x_transposes(1)
                for half in range(2):
                    project_k(1, half, 1)
                transposes(0, 0, 0)
                chunk_scores(0, 0)
                pe.wait_ge(s_wo, 16)

                def batch(b, last):
                    for c in range(TB):
                        t, par = TB * b + c, c % 2
                        has1, has2 = not (last and c == TB - 1), not (last and c >= TB - 2)
                        for g in range(G):
                            if g == G - 1 and has2:
                                x_transposes(t + 2)
                            if g < G - 1:
                                transposes(t, g + 1, par)
                            if has1:
                                if g < 2:
                                    project_q(t + 1, g, 1 - par)
                                else:
                                    project_v(t + 1, g - 2, 1 - par)
                            if g < G - 1:
                                chunk_scores(t, g + 1)
                            if c < TB - 1:
                                state_delta(b, c, g, par)
                            outputs(b, c, g, par)
                        if has2:
                            project_k(t + 2, 0, par)
                        o_transposes(t)
                        if has2:
                            project_k(t + 2, 1, par)
                        if has1:
                            transposes(t + 1, 0, 1 - par)
                        out_product(t, t + 3 if has2 else T)
                        if has1:
                            chunk_scores(t + 1, 0)

                batch(0, False)
                with pe.Fori(1, B - 1) as b:
                    batch(b, False)
                batch(B - 1, True)

            @block.scalar
            def _(act):
                def w_t_copy(r):
                    wait(act, w_tr, r + 1)
                    if r >= 2:
                        wait(act, w_mm, r - 1)
                    nc.scalar.copy(w_t[:, r % 2], pT[r % 2][:, :].rearrange("p (i n) -> p i n", i=4)
                                   ).then_inc(w_ev, 1)

                w_t_copy(0)
                for r in range(ROUNDS):
                    if r + 1 < ROUNDS:
                        w_t_copy(r + 1)
                    wait(act, w_mm, r + 1)
                    m, col = r // 4, 2 * P * (r % 4)
                    nc.scalar.copy(
                        w_feat[:, m, :, col:col + 2 * P].rearrange("p k (j n) -> p j k n", j=2),
                        pP[:, 512 * (r % 2):512 * (r % 2) + 512].rearrange("p (j k n) -> p j k n", j=2, k=KD)
                    ).then_inc(w_cp, 1)
                act.wait_ge(s_var, 1)
                nc.scalar.activation(rstd[:, :], rstd[:, :], ACT.Sqrt).then_inc(s_std, 1)

                def x_copy(t, par):
                    wait(act, x_tr, t + 1)
                    wait(act, v_proj, 2 * (t - 1))
                    nc.scalar.copy(xT[:, par], x_ps.rearrange("p (k n) -> p k n", k=KD)).then_inc(xT_ready, 1)

                def exponentials(m, t, half, par):
                    wait(act, shifted[m], 2 * t + half + 1)
                    e = feat[m][:, par, 8 * half:8 * half + 8, :]
                    nc.scalar.activation(e, e, ACT.Exp).then_inc(expd[m], 1)

                def v_copy(t, half, par):
                    wait(act, v_proj, 2 * t + half + 1)
                    wait(act, o_done, 4 * (t - 1))
                    wait(act, s_vz, 2)
                    nc.scalar.copy(v1[:, par, 8 * half:8 * half + 8, 0:HD],
                                   pP[:, 512 * half:512 * half + 512].rearrange("p (h d) -> p h d", h=H // 2)
                                   ).then_inc(v_copied, 1)

                def f_copies(t, g):
                    for m in (1, 0):
                        wait(act, f_tr[m], 4 * t + g + 1)
                        wait(act, o_done, 4 * t + g - 1)
                        nc.scalar.copy(fT[m][:, g % 2], pT[m][:, :].rearrange("p (h n) -> p h n", h=G)
                                       ).then_inc(fT_ready[m], 1)

                x_copy(0, 0)
                for m in range(2):
                    for half in range(2):
                        exponentials(m, 0, half, 0)
                for half in range(2):
                    v_copy(0, half, 0)
                x_copy(1, 1)
                for half in range(2):
                    exponentials(0, 1, half, 1)
                f_copies(0, 0)

                def batch(b, last):
                    for c in range(TB):
                        t, par = TB * b + c, c % 2
                        has1, has2 = not (last and c == TB - 1), not (last and c >= TB - 2)
                        f_copies(t, 1)
                        f_copies(t, 2)
                        if has1:
                            exponentials(1, t + 1, 0, 1 - par)
                            exponentials(1, t + 1, 1, 1 - par)
                        f_copies(t, 3)
                        if has1:
                            v_copy(t + 1, 0, 1 - par)
                        if has2:
                            x_copy(t + 2, par)
                        if has1:
                            v_copy(t + 1, 1, 1 - par)
                        for half in range(2):
                            wait(act, o_tr, 2 * t + half + 1)
                            wait(act, y_done, t)
                            nc.scalar.copy(oT[:, 4 * half:4 * half + 4, :],
                                           pT[half][:, :].rearrange("p (j n) -> p j n", j=4)
                                           ).then_inc(oT_ready, 1)
                        if has2:
                            exponentials(0, t + 2, 0, par)
                        if has1:
                            f_copies(t + 1, 0)
                        if has2:
                            exponentials(0, t + 2, 1, par)

                batch(0, False)
                with act.Fori(1, B - 1) as b:
                    batch(b, False)
                batch(B - 1, True)

            @block.vector
            def _(dve):
                own = Chain(dve, s_dve)
                for t in range(T):
                    if t % TB == 0:
                        dve.wait_ge(s_x[t // TB], 16)
                    own.did(nc.vector.bn_stats(stats[:, t, :], xr[:, t, :]))
                own.wait()
                for t in range(T):
                    own.did(nc.vector.bn_aggr(mv[:, t, :], stats[:, t, :]))
                own.wait()
                nc.vector.tensor_scalar(rstd[:, :], mv[:, :, 1], LN_EPS, None, ALU.add).then_inc(s_var, 1)
                dve.wait_ge(s_std, 1)
                own.did(nc.vector.reciprocal(rstd[:, :], rstd[:, :]))
                own.wait()

                def normalise(t):
                    wait(dve, x_tr, t)
                    nc.vector.tensor_scalar(xn[:, :], xr[:, bass.ds(t, 1), :].rearrange("p a d -> p (a d)"),
                                            mv[:, bass.ds(t, 1), 0], rstd[:, bass.ds(t, 1)],
                                            ALU.subtract, ALU.mult).then_inc(xn_ready, 1)

                normalise(0)
                def shift(m, t, half, par, own):
                    hs = slice(8 * half, 8 * half + 8)
                    f = pP[:, 512 * half:512 * half + 512].rearrange("p (h f) -> p h f", h=H // 2)
                    wait(dve, proj[m], 2 * t + half + 1)
                    wait(dve, o_done, 4 * (t - 1))
                    own.did(nc.vector.tensor_reduce(hi[:, m, hs], f, AX_X, ALU.max))
                    own.did(nc.vector.tensor_reduce(lo[:, m, hs], f, AX_X, ALU.min))
                    own.wait()
                    nc.vector.tensor_tensor(feat[m][:, par, hs, 0:HD], f,
                                            hi[:, m, hs].unsqueeze(2).broadcast_to([P, H // 2, HD]), ALU.subtract)
                    nc.vector.tensor_tensor(feat[m][:, par, hs, HD:F2],
                                            lo[:, m, hs].unsqueeze(2).broadcast_to([P, H // 2, HD]), f,
                                            ALU.subtract).then_inc(shifted[m], 1)

                def denominators(m, t, par, own):
                    wait(dve, expd[m], 2 * t + 2)
                    wait(dve, scaled[m], t)
                    own.did(nc.vector.tensor_reduce(
                        fsum[:, m], feat[m][:, par].rearrange("p h (s f) -> p (h s) f", s=2), AX_X, ALU.add))
                    own.wait()
                    nc.vector.reciprocal(fsum[:, m], fsum[:, m]).then_inc(summed[m], 1)

                def clamp(m, t, par):
                    wait(dve, scaled[m], t + 1)
                    nc.vector.tensor_scalar(feat[m][:, par], feat[m][:, par], FEAT_EPS, None,
                                            ALU.max).then_inc(f_ready[m], 1)

                def mask(t, g):
                    wait(dve, a_done, 4 * t + g + 1)
                    wait(dve, o_done, 4 * t + g - 1)
                    nc.vector.tensor_tensor(am[:, g % 2], pA[:, :, :],
                                            causal[:, :].unsqueeze(1).broadcast_to([P, G, P]),
                                            ALU.mult).then_inc(a_masked, 1)

                def update(b, c, g):
                    wait(dve, d_done, 12 * b + 4 * c + g + 1)
                    wait(dve, o_done, 4 * (TB * b + c) + g + 1)
                    st = state[:, G * g:G * g + G, :]
                    if c == 0:
                        nc.vector.tensor_copy(st, d_ps).then_inc(s_upd, 1)
                    else:
                        nc.vector.tensor_tensor(st, st, d_ps, ALU.add).then_inc(s_upd, 1)

                def normalise_o(t, g, own):
                    wait(dve, o_done, 4 * t + g + 1)
                    if g == 0:
                        wait(dve, o_tr, 2 * t)
                    own.did(nc.vector.tensor_scalar(z[:, :], o_ps[:, :, HD], FEAT_EPS, None, ALU.add))
                    own.wait()
                    own.did(nc.vector.reciprocal(rz[:, :], z[:, :]))
                    own.wait()
                    nc.vector.tensor_tensor(
                        o_sb[:, 256 * g:256 * g + 256].rearrange("p (h d) -> p h d", h=G),
                        o_ps[:, :, 0:HD], rz[:, :].unsqueeze(2).broadcast_to([P, G, HD]),
                        ALU.mult).then_inc(o_norm, 1)

                def residual(t):
                    wait(dve, y_done, t + 1)
                    xt = xr[:, bass.ds(t, 1), :].rearrange("p a d -> p (a d)")
                    nc.vector.tensor_tensor(xt, xt, y_ps, ALU.add).then_inc(x1_done, 1)

                for m in range(2):
                    for half in range(2):
                        shift(m, 0, half, 0, own)
                    if m == 0:
                        denominators(0, 0, 0, own)
                        normalise(1)
                denominators(1, 0, 0, own)
                clamp(0, 0, 0)
                shift(0, 1, 0, 1, own)
                clamp(1, 0, 0)
                shift(0, 1, 1, 1, own)
                denominators(0, 1, 1, own)
                dve.wait_ge(s_cz, 2)
                mask(0, 0)
                before = own.n

                def batch(b, last):
                    own = Chain(dve, s_dve, DVE_BATCH * b + before)
                    for c in range(TB):
                        t, par = TB * b + c, c % 2
                        has1, has2 = not (last and c == TB - 1), not (last and c >= TB - 2)
                        for g in range(G):
                            if g == 1 and has1:
                                shift(1, t + 1, 1, 1 - par, own)
                            if g == 2 and has1:
                                denominators(1, t + 1, 1 - par, own)
                            if g < G - 1:
                                mask(t, g + 1)
                            if g == 0 and has1:
                                shift(1, t + 1, 0, 1 - par, own)
                            if g == 1 and has1:
                                clamp(0, t + 1, 1 - par)
                            if c < TB - 1:
                                update(b, c, g)
                            normalise_o(t, g, own)
                            if g == 0 and has2:
                                normalise(t + 2)
                            if g == 2 and has1:
                                clamp(1, t + 1, 1 - par)
                        if has2:
                            shift(0, t + 2, 0, par, own)
                            shift(0, t + 2, 1, par, own)
                            denominators(0, t + 2, par, own)
                        residual(t)
                        if has1:
                            mask(t + 1, 0)
                    assert last or own.n == DVE_BATCH, own.n

                batch(0, False)
                with dve.Fori(1, B - 1) as b:
                    batch(b, False)
                batch(B - 1, True)


CD = 192
CS = CD // 2
M = 1024
JT = M // P
XH, XD = 16, 16
XV = 32
PAIRS = ((0, 0), (0, 1), (1, 0), (1, 1), (0, 2), (2, 0))
AUG = XD * len(PAIRS)
KR = AUG + 4
MASKED = 1e30
NG = B * G


def cross_attention(nc, ctx_in, mask, Wq, Wk, Wv, Wo, k_scr, q_scr, aug_scr, xr, stats, ks, qs,
                    w1, b1, w1_sb, b1_sb):
    with ExitStack() as ctx:
        def sb(name, shape, dt=F32):
            return ctx.enter_context(nc.sbuf_tensor(name, shape, dt))

        def ps(name, shape, dt=F32):
            return ctx.enter_context(nc.psum_tensor(name, shape, dt))

        def sem(name):
            return ctx.enter_context(nc.semaphore("b_" + name))

        ident = sb("b_ident", [P, P])
        ident_h = sb("b_ident_h", [P, P], BF16)
        wq = sb("b_wq", [P, KD, D])
        wo = sb("b_wo", [P, KD, D])
        wk = sb("b_wk", [CS, 2, D])
        wv = sb("b_wv", [CS, 2, D])
        m_col = sb("m_col", [P, B, JT], U8)
        any_on = sb("any_on", [P, B])
        big = sb("big", [P, B])
        q_scale = sb("q_scale", [P, B])
        bias = sb("bias", [P, G, JT])
        last_row = sb("last_row", [P, 1])
        other_rows = sb("other_rows", [P, 1])
        row_gain = sb("row_gain", [P, B])
        row_base = sb("row_base", [P, B])
        q_aug = sb("q_aug", [P, L], BF16)
        mv = sb("b_mv", [P, T, 2])
        rstd = sb("b_rstd", [P, T])
        xn = sb("b_xn", [P, TB, D])
        xT = sb("b_xT", [P, KD, L])
        cx = sb("cx", [P, JT, CD])
        cT = sb("cT", [CS, 2, M])
        rest = sb("rest", [P, 512])
        zero = sb("b_zero", [P, 1])
        parts = sb("parts", [P, 2, 3, 2, 512], BF16)
        v_new = sb("v_new", [P, G, JT, G * XD])
        v1 = sb("b_v1", [P, G, JT, G, XV])
        neg_max = sb("neg_max", [P, 2, TB, G])
        max_rest = sb("max_rest", [P, TB, G])
        max_parts = sb("max_parts", [P, TB, G, XV], BF16)
        pt = sb("pt", [P, 2, G, L])
        ot = sb("ot", [P, L])
        rz = sb("b_rz", [P, TB, G])
        o = sb("b_o", [P, TB, D])
        oT = xT
        m_row = qs[:, 1, 0:4, :].rearrange("p h n -> p (h n)").bitcast(U8).rearrange("p (b m) -> p b m", b=B)
        k_aug = ks[:, 1, 0:B, :]

        pS1 = ps("pS1", [P, 2, M])
        pS2 = ps("pS2", [P, 2, L])
        pO = ps("b_pO", [P, L])
        pM = ps("pM", [P, 512])

        s_wk, s_scale, s_w, s_mask, s_cx, s_id = sem("wk"), sem("scale"), sem("w"), sem("mask"), sem("cx"), sem("ident")
        s_dve, s_act = sem("dve"), sem("act")
        s_z, s_row, s_var, s_std, s_aug = sem("zero"), sem("row"), sem("var"), sem("std"), sem("aug")
        xn_ready = sem("xn")
        filled, emptied = sem("filled"), sem("emptied")
        head_done, rounded, split_done = sem("head"), sem("rounded"), sem("split")
        stored = [sem("k0_stored"), sem("k1_stored"), sem("q_stored")]
        aug_stored = sem("aug_stored")
        next_loaded, first_loaded, k_loaded, q_loaded = sem("next_loaded"), sem("first_loaded"), sem("k_loaded"), sem("q_loaded")
        placed = sem("placed")
        s1_done, max_done = sem("s1"), sem("max")
        m_ready, m_copied = sem("m_ready"), sem("m_copied")
        s2_done, exp_done, av_done, ot_ready = sem("s2"), sem("exp"), sem("av"), sem("ot")

        N_LOAD = 16 * (len(PAIRS) + 1)

        def small_steps(hg, j, first, last):
            plan = {(0, 2): [("o_turn", 3)] * (not first)}
            for g in range(1, G):
                plan[g, 2] = [("o_turn", g - 1)]
            if not first:
                plan[0, 3], plan[0, 4] = [("oT", 0)], [("oT", 1)]
                plan[0, 5], plan[0, 6] = [("y", 0)], [("y", 1)]
            for g in range(G):
                plan[g, 6] = plan.get((g, 6), []) + [("m_turn", g + 1)] * (g < G - 1 or not last)
            if not last:
                plan[0, 0], plan[0, 1], plan[0, 7], plan[1, 0] = [[("cT", i)] for i in range(4)]
                plan[1, 1], plan[1, 3], plan[1, 4] = [("k", 0)], [("k", 2)], [("k", 3)]
                plan[1, 2] = plan[1, 2] + [("k", 1)]
                plan[1, 5], plan[1, 6] = [("xT", 0)], [("xT", 1)] + plan[1, 6]
                plan[1, 7], plan[2, 0] = [("q", 0)], [("q", 1)]
                plan[2, 1], plan[2, 3], plan[2, 4], plan[2, 5] = [[("v", i)] for i in range(4)]
            return plan.get((hg, j), [])

        PREPARE = [("cT", i) for i in range(4)] + [("k", i) for i in range(4)] + \
            [("xT", 0), ("xT", 1), ("q", 0), ("q", 1)] + [("v", i) for i in range(4)]
        free_banks = [pM, pO, pS2[:, 0, :], pS2[:, 1, :]]

        def prepare_wait(n):
            kind, i = PREPARE[n]
            return n - i
        FINISH = [("o_turn", 3, pM, 0), ("oT", 0, pS2[:, 0, :], 1), ("oT", 1, pS2[:, 1, :], 1),
                  ("y", 0, pM, 3), ("y", 1, pS2[:, 0, :], 3)]

        OWN_FIRST, OWN_MIDDLE = 15, 16

        def slot(b, n):
            return bass.ds((3 * b + n) % 2, 1)

        def batch_of(b, kind, i, hg):
            if kind in ("cT", "k", "v", "xT", "q"):
                return b + 1
            return b - 1 if kind in ("oT", "y") or (kind == "o_turn" and i > hg) else b

        def steps_of(first, last):
            return sum(len(small_steps(g, j, first, last)) for g in range(G) for j in range(JT))

        START = len(PREPARE) + 1
        FIRST, MIDDLE = steps_of(True, False), steps_of(False, False)

        def steps_before(b):
            return (b - 1) * MIDDLE + (START + FIRST)

        def score_units(hg, j, last):
            ahead, u = (hg + 1, 2 * j + 4) if j < 6 else (hg + 2, 2 * j - 12)
            if ahead >= G and last:
                return []
            return [(ahead // G, ahead % G, u), (ahead // G, ahead % G, u + 1)]

        with nc.Block() as block:

            @block.sync
            def _(sp):
                def load_cx(b):
                    sp.dma_start(cx[:, :, :], ctx_in[b].rearrange("(j p) c -> p j c", p=P)).then_inc(s_cx, 16)

                def load_k(b, heads, done):
                    for s, pair in enumerate(PAIRS):
                        sp.dma_start(ks[XD * s:XD * s + XD, b % 2, heads],
                                     k_scr[b, pair[1]].rearrange("(h d) n -> d h n", d=XD)[:, heads]).then_inc(done, 16)

                def load_k_aug(b, heads, done):
                    sp.dma_start(ks[AUG:KR, b % 2, heads],
                                 aug_scr[b].unsqueeze(1).broadcast_to([4, heads.stop - heads.start, M])
                                 ).then_inc(done, 16)

                def load_q(b, heads, done):
                    for s, pair in enumerate(PAIRS):
                        sp.dma_start(qs[XD * s:XD * s + XD, b % 2, heads],
                                     q_scr[b, pair[0]].rearrange("(h d) n -> d h n", d=XD)[:, heads]).then_inc(done, 16)
                    sp.dma_start(qs[AUG:KR, b % 2, heads],
                                 q_aug[AUG:KR, :].unsqueeze(1).broadcast_to([4, heads.stop - heads.start, L])
                                 ).then_inc(done, 16)

                def store_k(b):
                    for half in range(2):
                        n = 3 * b + half
                        wait(sp, split_done, 2 * (n + 1))
                        for c in range(3):
                            sp.dma_start(k_scr[b, c].rearrange("(m p) n -> p m n", p=P)[:, :, 512 * half:512 * half + 512],
                                         parts[:, n % 2, c]).then_inc(stored[half], 16)
                    for half in range(2):
                        wait(sp, stored[half], 48 * (b + 1))

                def store_q(b):
                    n = 3 * b + 2
                    wait(sp, split_done, 2 * (n + 1))
                    for c in range(3):
                        sp.dma_start(q_scr[b, c].rearrange("(m p) n -> p m n", p=P),
                                     parts[:, n % 2, c]).then_inc(stored[2], 16)
                    wait(sp, stored[2], 48 * (b + 1))

                load_cx(0)
                for w, src in ((wk, Wk), (wv, Wv)):
                    sp.dma_start(w[:, :, :], src.rearrange("(s p) n -> p s n", p=CS)).then_inc(s_wk, 16)
                flat = mask.rearrange("b m -> (b m)").unsqueeze(0)
                sp.dma_start(m_row.rearrange("p b m -> p (b m)"),
                             flat.broadcast_to([P, B * M])).then_inc(s_mask, 16)
                with nc.allow_non_contiguous_dma(reason="4096 bytes of the mask"):
                    sp.dma_start(m_col[:, :, :], mask.rearrange("b (j p) -> p b j", p=P)).then_inc(s_mask, 16)
                for w, src in ((wq, Wq), (wo, Wo)):
                    sp.dma_start(w[:, :, :], src.rearrange("(k p) n -> p k n", p=P)).then_inc(s_w, 16)
                wait(sp, filled, 4)
                load_cx(1)
                now, later, every = slice(0, G), slice(G, XH), slice(0, XH)
                store_k(0)
                load_k(0, now, first_loaded)
                sp.wait_ge(s_aug, B + 1)
                for b in range(B):
                    sp.dma_start(aug_scr[b], k_aug[AUG:KR, b]).then_inc(aug_stored, 16)
                sp.wait_ge(aug_stored, 16 * B)
                load_k_aug(0, now, first_loaded)
                store_q(0)
                load_q(0, now, first_loaded)
                load_k(0, later, k_loaded)
                load_k_aug(0, later, k_loaded)
                load_q(0, later, q_loaded)
                for b in range(1, B):
                    n = sum(len(small_steps(0, j, b == 1, False)) for j in range(JT)) + 1
                    if b + 1 < B:
                        wait(sp, filled, n + (START if b == 1 else steps_before(b - 1)))
                        load_cx(b + 1)
                    store_k(b)
                    wait(sp, s2_done, G * JT * G * (b - 1))
                    load_k(b, every, k_loaded)
                    load_k_aug(b, every, k_loaded)
                    store_q(b)
                    load_q(b, every, q_loaded)

                sp.wait_ge(s2_done, G * JT * G * (B - 1))
                for k in range(KD):
                    sp.dma_start(w1_sb[:, :, k, :], w1[:, P * k:P * k + P, :].rearrange("e p h -> p e h")
                                 ).then_inc(next_loaded, 16)
                sp.dma_start(b1_sb[:, :, :].rearrange("p e h -> p (e h)"),
                             b1.rearrange("e h -> (e h)").unsqueeze(0).broadcast_to([P, E_ * FH])).then_inc(next_loaded, 16)
                sp.wait_ge(next_loaded, 16 * (KD + 1))

            @block.gpsimd
            def _(pool):
                make_identity(pool, ident[:, :], s_id)
                pool.memset(last_row[:, :], 0.0).then_inc(s_row, 1)
                pool.wait_ge(s_row, 1)
                pool.affine_select(out=last_row[:, :], in_=last_row[:, :], compare_op=ALU.not_equal, fill=1.0,
                                   base=-(KR - 1), pattern=[[0, 1]], channel_multiplier=1).then_inc(s_row, 1)
                pool.memset(q_aug[:, :], 0.0).then_inc(s_row, 1)
                pool.memset(max_parts[:, :, :, :], 0.0).then_inc(s_z, 1)
                pool.memset(v1[:, :, :, :, XD:XV], 0.0).then_inc(s_z, 1)
                pool.wait_ge(s_z, 2)
                pool.memset(v1[:, :, :, :, XD:XD + 1], 1.0).then_inc(s_z, 1)
                pool.memset(zero[:, :], 0.0).then_inc(s_z, 1)
                pool.wait_ge(s_z, 4)

                def split(b, kind, i, n):
                    s, m = (slot(b, i // 2), i % 2) if kind == "k" else (slot(b, 2), i)
                    part = [parts[:, s, c, m, :].rearrange("p a n -> p (a n)") for c in range(3)]
                    wait(pool, emptied, n + 1)
                    nc.gpsimd.tensor_tensor(part[1], rest[:, :], zero[:, :].broadcast_to([P, 512]), ALU.add
                                            ).then_inc(rounded, 1)
                    wait(pool, rounded, 6 * (b - 1) + (i if kind == "k" else 4 + i) + 1)
                    nc.gpsimd.tensor_tensor(part[2], rest[:, :], part[1], ALU.subtract).then_inc(split_done, 1)

                def batch(b, start, first):
                    n = 0
                    for hg in range(G):
                        for j in range(JT):
                            for kind, i in small_steps(hg, j, first, False):
                                if kind in ("k", "q"):
                                    split(batch_of(b, kind, i, hg), kind, i, start + n)
                                n += 1

                batch(0, START, True)
                with pool.Fori(1, B - 1) as b:
                    batch(b, steps_before(b), False)

            @block.tensor
            def _(pe):
                def small(b, kind, i, n, pM=pM, before=None):
                    wait(pe, emptied, n if before is None else before)
                    if kind == "cT":
                        wait(pe, s_cx, 16 * (b + 1))
                        for q in range(4):
                            j, s = 2 * i + q // 2, q % 2
                            ins = pe.transpose(pM[0:CS, P * q:P * q + P], cx[:, j, CS * s:CS * s + CS],
                                               ident[:, :])
                    elif kind == "k":
                        pe.wait_ge(s_wk, 32)
                        half, m = i // 2, i % 2
                        for s in range(2):
                            ins = pe.matmul(pM[:, :], wk[:, s, P * m:P * m + P],
                                            cT[:, s, 512 * half:512 * half + 512],
                                            start=(s == 0), stop=(s == 1))
                    elif kind == "v":
                        for q in range(2):
                            j = 2 * i + q
                            for s in range(2):
                                ins = pe.matmul(pM[:, D * q:D * q + D], cT[:, s, P * j:P * j + P],
                                                wv[:, s, :], start=(s == 0), stop=(s == 1))
                    elif kind == "xT":
                        wait(pe, xn_ready, b + 1)
                        for q in range(4):
                            t, k = 2 * i + q // 2, q % 2
                            ins = pe.transpose(pM[:, P * q:P * q + P], xn[:, t, P * k:P * k + P],
                                               ident[:, :])
                    elif kind == "q":
                        pe.wait_ge(s_w, 32)
                        for k in range(KD):
                            ins = pe.matmul(pM[:, :], wq[:, k, P * i:P * i + P], xT[:, k, :],
                                            start=(k == 0), stop=(k == KD - 1))
                    elif kind == "m_turn":
                        wait(pe, m_ready, G * b + i + 1)
                        for t in range(TB):
                            ins = pe.transpose(pM[:, 64 * t:64 * t + 64].bitcast(BF16),
                                               max_parts[:, t, :, :].rearrange("p h v -> p (h v)"),
                                               ident_h[:, :])
                    elif kind == "o_turn":
                        wait(pe, ot_ready, G * b + i + 1)
                        for t in range(TB):
                            ins = pe.transpose(pM[:, P * t:P * t + P], ot[:, P * t:P * t + P], ident[:, :])
                    elif kind == "oT":
                        for t in range(TB):
                            ins = pe.transpose(pM[:, P * t:P * t + P], o[:, t, P * i:P * i + P], ident[:, :])
                    elif kind == "y":
                        for q in range(2):
                            t = 2 * i + q
                            for k in range(KD):
                                ins = pe.matmul(pM[:, D * q:D * q + D], oT[:, k, P * t:P * t + P],
                                                wo[:, k, :], start=(k == 0), stop=(k == KD - 1))
                    ins.then_inc(filled, 1)

                def scores_by_token(b, hg, u):
                    U = 16 * (G * b + hg) + u
                    t, h, slot = u // G, G * hg + u % G, u % 2
                    if isinstance(b, int) and (b, hg, u) == (0, 0, 0):
                        wait(pe, first_loaded, 2 * N_LOAD)
                    elif u == 0 and hg == (1 if isinstance(b, int) and b == 0 else 0):
                        wait(pe, k_loaded, N_LOAD * (b + 1))
                        wait(pe, q_loaded, N_LOAD * (b + 1))
                    wait(pe, max_done, U - 1)
                    par = b % 2
                    for half in range(2):
                        ins = pe.matmul(
                            pS1[:, slot, 512 * half:512 * half + 512],
                            qs[0:KR, bass.ds(par, 1), h, P * t:P * t + P].rearrange("r a n -> r (a n)"),
                            ks[0:KR, bass.ds(par, 1), h, 512 * half:512 * half + 512
                               ].rearrange("r a n -> r (a n)"), start=True, stop=True)
                    ins.then_inc(s1_done, 1)

                def scores_by_context(b, hg, j, i, steps):
                    n = G * (JT * (G * b + hg) + j) + i
                    if j == 0 and i == 0:
                        wait(pe, emptied, steps)
                    wait(pe, exp_done, n - 1)
                    par, h = b % 2, G * hg + i
                    pe.matmul(pS2[:, i % 2, :],
                              ks[0:KR, bass.ds(par, 1), h, P * j:P * j + P].rearrange("r a n -> r (a n)"),
                              qs[0:KR, bass.ds(par, 1), h, :].rearrange("r a n -> r (a n)"),
                              start=True, stop=True).then_inc(s2_done, 1)

                def weighted_values(b, hg, j):
                    n = G * b + hg
                    wait(pe, exp_done, G * (JT * n + j + 1))
                    if j == 0:
                        wait(pe, ot_ready, n)
                        wait(pe, placed, n + 1)
                    for i in range(G):
                        ins = pe.matmul(pO[XV * i:XV * i + XV, :], v1[:, hg, j, i, :], pt[:, j % 2, i, :],
                                        start=(j == 0), stop=(j == JT - 1))
                    ins.then_inc(av_done, 1)

                pe.wait_ge(s_id, 3)
                for n, (kind, i) in enumerate(PREPARE):
                    small(0, kind, i, n, free_banks[i], prepare_wait(n))
                pe.wait_ge(s_z, 3)
                for u in range(16):
                    scores_by_token(0, 0, u)
                small(0, "m_turn", 0, START - 1)
                for u in range(4):
                    scores_by_token(0, 1, u)

                def batch(b, start, first, last):
                    n = 0
                    for hg in range(G):
                        for j in range(JT):
                            units = score_units(hg, j, last)
                            for i in range(G):
                                scores_by_context(b, hg, j, i, start + n)
                                if i == 1:
                                    for ahead, g, u in units[:1]:
                                        scores_by_token(b + ahead, g, u)
                                    if j:
                                        weighted_values(b, hg, j - 1)
                                    elif hg:
                                        weighted_values(b, hg - 1, JT - 1)
                                    elif not first:
                                        weighted_values(b - 1, G - 1, JT - 1)
                                    for kind, k in small_steps(hg, j, first, last)[:-1]:
                                        small(batch_of(b, kind, k, hg), kind, k, start + n)
                                        n += 1
                            for ahead, g, u in units[1:]:
                                scores_by_token(b + ahead, g, u)
                            for kind, i in small_steps(hg, j, first, last)[-1:]:
                                small(batch_of(b, kind, i, hg), kind, i, start + n)
                                n += 1
                    return start + n

                batch(0, START, True, False)
                with pe.Fori(1, B - 1) as b:
                    batch(b, steps_before(b), False, False)
                n = batch(B - 1, steps_before(B - 1), False, True)
                weighted_values(B - 1, G - 1, JT - 1)
                for q, (kind, i, bank, done) in enumerate(FINISH):
                    small(B - 1, kind, i, n + q, bank, n + done)

            @block.scalar
            def _(act):
                act.wait_ge(s_id, 2)
                nc.scalar.copy(ident_h[:, :], ident[:, :]).then_inc(s_id, 1)
                act.wait_ge(s_var, 1)
                nc.scalar.activation(rstd[:, :], rstd[:, :], ACT.Sqrt).then_inc(s_std, 1)

                def small(b, kind, i, n, pM=pM):
                    if kind in ("y", "o_turn"):
                        return
                    wait(act, filled, n + 1)
                    if kind == "cT":
                        nc.scalar.copy(cT[:, :, 2 * P * i:2 * P * i + 2 * P].rearrange("c s (j n) -> c j s n", j=2),
                                       pM[0:CS, :].rearrange("c (j s n) -> c j s n", j=2, s=2)
                                       ).then_inc(emptied, 1)
                    elif kind == "xT":
                        nc.scalar.copy(xT[:, :, 2 * P * i:2 * P * i + 2 * P].rearrange("c k (t n) -> c t k n", t=2),
                                       pM[:, :].rearrange("c (t k n) -> c t k n", t=2, k=2)
                                       ).then_inc(emptied, 1)
                    elif kind == "k":
                        wait(act, stored[1 + i // 2], 48 * b)
                        nc.scalar.copy(parts[:, slot(b, i // 2), 0, i % 2, :].rearrange("p a n -> p (a n)"),
                                       pM[:, :]).then_inc(head_done, 1)
                    elif kind == "q":
                        wait(act, stored[0], 48 * (b + 1))
                        act.wait_ge(s_scale, 1)
                        nc.scalar.activation(parts[:, slot(b, 2), 0, i, :].rearrange("p a n -> p (a n)"), pM[:, :],
                                             ACT.Copy, scale=q_scale[:, bass.ds(b, 1)]).then_inc(head_done, 1)
                    elif kind == "v":
                        if i == 0:
                            wait(act, placed, G * b)
                        nc.scalar.copy(v_new[:, :, 2 * i:2 * i + 2, :].rearrange("p g j c -> p j g c"),
                                       pM[:, :].rearrange("p (j g c) -> p j g c", j=2, g=G)
                                       ).then_inc(emptied, 1)
                    elif kind == "oT":
                        nc.scalar.copy(oT[:, i, :], pM[:, :]).then_inc(emptied, 1)
                    elif kind == "m_turn":
                        bb, g = (b + 1, 0) if i == G else (b, i)
                        act.wait_ge(s_id, 3)
                        for q in range(G // 2):
                            ins = nc.scalar.copy(
                                qs[AUG:KR, bass.ds(bb % 2, 1), G * g + q, :].rearrange("r a n -> r (a n)"),
                                pM[XV * q:XV * q + 4, 0:TB * 64].bitcast(BF16))
                        ins.then_inc(m_copied, 1)

                def exponentials(b, hg, j, between=None):
                    n = JT * (G * b + hg) + j
                    wait(act, av_done, n - 1)
                    if j == 0:
                        wait(act, placed, G * b + hg + 1)
                    for i in range(G):
                        wait(act, s2_done, G * n + i + 1)
                        nc.scalar.activation(pt[:, j % 2, i, :], pS2[:, i % 2, :], ACT.Exp,
                                             bias=bias[:, hg, j:j + 1]).then_inc(exp_done, 1)
                        if i == 1:
                            between()

                def values_copy(n):
                    wait(act, av_done, JT * n)
                    nc.scalar.copy(ot[:, :], pO[:, :]).then_inc(ot_ready, 1)

                for n, (kind, i) in enumerate(PREPARE):
                    small(0, kind, i, n, free_banks[i])
                small(0, "m_turn", 0, START - 1)

                def batch(b, start, first, last):
                    n = 0
                    for hg in range(G):
                        for j in range(JT):
                            def between():
                                nonlocal n
                                if j == 0 and (hg or not first):
                                    values_copy(G * b + hg)
                                for kind, i in small_steps(hg, j, first, last)[:-1]:
                                    small(batch_of(b, kind, i, hg), kind, i, start + n)
                                    n += 1

                            exponentials(b, hg, j, between)
                            for kind, i in small_steps(hg, j, first, last)[-1:]:
                                small(batch_of(b, kind, i, hg), kind, i, start + n)
                                n += 1
                    return start + n

                batch(0, START, True, False)
                with act.Fori(1, B - 1) as b:
                    batch(b, steps_before(b), False, False)
                n = batch(B - 1, steps_before(B - 1), False, True)
                values_copy(NG)
                for q, (kind, i, bank, _done) in enumerate(FINISH):
                    small(B - 1, kind, i, n + q, bank)

            @block.vector
            def _(dve):
                own = Chain(dve, s_dve)

                def small(b, kind, i, n, own, pM=pM, first_batch=False):
                    if kind in ("k", "q"):
                        s, m = (slot(b, i // 2), i % 2) if kind == "k" else (slot(b, 2), i)
                        head = parts[:, s, 0, m, :].rearrange("p a n -> p (a n)")
                        nth = 6 * b + (i if kind == "k" else 4 + i)
                        wait(dve, head_done, nth + 1)
                        wait(dve, split_done, nth)
                        if kind == "k":
                            nc.vector.tensor_tensor(rest[:, :], pM[:, :], head, ALU.subtract
                                                    ).then_inc(emptied, 1)
                        else:
                            nc.vector.scalar_tensor_tensor(rest[:, :], pM[:, :], q_scale[:, bass.ds(b, 1)],
                                                           head, ALU.mult, ALU.subtract).then_inc(emptied, 1)
                        if first_batch:
                            part = [parts[:, s, c, m, :].rearrange("p a n -> p (a n)") for c in range(3)]
                            wait(dve, emptied, n + 1)
                            own.did(nc.vector.tensor_copy(part[1], rest[:, :]))
                            own.wait()
                            nc.vector.tensor_tensor(part[2], rest[:, :], part[1], ALU.subtract).then_inc(split_done, 1)
                    elif kind == "o_turn":
                        wait(dve, filled, n + 1)
                        turned = pM[:, :].rearrange("p (t h v) -> p t h v", t=TB, h=G)
                        own.did(nc.vector.reciprocal(rz[:, :, :], turned[:, :, :, XD]))
                        own.wait()
                        nc.vector.tensor_tensor(
                            o[:, :, G * XD * i:G * XD * i + G * XD].rearrange("p t (h d) -> p t h d", h=G),
                            turned[:, :, :, 0:XD], rz[:, :, :].unsqueeze(3).broadcast_to([P, TB, G, XD]),
                            ALU.mult).then_inc(emptied, 1)
                    elif kind == "m_turn":
                        wait(dve, filled, n + 1)
                        bb, g = (b + 1, 0) if i == G else (b, i)
                        for q in range(G // 2, G):
                            if q == G - 1:
                                wait(dve, m_copied, G * b + i + 1)
                            ins = nc.vector.tensor_copy(
                                qs[AUG:KR, bass.ds(bb % 2, 1), G * g + q, :].rearrange("r a n -> r (a n)"),
                                pM[XV * q:XV * q + 4, 0:TB * 64].bitcast(BF16))
                        ins.then_inc(emptied, 1)
                    elif kind == "y":
                        wait(dve, filled, n + 1)
                        xt = xr[:, bass.ds(TB * b + 2 * i, 2), :]
                        nc.vector.tensor_tensor(xt, xt, pM[:, :].rearrange("p (t d) -> p t d", t=2),
                                                ALU.add).then_inc(emptied, 1)

                def normalise(b):
                    for t in range(TB):
                        ins = nc.vector.tensor_scalar(
                            xn[:, t, :], xr[:, bass.ds(TB * b + t, 1), :].rearrange("p a d -> p (a d)"),
                            mv[:, bass.ds(TB * b + t, 1), 0], rstd[:, bass.ds(TB * b + t, 1)],
                            ALU.subtract, ALU.mult)
                    ins.then_inc(xn_ready, 1)

                for t in range(T):
                    own.did(nc.vector.bn_stats(stats[:, t, :], xr[:, t, :]))
                own.wait()
                for t in range(T):
                    own.did(nc.vector.bn_aggr(mv[:, t, :], stats[:, t, :]))
                own.wait()
                nc.vector.tensor_scalar(rstd[:, :], mv[:, :, 1], LN_EPS, None, ALU.add).then_inc(s_var, 1)
                dve.wait_ge(s_std, 1)
                own.did(nc.vector.reciprocal(rstd[:, :], rstd[:, :]))
                own.wait()
                normalise(0)

                def prepare(kinds):
                    for n, (kind, i) in enumerate(PREPARE):
                        if kind in kinds:
                            small(0, kind, i, n, own, free_banks[i], first_batch=True)

                prepare(("k",))
                dve.wait_ge(s_mask, 32)
                own.did(nc.vector.tensor_reduce(any_on[:, :], m_row, AX_X, ALU.max))
                own.wait()
                nc.vector.tensor_scalar(q_scale[:, :], any_on[:, :], XD ** -0.5, None, ALU.mult).then_inc(s_scale, 1)
                own.did(nc.vector.tensor_scalar(big[:, :], any_on[:, :], MASKED, None, ALU.mult))
                dve.wait_ge(s_row, 3)
                own.did(nc.vector.tensor_scalar(other_rows[:, :], last_row[:, :], -1.0, 1.0, ALU.mult, ALU.add))
                own.wait()
                own.did(nc.vector.tensor_scalar(row_gain[:, :], big[:, :], last_row[:, :], None, ALU.mult))
                own.wait()
                own.did(nc.vector.tensor_scalar(row_base[:, :], row_gain[:, :], -1.0, other_rows[:, :],
                                                ALU.mult, ALU.add))
                own.wait()
                for b in range(B):
                    nc.vector.tensor_scalar(k_aug[AUG:KR, b], m_row[AUG:KR, b], row_gain[AUG:KR, b:b + 1],
                                            row_base[AUG:KR, b:b + 1], ALU.mult, ALU.add).then_inc(s_aug, 1)
                nc.vector.tensor_scalar(q_aug[:, :], q_aug[:, :], last_row[:, :], None, ALU.add).then_inc(s_aug, 1)
                prepare(("q",))

                def maximum(b, hg, u):
                    U = 16 * (G * b + hg) + u
                    wait(dve, s1_done, U + 1)
                    nc.vector.tensor_reduce(neg_max[:, hg % 2, u // G, u % G:u % G + 1], pS1[:, u % 2, :],
                                            AX_X, ALU.max, negate=True).then_inc(max_done, 1)

                def place(b, hg):
                    wait(dve, av_done, JT * (G * (b - 1) + hg + 1))
                    nc.vector.tensor_copy(v1[:, hg, :, :, 0:XD],
                                          v_new[:, hg].rearrange("p j (i d) -> p j i d", i=G))
                    nc.vector.tensor_scalar(bias[:, hg, :], m_col[:, bass.ds(b, 1), :].rearrange("p a j -> p (a j)"),
                                            -1.0, big[:, bass.ds(b, 1)], ALU.add, ALU.mult).then_inc(placed, 1)

                def split_max(b, hg, own, steps):
                    wait(dve, max_done, 16 * (G * b + hg + 1))
                    wait(dve, filled, steps)
                    nm = neg_max[:, hg % 2]
                    own.did(nc.vector.tensor_copy(max_parts[:, :, :, 0], nm))
                    own.wait()
                    own.did(nc.vector.tensor_tensor(max_rest[:, :, :], nm, max_parts[:, :, :, 0], ALU.subtract))
                    own.wait()
                    own.did(nc.vector.tensor_copy(max_parts[:, :, :, 1], max_rest[:, :, :]))
                    own.wait()
                    nc.vector.tensor_tensor(max_parts[:, :, :, 2], max_rest[:, :, :], max_parts[:, :, :, 1],
                                            ALU.subtract).then_inc(m_ready, 1)

                dve.wait_ge(s_z, 1)
                wait(dve, emptied, len(PREPARE))
                dve.wait_ge(s_z, 3)
                for hg in range(G):
                    place(0, hg)
                for u in range(16):
                    maximum(0, 0, u)
                split_max(0, 0, own, 0)
                small(0, "m_turn", 0, START - 1, own)
                for u in range(4):
                    maximum(0, 1, u)
                before = own.n

                def batch(b, start, first, last, own):
                    n, t_next = 0, 0
                    for hg in range(G):
                        for j in range(JT):
                            if j == 6 and (hg < G - 1 or not last):
                                if hg < G - 1:
                                    split_max(b, hg + 1, own, start + n)
                                else:
                                    split_max(b + 1, 0, own, start + n)
                            units = score_units(hg, j, last)
                            for ahead, g, u in units[:1]:
                                maximum(b + ahead, g, u)
                            for kind, i in small_steps(hg, j, first, last)[:-1]:
                                small(batch_of(b, kind, i, hg), kind, i, start + n, own)
                                n += 1
                            for ahead, g, u in units[1:]:
                                maximum(b + ahead, g, u)
                            for kind, i in small_steps(hg, j, first, last)[-1:]:
                                small(batch_of(b, kind, i, hg), kind, i, start + n, own)
                                n += 1
                            if (hg, j) == (0, 7) and not last:
                                normalise(b + 1)
                            if (hg, j) == (0, 2) and not first:
                                place(b, G - 1)
                            if last and 1 <= hg and t_next < T - TB:
                                if t_next == 0:
                                    wait(dve, emptied, start + n)
                                nc.vector.bn_stats(stats[:, t_next, :], xr[:, t_next, :])
                                t_next += 1
                            if (hg, j) == (2, 5) and not last:
                                wait(dve, emptied, start + n)
                                place(b + 1, 0)
                                place(b + 1, 1)
                            if (hg, j) == (3, 2) and not last:
                                place(b + 1, 2)
                    return start + n

                def owned(b):
                    return Chain(dve, s_dve, before + OWN_FIRST + OWN_MIDDLE * (b - 1))

                own = Chain(dve, s_dve, before)
                batch(0, START, True, False, own)
                assert own.n == OWN_FIRST, own.n
                with dve.Fori(1, B - 1) as b:
                    own = owned(b)
                    batch(b, steps_before(b), False, False, own)
                    assert own.n == OWN_MIDDLE, own.n
                own = owned(B - 1)
                n = batch(B - 1, steps_before(B - 1), False, True, own)
                for q, (kind, i, bank, _done) in enumerate(FINISH):
                    small(B - 1, kind, i, n + q, own, bank)
                wait(dve, emptied, n + len(FINISH))
                for t in range(T - TB, T):
                    own.did(nc.vector.bn_stats(stats[:, t, :], xr[:, t, :]))




E_, FH = 8, 512
TE = T * E_
KH = FH // P
PICKS = 2 * T
SLOTS = 2 * T + E_


def experts(nc, gate_w, ln1_g, ln1_b, w2, b2, ln_g, ln_b, f_rows, y_rows, xr, stats, w1_sb, b1_sb, w2_sb,
            out):
    with ExitStack() as ctx:
        def sb(name, shape, dt=F32):
            return ctx.enter_context(nc.sbuf_tensor("c_" + name, shape, dt))

        def ps(name, shape, dt=F32):
            return ctx.enter_context(nc.psum_tensor("c_" + name, shape, dt))

        def sem(name):
            return ctx.enter_context(nc.semaphore("c_" + name))

        ident = sb("ident", [P, P])
        earlier = sb("earlier", [P, P])
        ones = sb("ones", [P, P])
        half = sb("half", [P, 1])
        b2_sb = sb("b2", [P, E_, D])
        gb = sb("gb", [P, 2, E_, KH])
        lng = sb("lng", [P, D])
        lnb = sb("lnb", [P, D])
        gate = sb("gate", [P, KD, 32])
        f = sb("f", [P, T, D])
        mv = sb("mv", [P, T, 2])
        rstd = sb("rstd", [P, T])
        fT = sb("fT", [P, KD, B * L])
        lgT = sb("lgT", [P, 512])
        g1 = sb("g1", [P, T, E_])
        g2 = sb("g2", [P, T, E_])
        eq = sb("eq", [P, T, E_])
        sel = sb("sel", [P, 2, T, E_])
        both = sb("both", [P, T, E_])
        rank = sb("rank", [P, T, E_])
        tot = sb("tot", [P, 2, T, E_])
        order = sb("order", [P, E_])
        order_i = sb("order_i", [P, E_], I32)
        slot_i = sb("slot_i", [P, SLOTS], I32)
        slot = sb("slot", [P, SLOTS])
        lanes_i = sb("lanes_i", [P, P], I32)
        lanes = sb("lanes", [P, P])
        of_tile_i = sb("of_tile_i", [P, PICKS], I32)
        of_tile = sb("of_tile", [P, PICKS])
        of_lane_i = sb("of_lane_i", [P, PICKS], I32)
        of_lane = sb("of_lane", [P, PICKS])
        spare_i = sb("spare_i", [P, SLOTS], I32)
        spare = sb("spare", [P, SLOTS])
        top = sb("top", [P, 2, T])
        tmp = sb("tmp", [P, T])
        pos = sb("pos", [P, 2, T])
        hi_i = sb("hi_i", [P, 2, T], I32)
        hi = sb("c_hi", [P, 2, T])
        lo = sb("c_lo", [P, 2, T])
        n_e = sb("n_e", [P, E_])
        tiles_i = sb("tiles_i", [P, E_], I32)
        ends = sb("ends", [P, 2, E_])
        over = sb("over", [P, SLOTS, E_])
        s_exp = sb("s_exp", [P, SLOTS])
        s_tab = sb("s_tab", [P, SLOTS], I32)
        y_base = sb("y_base", [P, E_])
        pair = sb("pair", [P, SLOTS])
        unused = sb("unused", [P, SLOTS])
        rows_i = sb("rows_i", [P, SLOTS], I32)
        from_rows = sb("from_rows", [P, SLOTS])
        to_rows = sb("to_rows", [P, SLOTS])
        from_now = sb("from_now", [P, 4], I32)
        to_now = sb("to_now", [P, 2], I32)
        xs = sb("xs", [P, 4, D])
        xsT = sb("xsT", [P, 2, KD, P])
        h = sb("h", [P, 2, FH])
        hst = sb("hst", [P, 2, 6])
        hmv = sb("hmv", [P, 2, 2])
        hrs = sb("hrs", [P, 2, 1])
        hT = sb("hT", [P, 2, KH, P])
        gbn = sb("gbn", [P, 2, 2, KH])
        ys = sb("ys", [P, 2, D])
        y = sb("y", [P, 4, 2, D])
        spread = sb("spread", [P, 4, 2, P])
        acc = fT[:, :, :].rearrange("p k n -> p (k n)").rearrange("p (t d) -> p t d", t=T)
        acc_2d, y_2d = fT[:, :, :].rearrange("p k n -> p (k n)"), y[:, :, :, :].rearrange("p a k d -> p (a k d)")
        at_lane = acc_2d[:, 0:PICKS * P // 2].bitcast(BF16).rearrange("p (n l) -> p n l", n=PICKS)
        at_tile = acc_2d[:, PICKS * P // 2:PICKS * P // 2 + PICKS * SLOTS].rearrange("p (n s) -> p n s", n=PICKS)
        numbers = y_2d[:, 0:PICKS * SLOTS].bitcast(BF16).rearrange("p (n s) -> p n s", n=PICKS)

        pX = [ps("pX0", [P, 512]), ps("pX1", [P, 512])]
        pH = [ps("pH0", [P, 512]), ps("pH1", [P, 512])]
        pT = [ps("pT0", [P, 512]), ps("pT1", [P, 512])]
        pY = [ps("pY0", [P, 512]), ps("pY1", [P, 512])]
        pC = [bank[:, 0:D] for bank in pX + pH + pT + pY]

        s_gate, s_w2, s_par, s_ln = sem("gate"), sem("w2"), sem("par"), sem("ln")
        s_id, s_k, s_gz, s_dve = sem("ident"), sem("consts"), sem("gate0"), sem("dve")
        s_var, s_rstd, f_ready = sem("var"), sem("rstd"), sem("f")
        t_done, t_copied, lg_done, lg_copied = sem("t_done"), sem("t_copied"), sem("lg"), sem("lg_copied")
        lt_done, g_ready, g_exp, both_ready, rank_done = sem("lt"), sem("g"), sem("gexp"), sem("both"), sem("rank")
        f_stored, hot_ready, pairs_done, tab_ready = sem("f_stored"), sem("hot"), sem("pairs"), sem("tab")
        maps_ready, xr_ready = sem("maps"), sem("xr")
        def two(name):
            return [sem(name + "0"), sem(name + "1")]

        xs_in, xs_t, xsT_ready = [sem(f"xs_in{j}") for j in range(4)], two("xs_t"), two("xsT")
        h_done, h_read, h_var, h_rstd, h_norm = two("h"), two("h_read"), two("h_var"), two("h_rstd"), two("h_norm")
        h_t, hT_ready, gb_now = two("h_t"), two("hT"), two("gb_now")
        y_done, y_ready, y_out = two("y"), two("ys"), two("y_out")
        y_in = [sem(f"y_in{i}") for i in range(4)]
        spread_ready, a_done, a_stats, a_used, a_std, o_ready, o_out = sem("spread"), sem("a"), sem("a_st"), sem("a_used"), sem("a_std"), sem("o"), sem("o_out")

        OWN_TILE = 2
        ROUNDS = SLOTS // 4

        def at(i, j):
            return i + j // 4, j % 4

        def nth(i, j):
            return 2 * i + j // 2

        def slot_steps(engine, step):
            for j in range(4):
                step(0, j)
            slot_rounds(engine, step)

        def slot_rounds(engine, step):
            with engine.Fori(1, ROUNDS - 1) as i:
                for j in range(4):
                    step(i, j)
            for j in range(4):
                step(ROUNDS - 1, j)

        def exists(i, j):
            return not isinstance(i, int) or 0 <= 4 * i + j < SLOTS

        with nc.Block() as block:

            @block.sync
            def _(sp):
                sp.wait_ge(s_gz, 1)
                sp.dma_start(gate[:, :, 0:E_], gate_w.rearrange("(k p) e -> p k e", p=P)).then_inc(s_gate, 16)
                with nc.allow_non_contiguous_dma(reason="two vectors of each expert, by hidden unit"):
                    for i, v in enumerate((ln1_g, ln1_b)):
                        sp.dma_start(gb[:, i], v.rearrange("e (c p) -> p e c", p=P)).then_inc(s_par, 16)
                for k in range(KH):
                    sp.dma_start(w2_sb[:, :, k, :], w2[:, P * k:P * k + P, :].rearrange("e p d -> p e d")
                                 ).then_inc(s_w2, 16)
                sp.dma_start(b2_sb[:, :, :].rearrange("p e h -> p (e h)"),
                             b2.rearrange("e h -> (e h)").unsqueeze(0).broadcast_to([P, E_ * D])).then_inc(s_par, 16)
                for t, v in ((lng, ln_g), (lnb, ln_b)):
                    sp.dma_start(t[:, :], v.unsqueeze(0).broadcast_to([P, D])).then_inc(s_ln, 16)

                sp.wait_ge(f_stored, 16 * B)
                for par in range(2):
                    sp.wait_ge(y_out[par], 16 * (SLOTS // 2))
                for t in range(T):
                    if t >= 4:
                        wait(sp, a_done, t - 3)
                    sp.dma_start(y[:, t % 4], y_rows[2 * P * t:2 * P * t + 2 * P, :].rearrange("(p k) d -> p k d", k=2)
                                 ).then_inc(y_in[t % 4], 16)

            @block.gpsimd
            def _(pool):
                pool.memset(gate[:, :, :], 0.0).then_inc(s_gz, 1)
                pool.memset(half[:, :], -0.5).then_inc(s_k, 1)
                pool.wait_ge(s_k, 1)
                make_identity(pool, ident[:, :], s_id)
                pool.memset(ones[:, :], 1.0).then_inc(s_k, 1)
                pool.memset(earlier[:, :], 1.0).then_inc(s_k, 1)
                pool.wait_ge(s_k, 3)
                pool.affine_select(out=earlier[:, :], in_=earlier[:, :], compare_op=ALU.is_gt, fill=0.0,
                                   base=0, pattern=[[1, P]], channel_multiplier=-1).then_inc(s_k, 1)
                pool.iota(order_i[:, :], pattern=[[-1, E_]], base=E_, channel_multiplier=0).then_inc(s_k, 1)
                pool.iota(lanes_i[:, :], pattern=[[1, P]], base=0, channel_multiplier=0).then_inc(s_k, 1)
                pool.iota(slot_i[:, :], pattern=[[1, SLOTS]], base=0, channel_multiplier=0).then_inc(s_k, 1)
                pool.iota(of_tile_i[:, :], pattern=[[0, 2], [2 * P, T]], base=0, channel_multiplier=0).then_inc(s_k, 1)
                pool.iota(of_lane_i[:, :], pattern=[[1, 2], [0, T]], base=1, channel_multiplier=2).then_inc(s_k, 1)
                pool.iota(spare_i[:, :], pattern=[[P, SLOTS]], base=2 * B * L + 1, channel_multiplier=1
                          ).then_inc(s_k, 1)
                pool.wait_ge(s_ln, 32)
                pool.wait_ge(f_ready, T)
                nc.gpsimd.tensor_tensor(xr[:, :, :], xr[:, :, :], lnb[:, :].unsqueeze(1).broadcast_to([P, T, D]),
                                        ALU.add).then_inc(xr_ready, 1)

                def gather(i, j):
                    pool.indirect_dma_start(
                        out=xs[:, j, :], out_offset=None, in_=f_rows,
                        in_offset=bass.IndirectOffsetOnAxis(ap=from_now[:, j:j + 1].bitcast(U32), axis=0)
                    ).then_inc(xs_in[j], 16)

                def scatter(i, j):
                    par = j % 2
                    if isinstance(i, int):
                        wait(pool, y_ready[par], nth(i, j) + 1)
                    pool.indirect_dma_start(
                        out=y_rows, out_offset=bass.IndirectOffsetOnAxis(
                            ap=to_now[:, par:par + 1].bitcast(U32), axis=0),
                        in_=ys[:, par, :], in_offset=None).then_inc(y_out[par], 16)

                def power(i, j):
                    par = j % 2
                    wait(pool, h_var[par], nth(i, j) + 1)
                    nc.gpsimd.tensor_tensor(hrs[:, par, :], hrs[:, par, :], half[:, :], ALU.pow).then_inc(h_rstd[par], 1)

                pool.wait_ge(maps_ready, 1)
                pool.wait_ge(f_stored, 16 * B)
                for j in range(4):
                    gather(0, j)
                power(0, 0)

                def step(i, j):
                    if exists(i, j + 1):
                        power(*at(i, j + 1))
                    if exists(i, j + 4):
                        gather(*at(i, j + 4))
                    if exists(i, j - 2):
                        scatter(*at(i, j - 2))

                slot_steps(pool, step)
                for j in (2, 3):
                    scatter(ROUNDS - 1, j)

            @block.tensor
            def _(pe):
                pe.wait_ge(s_id, 2)
                for n in range(2 * T // 4):
                    wait(pe, f_ready, 2 * n + 2)
                    if n >= 2:
                        wait(pe, t_copied, n - 1)
                    for q in range(4):
                        t, k = 2 * n + q // 2, q % 2
                        ins = pe.transpose(pX[n % 2][:, P * q:P * q + P], f[:, t, P * k:P * k + P], ident[:, :])
                    ins.then_inc(t_done, 1)
                pe.wait_ge(s_gate, 16)
                pe.wait_ge(t_copied, T // 2)
                for k in range(KD):
                    for q in range(B):
                        ins = pe.matmul(pH[0][32 * q:32 * q + 32, :], gate[:, k, :], fT[:, k, L * q:L * q + L],
                                        start=(k == 0), stop=(k == KD - 1))
                ins.then_inc(lg_done, 1)
                pe.wait_ge(lg_copied, 1)
                for c in range(TB):
                    ins = pe.transpose(pH[1][:, P * c:P * c + P], lgT[:, P * c:P * c + P], ident[:, :])
                ins.then_inc(lt_done, 1)
                pe.wait_ge(both_ready, 1)
                pe.wait_ge(s_k, 4)
                sel_2d = both[:, :, :].rearrange("p t e -> p (t e)")
                pe.matmul(pT[0][:, 0:TE], earlier[:, :], sel_2d, start=True, stop=True).then_inc(rank_done, 1)
                pe.matmul(pT[1][:, 0:TE], ones[:, :], sel_2d, start=True, stop=True).then_inc(rank_done, 1)

                pe.wait_ge(hot_ready, 1)
                for n in range(PICKS):
                    ins = pe.matmul(pT[0][:, 0:2 * SLOTS], at_lane[:, n, :], numbers[:, n, :],
                                    start=(n == 0), stop=(n == PICKS - 1))
                ins.then_inc(pairs_done, 1)

                pe.wait_ge(tab_ready, 1)

                def x_transposes(i, j):
                    par = j % 2
                    wait(pe, xs_in[j], 16 * (i + 1))
                    wait(pe, xsT_ready[par], nth(i, j))
                    for k in range(KD):
                        ins = pe.transpose(pX[par][:, P * k:P * k + P], xs[:, j, P * k:P * k + P], ident[:, :])
                    ins.then_inc(xs_t[par], 1)

                def up(i, j):
                    par = j % 2
                    e = pe.value_load(s_tab[0:1, bass.ds(4 * i + j, 1)], min_val=0, max_val=E_ - 1)
                    wait(pe, xsT_ready[par], nth(i, j) + 1)
                    wait(pe, h_read[par], nth(i, j))
                    for k in range(KD):
                        ins = pe.matmul(pH[par][:, :], xsT[:, par, k, :],
                                        w1_sb[:, bass.ds(e, 1), k, :].rearrange("p a h -> p (a h)"),
                                        start=(k == 0), stop=(k == KD - 1))
                    ins.then_inc(h_done[par], 1)

                def h_transposes(i, j):
                    par = j % 2
                    wait(pe, h_norm[par], nth(i, j) + 1)
                    wait(pe, hT_ready[par], nth(i, j))
                    for k in range(KH):
                        ins = pe.transpose(pT[par][:, P * k:P * k + P], h[:, par, P * k:P * k + P], ident[:, :])
                    ins.then_inc(h_t[par], 1)

                def down(i, j):
                    par = j % 2
                    e = pe.value_load(s_tab[0:1, bass.ds(4 * i + j, 1)], min_val=0, max_val=E_ - 1)
                    wait(pe, hT_ready[par], nth(i, j) + 1)
                    wait(pe, y_ready[par], nth(i, j))
                    for k in range(KH):
                        ins = pe.matmul(pY[par][:, 0:D], hT[:, par, k, :],
                                        w2_sb[:, bass.ds(e, 1), k, :].rearrange("p a d -> p (a d)"),
                                        start=(k == 0), stop=(k == KH - 1))
                    ins.then_inc(y_done[par], 1)

                x_transposes(0, 0)
                x_transposes(0, 1)
                up(0, 0)

                def step(i, j):
                    if exists(i, j + 1):
                        up(*at(i, j + 1))
                    h_transposes(i, j)
                    if exists(i, j + 2):
                        x_transposes(*at(i, j + 2))
                    if exists(i, j - 1):
                        down(*at(i, j - 1))

                step(0, 0)
                pe.wait_ge(s_w2, 16 * KH)
                for j in range(1, 4):
                    step(0, j)
                slot_rounds(pe, step)
                down(ROUNDS - 1, 3)

                for par in range(2):
                    pe.wait_ge(y_ready[par], SLOTS // 2)
                for t in range(T):
                    wait(pe, a_used, t - 7)
                    pe.matmul(pC[t % 8], ident[:, :], f[:, t, :], start=True, stop=False)
                    pe.wait_ge(spread_ready, t + 1)
                    wait(pe, y_in[t % 4], 16 * (t // 4 + 1))
                    for k in range(2):
                        ins = pe.matmul(pC[t % 8], spread[:, t % 4, k, :], y[:, t % 4, k, :],
                                        start=False, stop=(k == 1))
                    ins.then_inc(a_done, 1)

            @block.scalar
            def _(act):
                act.wait_ge(s_var, 1)
                nc.scalar.activation(rstd[:, :], rstd[:, :], ACT.Sqrt).then_inc(s_rstd, 1)
                for n in range(T // 2):
                    wait(act, t_done, n + 1)
                    nc.scalar.copy(fT[:, :, 2 * P * n:2 * P * n + 2 * P].rearrange("p k (t n) -> p t k n", t=2),
                                   pX[n % 2][:, :].rearrange("p (t k n) -> p t k n", t=2, k=2)
                                   ).then_inc(t_copied, 1)
                for b in range(B):
                    wait(act, f_ready, TB * (b + 1))
                    act.dma_start(f_rows[L * b:L * b + L, :].rearrange("(c p) d -> p c d", p=P),
                                  f[:, TB * b:TB * b + TB, :]).then_inc(f_stored, 16)
                act.wait_ge(lg_done, 1)
                nc.scalar.copy(lgT[:, :], pH[0][:, :]).then_inc(lg_copied, 1)
                act.wait_ge(g_ready, 1)
                nc.scalar.activation(g1[:, :, :], g1[:, :, :], ACT.Exp).then_inc(g_exp, 1)
                act.wait_ge(s_par, 48)

                def x_copy(i, j):
                    par = j % 2
                    wait(act, xs_t[par], nth(i, j) + 1)
                    wait(act, h_done[par], nth(i, j))
                    nc.scalar.copy(xsT[:, par], pX[par][:, 0:D].rearrange("p (k n) -> p k n", k=KD)
                                   ).then_inc(xsT_ready[par], 1)

                def gelu(i, j):
                    par = j % 2
                    wait(act, gb_now[par], nth(i, j) + 1)
                    wait(act, y_done[par], nth(i, j))
                    wait(act, h_t[par], nth(i, j) + 1)
                    for k in range(KH):
                        ins = nc.scalar.activation(hT[:, par, k, :], pT[par][:, P * k:P * k + P], ACT.Gelu,
                                                   bias=gbn[:, par, 1, k:k + 1], scale=gbn[:, par, 0, k:k + 1])
                    ins.then_inc(hT_ready[par], 1)

                x_copy(0, 0)
                x_copy(0, 1)

                def step(i, j):
                    if exists(i, j + 2):
                        x_copy(*at(i, j + 2))
                    gelu(i, j)

                slot_steps(act, step)

                def spread_weights(t):
                    wait(act, a_done, t - 3)
                    for k in range(2):
                        ins = nc.scalar.activation(spread[:, t % 4, k, :], ident[:, :], ACT.Copy,
                                                   scale=top[:, k, t:t + 1])
                    ins.then_inc(spread_ready, 1)

                def store(t):
                    act.wait_ge(o_ready, t + 1)
                    act.dma_start(out[t // TB, P * (t % TB):P * (t % TB) + P, :], acc[:, t, :]).then_inc(o_out, 16)

                for t in range(4):
                    spread_weights(t)
                for n in range(T // 4):
                    for t in range(4 * n + 4, min(4 * n + 8, T)):
                        spread_weights(t)
                    act.wait_ge(a_stats, n + 1)
                    nc.scalar.activation(rstd[:, 4 * n:4 * n + 4], rstd[:, 4 * n:4 * n + 4], ACT.Sqrt).then_inc(a_std, 1)
                    if n:
                        for t in range(4 * n - 4, 4 * n):
                            store(t)
                for t in range(T - 4, T):
                    store(t)
                act.wait_ge(o_out, 16 * T)

            @block.vector
            def _(dve):
                own = Chain(dve, s_dve)

                def did(ins):
                    own.did(ins)
                    own.wait()

                for t in range(T):
                    own.did(nc.vector.bn_aggr(mv[:, t, :], stats[:, t, :]))
                own.wait()
                nc.vector.tensor_scalar(rstd[:, :], mv[:, :, 1], LN_EPS, None, ALU.add).then_inc(s_var, 1)
                dve.wait_ge(s_rstd, 1)
                own.did(nc.vector.reciprocal(rstd[:, :], rstd[:, :]))
                own.wait()
                for t in range(T):
                    nc.vector.tensor_scalar(f[:, t, :], xr[:, t, :], mv[:, t, 0:1], rstd[:, t:t + 1],
                                            ALU.subtract, ALU.mult).then_inc(f_ready, 1)
                dve.wait_ge(s_k, 10)
                own.did(nc.vector.tensor_copy(order[:, :], order_i[:, :]))
                for to, what in ((slot, slot_i), (lanes, lanes_i), (of_tile, of_tile_i), (of_lane, of_lane_i),
                                 (spare, spare_i)):
                    own.did(nc.vector.tensor_copy(to[:, :], what[:, :]))

                dve.wait_ge(lt_done, 1)
                did(nc.vector.tensor_copy(
                    g1[:, :, :].rearrange("p (q c) e -> p c q e", q=B),
                    pH[1][:, :].rearrange("p (c q e) -> p c q e", c=TB, q=B)[:, :, :, 0:E_]))
                did(nc.vector.tensor_reduce(tmp[:, :], g1[:, :, :], AX_X, ALU.max))
                nc.vector.tensor_tensor(g1[:, :, :], g1[:, :, :], tmp[:, :].unsqueeze(2).broadcast_to([P, T, E_]),
                                        ALU.subtract).then_inc(g_ready, 1)
                dve.wait_ge(g_exp, 1)
                g = g1
                for c in range(2):
                    did(nc.vector.tensor_reduce(top[:, c, :], g[:, :, :], AX_X, ALU.max))
                    did(nc.vector.tensor_tensor(eq[:, :, :], g[:, :, :],
                                                top[:, c, :].unsqueeze(2).broadcast_to([P, T, E_]), ALU.is_equal))
                    did(nc.vector.tensor_tensor(eq[:, :, :], eq[:, :, :],
                                                order[:, :].unsqueeze(1).broadcast_to([P, T, E_]), ALU.mult))
                    did(nc.vector.tensor_reduce(tmp[:, :], eq[:, :, :], AX_X, ALU.max))
                    did(nc.vector.tensor_tensor(sel[:, c], eq[:, :, :],
                                                tmp[:, :].unsqueeze(2).broadcast_to([P, T, E_]), ALU.is_equal))
                    if c == 0:
                        did(nc.vector.scalar_tensor_tensor(
                            g2[:, :, :].rearrange("p t e -> p (t e)"), sel[:, 0].rearrange("p t e -> p (t e)"),
                            -2.0, g1[:, :, :].rearrange("p t e -> p (t e)"), ALU.mult, ALU.add))
                        g = g2
                nc.vector.tensor_tensor(both[:, :, :], sel[:, 0], sel[:, 1], ALU.add).then_inc(both_ready, 1)
                did(nc.vector.tensor_tensor(tmp[:, :], top[:, 0, :], top[:, 1, :], ALU.add))
                did(nc.vector.reciprocal(tmp[:, :], tmp[:, :]))
                own.did(nc.vector.tensor_tensor(top[:, :, :], top[:, :, :],
                                                tmp[:, :].unsqueeze(1).broadcast_to([P, 2, T]), ALU.mult))
                dve.wait_ge(rank_done, 2)
                did(nc.vector.tensor_copy(tot[:, 0].rearrange("p t e -> p (t e)"), pT[1][:, 0:TE]))
                cur = 0
                for step in (1, 2, 4, 8):
                    nc.vector.tensor_copy(tot[:, 1 - cur, 0:step, :], tot[:, cur, 0:step, :])
                    did(nc.vector.tensor_tensor(tot[:, 1 - cur, step:T, :], tot[:, cur, step:T, :],
                                                tot[:, cur, 0:T - step, :], ALU.add))
                    cur = 1 - cur
                total = tot[:, cur]
                did(nc.vector.tensor_scalar(tiles_i[:, :], total[:, T - 1, :], float(P - 1), None, ALU.add))
                did(nc.vector.tensor_scalar(tiles_i[:, :], tiles_i[:, :], 7, None, ALU.logical_shift_right))
                own.did(nc.vector.tensor_copy(n_e[:, :], tiles_i[:, :]))
                did(nc.vector.tensor_copy(ends[:, 0, :], tiles_i[:, :]))
                cur = 0
                for step in (1, 2, 4):
                    nc.vector.tensor_copy(ends[:, 1 - cur, 0:step], ends[:, cur, 0:step])
                    did(nc.vector.tensor_tensor(ends[:, 1 - cur, step:E_], ends[:, cur, step:E_],
                                                ends[:, cur, 0:E_ - step], ALU.add))
                    cur = 1 - cur
                end = ends[:, cur, :]
                did(nc.vector.tensor_tensor(y_base[:, :], end, n_e[:, :], ALU.subtract))
                did(nc.vector.tensor_scalar(y_base[:, :], y_base[:, :], float(P), None, ALU.mult))
                own.did(nc.vector.tensor_tensor(rank[:, 0, :], pT[0][:, 0:E_], y_base[:, :], ALU.add))
                did(nc.vector.tensor_tensor(rank[:, 1:T, :].rearrange("p t e -> p (t e)"), pT[0][:, E_:TE],
                                            total[:, 0:T - 1, :].rearrange("p t e -> p (t e)"), ALU.add))
                did(nc.vector.tensor_tensor(rank[:, 1:T, :], rank[:, 1:T, :],
                                            y_base[:, :].unsqueeze(1).broadcast_to([P, T - 1, E_]), ALU.add))
                for c in range(2):
                    did(nc.vector.tensor_tensor(eq[:, :, :], sel[:, c], rank[:, :, :], ALU.mult))
                    did(nc.vector.tensor_reduce(pos[:, c, :], eq[:, :, :], AX_X, ALU.add))
                did(nc.vector.tensor_copy(hi_i[:, :, :], pos[:, :, :]))
                did(nc.vector.tensor_scalar(hi_i[:, :, :], hi_i[:, :, :], 7, None, ALU.logical_shift_right))
                did(nc.vector.tensor_copy(hi[:, :, :], hi_i[:, :, :]))
                hi_2d, lo_2d, pos_2d = (v[:, :, :].rearrange("p c t -> p (c t)") for v in (hi, lo, pos))
                did(nc.vector.scalar_tensor_tensor(lo_2d, hi_2d, -float(P), pos_2d, ALU.mult, ALU.add))
                own.did(nc.vector.tensor_tensor(at_tile, hi_2d.unsqueeze(2).broadcast_to([P, PICKS, SLOTS]),
                                                slot[:, :].unsqueeze(1).broadcast_to([P, PICKS, SLOTS]), ALU.is_equal))
                own.did(nc.vector.tensor_tensor(at_lane, lo_2d.unsqueeze(2).broadcast_to([P, PICKS, P]),
                                                lanes[:, :].unsqueeze(1).broadcast_to([P, PICKS, P]), ALU.is_equal))
                own.wait()
                own.did(nc.vector.tensor_tensor(numbers[:, :, 0:SLOTS], at_tile,
                                                of_tile[:, :].unsqueeze(2).broadcast_to([P, PICKS, SLOTS]), ALU.mult))
                own.wait()
                nc.vector.tensor_tensor(numbers[:, :, SLOTS:2 * SLOTS], at_tile,
                                        of_lane[:, :].unsqueeze(2).broadcast_to([P, PICKS, SLOTS]), ALU.mult
                                        ).then_inc(hot_ready, 1)
                did(nc.vector.tensor_tensor(over[:, :, :], slot[:, :].unsqueeze(2).broadcast_to([P, SLOTS, E_]),
                                            end.unsqueeze(1).broadcast_to([P, SLOTS, E_]), ALU.is_ge))
                did(nc.vector.tensor_reduce(s_exp[:, :], over[:, :, :], AX_X, ALU.add))
                nc.vector.tensor_scalar(s_tab[:, :], s_exp[:, :], float(E_ - 1), None, ALU.min).then_inc(tab_ready, 1)
                dve.wait_ge(pairs_done, 1)
                did(nc.vector.tensor_copy(pair[:, :], pT[0][:, 0:SLOTS]))
                did(nc.vector.tensor_tensor(pair[:, :], pair[:, :], pT[0][:, SLOTS:2 * SLOTS], ALU.add))
                did(nc.vector.tensor_scalar(rows_i[:, :], pair[:, :], -1.0, 0.0, ALU.add, ALU.max))
                did(nc.vector.tensor_scalar(rows_i[:, :], rows_i[:, :], 1, None, ALU.logical_shift_right))
                nc.vector.tensor_copy(from_now[:, :], rows_i[:, 0:4]).then_inc(maps_ready, 1)
                own.did(nc.vector.tensor_copy(from_rows[:, :], rows_i[:, :]))
                did(nc.vector.scalar_tensor_tensor(unused[:, :], pair[:, :], 0.0, spare[:, :], ALU.is_equal, ALU.mult))
                nc.vector.scalar_tensor_tensor(to_rows[:, :], pair[:, :], -1.0, unused[:, :], ALU.add, ALU.add
                                               ).then_inc(maps_ready, 1)
                dve.wait_ge(maps_ready, 2)
                dve.wait_ge(tab_ready, 1)
                dve.wait_ge(s_par, 48)

                def first(i, j, own):
                    par = j % 2
                    e = dve.value_load(s_tab[0:1, bass.ds(4 * i + j, 1)], min_val=0, max_val=E_ - 1)
                    wait(dve, h_done[par], nth(i, j) + 1)
                    wait(dve, h_t[par], nth(i, j))
                    nc.vector.tensor_tensor(h[:, par, :], pH[par][:, :],
                                            b1_sb[:, bass.ds(e, 1), :].rearrange("p a h -> p (a h)"),
                                            ALU.add).then_inc(h_read[par], 1)
                    wait(dve, h_read[par], nth(i, j) + 1)
                    own.did(nc.vector.bn_stats(hst[:, par, :], h[:, par, :]))
                    wait(dve, hT_ready[par], nth(i, j))
                    own.wait()
                    nc.vector.tensor_scalar(gbn[:, par, :, :], gb[:, :, bass.ds(e, 1), :].rearrange("p g a k -> p g (a k)"),
                                            1.0, None, ALU.mult).then_inc(gb_now[par], 1)
                    own.did(nc.vector.bn_aggr(hmv[:, par, :], hst[:, par, :]))
                    if exists(i, j + 3) and (not isinstance(i, int) or 4 * i + j > 0):
                        ahead, k = at(i, j + 3)
                        nc.vector.tensor_scalar(from_now[:, k:k + 1], from_rows[:, bass.ds(4 * ahead + k, 1)],
                                                1.0, None, ALU.mult)
                    own.wait()
                    nc.vector.tensor_scalar(hrs[:, par, :], hmv[:, par, 1:2], LN_EPS, None, ALU.add
                                            ).then_inc(h_var[par], 1)

                def second(i, j):
                    par = j % 2
                    wait(dve, h_rstd[par], nth(i, j) + 1)
                    nc.vector.tensor_scalar(h[:, par, :], h[:, par, :], hmv[:, par, 0:1], hrs[:, par, :],
                                            ALU.subtract, ALU.mult).then_inc(h_norm[par], 1)

                def third(i, j):
                    par = j % 2
                    e = dve.value_load(s_tab[0:1, bass.ds(4 * i + j, 1)], min_val=0, max_val=E_ - 1)
                    wait(dve, y_done[par], nth(i, j) + 1)
                    wait(dve, y_out[par], 16 * nth(i, j))
                    nc.vector.tensor_scalar(to_now[:, par:par + 1], to_rows[:, bass.ds(4 * i + j, 1)],
                                            1.0, None, ALU.mult)
                    nc.vector.tensor_tensor(ys[:, par, :], pY[par][:, 0:D],
                                            b2_sb[:, bass.ds(e, 1), :].rearrange("p a d -> p (a d)"),
                                            ALU.add).then_inc(y_ready[par], 1)

                before = own.n
                first(0, 0, own)
                second(0, 0)

                def step(i, j):
                    own = Chain(dve, s_dve, before + OWN_TILE * (4 * i + j + 1))
                    if exists(i, j + 1):
                        first(*at(i, j + 1), own)
                        second(*at(i, j + 1))
                    if exists(i, j - 1):
                        third(*at(i, j - 1))

                slot_steps(dve, step)
                third(ROUNDS - 1, 3)

                dve.wait_ge(s_ln, 32)
                dve.wait_ge(xr_ready, 1)
                own = Chain(dve, s_dve, before + OWN_TILE * SLOTS)

                def statistics(n):
                    for t in range(4 * n, 4 * n + 4):
                        wait(dve, a_done, t + 1)
                        own.did(nc.vector.bn_stats(stats[:, t, :], pC[t % 8]))
                    own.wait()
                    for t in range(4 * n, 4 * n + 4):
                        own.did(nc.vector.bn_aggr(mv[:, t, :], stats[:, t, :]))
                    own.wait()
                    nc.vector.tensor_scalar(rstd[:, 4 * n:4 * n + 4], mv[:, 4 * n:4 * n + 4, 1], LN_EPS, None, ALU.add
                                            ).then_inc(a_stats, 1)

                def finish(n):
                    wait(dve, a_std, n + 1)
                    own.did(nc.vector.reciprocal(rstd[:, 4 * n:4 * n + 4], rstd[:, 4 * n:4 * n + 4]))
                    for t in range(4 * n, 4 * n + 4):
                        nc.vector.scalar_tensor_tensor(acc[:, t, :], pC[t % 8], mv[:, t, 0:1], lng[:, :],
                                                       ALU.subtract, ALU.mult).then_inc(a_used, 1)
                    own.wait()
                    for t in range(4 * n, 4 * n + 4):
                        wait(dve, a_used, t + 1)
                        nc.vector.scalar_tensor_tensor(acc[:, t, :], acc[:, t, :], rstd[:, t:t + 1], xr[:, t, :],
                                                       ALU.mult, ALU.add).then_inc(o_ready, 1)

                for n in range(T // 4):
                    statistics(n)
                    if n:
                        finish(n - 1)
                finish(T // 4 - 1)




def decoder_layer(nc, x, ctx_in, mask, a_wq, a_wk, a_wv, a_wo, a_kq, a_kk, x_wq, x_wk, x_wv, x_wo,
                  gate_w, w1, b1, ln1_g, ln1_b, w2, b2, ln_g, ln_b, out):
    k_scr = nc.dram_tensor("k_scr", (B, 3, D, M), BF16).ap()
    q_scr = nc.dram_tensor("q_scr", (B, 3, D, L), BF16).ap()
    aug_scr = nc.dram_tensor("aug_scr", (B, 4, M), BF16).ap()
    f_rows = nc.dram_tensor("f_rows", (B * L, D), F32).ap()
    y_rows = nc.dram_tensor("y_rows", (2 * B * L + SLOTS * P, D), F32).ap()
    with nc.sbuf_tensor("xr", [P, T, D], F32) as xr, nc.sbuf_tensor("stats", [P, T, 6], F32) as stats:
        linear_attention(nc, x, a_wq, a_wk, a_wv, a_wo, a_kq, a_kk, xr)
        with nc.sbuf_tensor("ks", [P, 2, XH, M], BF16) as ks, nc.sbuf_tensor("qs", [P, 2, XH, L], BF16) as qs:
            w1_sb = ks[:, 0].rearrange("p h n -> p (h n)").bitcast(F32).rearrange("p (e k h) -> p e k h", e=E_, k=KD)
            w2_sb = ks[:, 1].rearrange("p h n -> p (h n)").bitcast(F32).rearrange("p (e k d) -> p e k d", e=E_, k=KH)
            b1_sb = qs[:, 0].rearrange("p h n -> p (h n)").bitcast(F32).rearrange("p (e h) -> p e h", e=E_)
            cross_attention(nc, ctx_in, mask, x_wq, x_wk, x_wv, x_wo, k_scr, q_scr, aug_scr, xr, stats, ks, qs,
                            w1, b1, w1_sb, b1_sb)
            experts(nc, gate_w, ln1_g, ln1_b, w2, b2, ln_g, ln_b, f_rows, y_rows, xr, stats,
                    w1_sb, b1_sb, w2_sb, out)


_INS = ['x', 'ctx_768', 'mask_BxS2_bf1', 'L0_attn_Wq', 'L0_attn_Wk', 'L0_attn_Wv', 'L0_attn_Wo',
        'L0_attn_Kq', 'L0_attn_Kk', 'L0_xattn_Wq', 'L0_xattn_Wk', 'L0_xattn_Wv', 'L0_xattn_Wo',
        'L0_ffn_gate_w', 'L0_ffn_w1', 'L0_ffn_b1', 'L0_ffn_ln1_g', 'L0_ffn_ln1_b', 'L0_ffn_w2',
        'L0_ffn_b2', 'L0_ffn_ln_g', 'L0_ffn_ln_b']
_OUTS = [((B, L, D), 'float32')]


def kernel(**inputs):
    import numpy as _np
    import concourse.bacc as _bacc
    from concourse import mybir as _mybir
    from concourse.bass_utils import run_bass_kernel_spmd as _run

    nc = _bacc.Bacc("TRN2", target_bir_lowering=False, num_devices=1)
    arrays, args = {}, []
    for name in _INS:
        a = _np.ascontiguousarray(inputs[name])
        if a.dtype.kind == "b":
            a = a.view(_np.uint8)
        arrays[f"in_{name}_dram"] = a
        args.append(nc.dram_tensor(f"in_{name}_dram", a.shape, _mybir.dt.from_np(a.dtype), kind="ExternalInput").ap())
    for i, (shape, dtype) in enumerate(_OUTS):
        dt = _mybir.dt.from_np(_np.dtype(dtype))
        args.append(nc.dram_tensor(f"out_{i}_dram", shape, dt, kind="ExternalOutput").ap())
    decoder_layer(nc, *args)
    r = _run(nc, [arrays], core_ids=[0])
    got = tuple(r.results[0][f"out_{i}_dram"] for i in range(len(_OUTS)))
    return got[0]
```
